# Optimizing a Trainium2 kernel written in Bass

```python
import numpy as np
import jax
import jax.numpy as jnp

def _softmax(x, axis=-1):
    return jax.nn.softmax(x, axis=axis)

def _gelu(x):
    return jax.nn.gelu(x, approximate=True)

def _silu(x):
    return jax.nn.silu(x)

def _sigmoid(x):
    return jax.nn.sigmoid(x)

def _layernorm(x, axis=-1, eps=1e-05):
    m = jnp.mean(x, axis=axis, keepdims=True)
    v = jnp.var(x, axis=axis, keepdims=True)
    return (x - m) / jnp.sqrt(v + eps)

def _scatter_add(tgt, idx, src, axis=0):
    return tgt.at[idx].add(src)

def _segment_sum(src, seg, n):
    return jax.ops.segment_sum(src, seg, n)
kernel_name = 'mk_adaln_d2_jaxref_r8_884275'

def setup_inputs(seed: int=0):
    np.random.seed(seed)
    _w = jnp.asarray

    def _L0_attn_setup():
        import jax, jax.numpy as jnp
        import numpy as np
        B, N, D = (8, 128, 512)
        H = 8
        HEAD_DIM = D // H
        E = HEAD_DIM // H
        key = jax.random.key(seed)
        ks = jax.random.split(key, 7)
        s = 0.02
        return {'x': jax.random.normal(ks[0], (B, N, D), dtype=jnp.float32), 'Wqk_w': jax.random.normal(ks[1], (2 * HEAD_DIM, D), dtype=jnp.float32) * s, 'Wqk_b': jnp.zeros((2 * HEAD_DIM,), dtype=jnp.float32), 'Wv_w': jax.random.normal(ks[2], (HEAD_DIM, D), dtype=jnp.float32) * s, 'Wv_b': jnp.zeros((HEAD_DIM,), dtype=jnp.float32), 'Wo_w': jax.random.normal(ks[3], (D, HEAD_DIM), dtype=jnp.float32) * s, 'Wo_b': jnp.zeros((D,), dtype=jnp.float32)}
    _L0_attn_in = _L0_attn_setup()

    def _L0_ffn_setup():
        import jax, jax.numpy as jnp
        import numpy as np
        NUM_EXPERTS = 8
        D_IN = 512
        D_OUT = 512
        key = jax.random.key(seed)
        k_x, k_gw, k_gb, k_ew, k_eb = jax.random.split(key, 5)
        x = jax.random.normal(k_x, (4, 256, D_IN), dtype=jnp.float32)
        gate_w = jax.random.normal(k_gw, (NUM_EXPERTS, D_IN), dtype=jnp.float32) * 0.02
        gate_b = jax.random.normal(k_gb, (NUM_EXPERTS,), dtype=jnp.float32) * 0.02
        expert_w = jax.random.normal(k_ew, (NUM_EXPERTS, D_OUT, D_IN), dtype=jnp.float32) * 0.02
        expert_b = jax.random.normal(k_eb, (NUM_EXPERTS, D_OUT), dtype=jnp.float32) * 0.02
        return {'x': x, 'gate_w': gate_w, 'gate_b': gate_b, 'expert_w': expert_w, 'expert_b': expert_b}
    _L0_ffn_in = _L0_ffn_setup()
    _L0_c = _w((lambda *s: np.random.randn(*s).astype(np.float32) * 0.05)(1, 512))
    _L0_wmod = _w((lambda *s: np.random.randn(*s).astype(np.float32) * 0.05)(512, 6 * 512) * 512 ** (-0.5))

    def _L1_attn_setup():
        import jax, jax.numpy as jnp
        import numpy as np
        H = 512
        D = 1024
        N = 16
        K = 4
        R = 32
        BATCH = 1
        L = 256
        EPS = 1e-06

        def _rmsnorm(x, w):
            return x * jax.lax.rsqrt(jnp.mean(x * x, axis=-1, keepdims=True) + EPS) * w
        key = jax.random.key(seed)
        ks = jax.random.split(key, 10)
        s = 0.02
        return {'hidden_states': jax.random.normal(ks[0], (BATCH, L, H), jnp.float32), 'W_in': jax.random.normal(ks[1], (2 * D, H), jnp.float32) * s, 'conv_w': jax.random.normal(ks[2], (D, K), jnp.float32) * s, 'conv_b': jax.random.normal(ks[3], (D,), jnp.float32) * s, 'Wx': jax.random.normal(ks[4], (R + 2 * N, D), jnp.float32) * s, 'dt_ln_w': jnp.ones((R,), jnp.float32), 'b_ln_w': jnp.ones((N,), jnp.float32), 'c_ln_w': jnp.ones((N,), jnp.float32), 'Wdt': jax.random.normal(ks[5], (D, R), jnp.float32) * s, 'dt_bias': jax.random.normal(ks[6], (D,), jnp.float32) * s, 'A': -jnp.exp(jax.random.normal(ks[7], (D, N), jnp.float32) * 0.5), 'D_param': jnp.ones((D,), jnp.float32), 'W_out': jax.random.normal(ks[8], (H, D), jnp.float32) * s}
    _L1_attn_in = _L1_attn_setup()

    def _L1_ffn_setup():
        import jax, jax.numpy as jnp
        import numpy as np
        B, L, H, Dh, M = (4, 256, 16, 32, 128)
        D = H * Dh
        key = jax.random.key(seed)
        kx, ku, kd, kp = jax.random.split(key, 4)
        x = jax.random.normal(kx, (B, L, D), dtype=jnp.float32)
        up = jax.random.normal(ku, (H, Dh, M), dtype=jnp.float32)
        down = jax.random.normal(kd, (H, M, Dh), dtype=jnp.float32)
        perm = jax.random.permutation(kp, D)
        return {'x': x, 'up': up, 'down': down, 'perm': perm}
    _L1_ffn_in = _L1_ffn_setup()
    _L1_c = _w((lambda *s: np.random.randn(*s).astype(np.float32) * 0.05)(1, 512))
    _L1_wmod = _w((lambda *s: np.random.randn(*s).astype(np.float32) * 0.05)(512, 6 * 512) * 512 ** (-0.5))
    _d = {'L0_attn_x': _L0_attn_in['x'], 'L0_attn_Wqk_w': _L0_attn_in['Wqk_w'], 'L0_attn_Wqk_b': _L0_attn_in['Wqk_b'], 'L0_attn_Wv_w': _L0_attn_in['Wv_w'], 'L0_attn_Wv_b': _L0_attn_in['Wv_b'], 'L0_attn_Wo_w': _L0_attn_in['Wo_w'], 'L0_attn_Wo_b': _L0_attn_in['Wo_b'], 'L0_ffn_gate_w': _L0_ffn_in['gate_w'], 'L0_ffn_gate_b': _L0_ffn_in['gate_b'], 'L0_ffn_expert_w': _L0_ffn_in['expert_w'], 'L0_ffn_expert_b': _L0_ffn_in['expert_b'], 'L0_c': _L0_c, 'L0_wmod': _L0_wmod, 'L1_attn_W_in': _L1_attn_in['W_in'], 'L1_attn_conv_w': _L1_attn_in['conv_w'], 'L1_attn_conv_b': _L1_attn_in['conv_b'], 'L1_attn_Wx': _L1_attn_in['Wx'], 'L1_attn_dt_ln_w': _L1_attn_in['dt_ln_w'], 'L1_attn_b_ln_w': _L1_attn_in['b_ln_w'], 'L1_attn_c_ln_w': _L1_attn_in['c_ln_w'], 'L1_attn_Wdt': _L1_attn_in['Wdt'], 'L1_attn_dt_bias': _L1_attn_in['dt_bias'], 'L1_attn_A': _L1_attn_in['A'], 'L1_attn_D_param': _L1_attn_in['D_param'], 'L1_attn_W_out': _L1_attn_in['W_out'], 'L1_ffn_up': _L1_ffn_in['up'], 'L1_ffn_down': _L1_ffn_in['down'], 'L1_ffn_perm': _L1_ffn_in['perm'], 'L1_c': _L1_c, 'L1_wmod': _L1_wmod}
    _x0 = _d['L0_attn_x']
    _d['L0_attn_x'] = jax.random.normal(jax.random.fold_in(jax.random.key(seed), 1), (1, 2048, 512), dtype=_x0.dtype)
    del _x0
    return _d

def reference(L0_attn_x, L0_attn_Wqk_w, L0_attn_Wqk_b, L0_attn_Wv_w, L0_attn_Wv_b, L0_attn_Wo_w, L0_attn_Wo_b, L0_ffn_gate_w, L0_ffn_gate_b, L0_ffn_expert_w, L0_ffn_expert_b, L0_c, L0_wmod, L1_attn_W_in, L1_attn_conv_w, L1_attn_conv_b, L1_attn_Wx, L1_attn_dt_ln_w, L1_attn_b_ln_w, L1_attn_c_ln_w, L1_attn_Wdt, L1_attn_dt_bias, L1_attn_A, L1_attn_D_param, L1_attn_W_out, L1_ffn_up, L1_ffn_down, L1_ffn_perm, L1_c, L1_wmod):

    def _L0_attn_ref(x, Wqk_w, Wqk_b, Wv_w, Wv_b, Wo_w, Wo_b):
        import jax, jax.numpy as jnp
        import numpy as np
        B, N, D = (8, 128, 512)
        H = 8
        HEAD_DIM = D // H
        E = HEAD_DIM // H
        b, n, _ = x.shape
        qk = (x @ Wqk_w.T + Wqk_b).reshape(b, n, H, E, 2)
        q = jnp.transpose(qk[..., 0], (0, 2, 1, 3))
        k = jnp.transpose(qk[..., 1], (0, 2, 1, 3))
        v = (x @ Wv_w.T + Wv_b).reshape(b, n, H, E)
        v = jnp.transpose(v, (0, 2, 1, 3))
        scores = jnp.einsum('bhqd,bhkd->bhqk', q, k)
        attn = jax.nn.softmax(scores, axis=-1) / jnp.asarray(HEAD_DIM ** 0.5, x.dtype)
        out = jnp.einsum('bhsl,bhlv->bhsv', attn, v)
        out = jnp.transpose(out, (0, 2, 1, 3)).reshape(b, n, H * E)
        return out @ Wo_w.T + Wo_b

    def _L0_ffn_ref(x, gate_w, gate_b, expert_w, expert_b):
        import jax, jax.numpy as jnp
        import numpy as np
        NUM_EXPERTS = 8
        D_IN = 512
        D_OUT = 512
        orig_shape = x.shape
        xf = x.reshape(-1, x.shape[-1])
        gate_logits = xf @ gate_w.T + gate_b
        gates = jax.nn.softmax(gate_logits, axis=-1)
        selected = jnp.argmax(gates, axis=-1)
        out = jnp.zeros((xf.shape[0], expert_w.shape[1]), dtype=xf.dtype)
        for j in range(expert_w.shape[0]):
            yj = xf @ expert_w[j].T + expert_b[j]
            out = out + jnp.where((selected == j)[:, None], yj, 0.0)
        return out.reshape(*orig_shape[:-1], expert_w.shape[1])

    def _L1_attn_ref(hidden_states, W_in, conv_w, conv_b, Wx, dt_ln_w, b_ln_w, c_ln_w, Wdt, dt_bias, A, D_param, W_out):
        import jax, jax.numpy as jnp
        import numpy as np
        H = 512
        D = 1024
        N = 16
        K = 4
        R = 32
        BATCH = 1
        L = 256
        EPS = 1e-06

        def _rmsnorm(x, w):
            return x * jax.lax.rsqrt(jnp.mean(x * x, axis=-1, keepdims=True) + EPS) * w
        proj = hidden_states @ W_in.T
        u, gate = jnp.split(proj, 2, axis=-1)
        x = jnp.transpose(u, (0, 2, 1))
        x = jax.lax.conv_general_dilated(x, conv_w[:, None, :], window_strides=(1,), padding=[(K - 1, 0)], dimension_numbers=('NCH', 'OIH', 'NCH'), feature_group_count=D)
        u = jax.nn.silu(jnp.transpose(x, (0, 2, 1)) + conv_b)
        ssm_p = u @ Wx.T
        dt, Bm, Cm = jnp.split(ssm_p, [R, R + N], axis=-1)
        dt = _rmsnorm(dt, dt_ln_w)
        Bm = _rmsnorm(Bm, b_ln_w)
        Cm = _rmsnorm(Cm, c_ln_w)
        delta = jax.nn.softplus(dt @ Wdt.T + dt_bias)

        def step(state, xs):
            d_t, B_t, C_t, u_t = xs
            dA = jnp.exp(d_t[..., None] * A)
            state = dA * state + (d_t * u_t)[..., None] * B_t[:, None, :]
            y_t = jnp.einsum('bdn,bn->bd', state, C_t)
            return (state, y_t)
        init = jnp.zeros((hidden_states.shape[0], D, N), hidden_states.dtype)
        xs = (jnp.swapaxes(delta, 0, 1), jnp.swapaxes(Bm, 0, 1), jnp.swapaxes(Cm, 0, 1), jnp.swapaxes(u, 0, 1))
        _, ys = jax.lax.scan(step, init, xs)
        y = jnp.swapaxes(ys, 0, 1) + u * D_param
        y = y * jax.nn.silu(gate)
        return y @ W_out.T

    def _L1_ffn_ref(x, up, down, perm):
        import jax, jax.numpy as jnp
        import numpy as np
        B, L, H, Dh, M = (4, 256, 16, 32, 128)
        D = H * Dh
        b, l, Dm = x.shape
        h, d = (up.shape[0], up.shape[1])
        unperm = jnp.argsort(perm)
        t = x.reshape(b * l, Dm)
        t = t[:, perm]
        t = t.reshape(b * l, h, d)
        t = jnp.einsum('bhd,hdm->bhm', t, up)
        t = jax.nn.gelu(t, approximate=False)
        t = jnp.einsum('bhm,hmd->bhd', t, down)
        t = t.reshape(b * l, h * d)
        t = t[:, unperm]
        out = t.reshape(b, l, Dm)
        return out
    x = L0_attn_x
    mod = (_silu(L0_c) @ L0_wmod).reshape(L0_c.shape[0], 6, 1, -1)
    sa, ca, ga, sb, cb, gb = (mod[:, 0], mod[:, 1], mod[:, 2], mod[:, 3], mod[:, 4], mod[:, 5])
    ga = (2 * (ga >= 0) - 1) * jnp.maximum(jnp.abs(ga), 0.25)
    gb = (2 * (gb >= 0) - 1) * jnp.maximum(jnp.abs(gb), 0.25)
    h = _layernorm(x, axis=-1) * (1 + ca) + sa
    x = x + ga * _L0_attn_ref(h, L0_attn_Wqk_w, L0_attn_Wqk_b, L0_attn_Wv_w, L0_attn_Wv_b, L0_attn_Wo_w, L0_attn_Wo_b)
    h = _layernorm(x, axis=-1) * (1 + cb) + sb
    x = x + gb * _L0_ffn_ref(h, L0_ffn_gate_w, L0_ffn_gate_b, L0_ffn_expert_w, L0_ffn_expert_b)
    mod = (_silu(L1_c) @ L1_wmod).reshape(L1_c.shape[0], 6, 1, -1)
    sa, ca, ga, sb, cb, gb = (mod[:, 0], mod[:, 1], mod[:, 2], mod[:, 3], mod[:, 4], mod[:, 5])
    ga = (2 * (ga >= 0) - 1) * jnp.maximum(jnp.abs(ga), 0.25)
    gb = (2 * (gb >= 0) - 1) * jnp.maximum(jnp.abs(gb), 0.25)
    h = _layernorm(x, axis=-1) * (1 + ca) + sa
    x = x + ga * _L1_attn_ref(h, L1_attn_W_in, L1_attn_conv_w, L1_attn_conv_b, L1_attn_Wx, L1_attn_dt_ln_w, L1_attn_b_ln_w, L1_attn_c_ln_w, L1_attn_Wdt, L1_attn_dt_bias, L1_attn_A, L1_attn_D_param, L1_attn_W_out)
    h = _layernorm(x, axis=-1) * (1 + cb) + sb
    x = x + gb * _L1_ffn_ref(h, L1_ffn_up, L1_ffn_down, L1_ffn_perm)
    return x

_drawn_inputs = setup_inputs


def setup_inputs(seed=0):
    import zlib

    import numpy as np

    out = dict(_drawn_inputs(seed))
    spreads = {'L0_attn_Wqk_b': (0.0, 0.8),
     'L0_attn_Wv_b': (0.0, 0.8),
     'L0_attn_Wo_b': (0.0, 0.1),
     'L1_attn_dt_ln_w': (1.0, 0.6),
     'L1_attn_b_ln_w': (1.0, 0.6),
     'L1_attn_c_ln_w': (1.0, 0.6),
     'L1_attn_D_param': (1.0, 0.6)}
    factors = {'L0_attn_Wqk_w': 8.0,
     'L0_attn_Wv_w': 8.0,
     'L0_attn_Wo_w': 8.0,
     'L0_ffn_expert_b': 8.0,
     'L1_attn_W_in': 8.0,
     'L1_attn_conv_w': 8.0,
     'L1_attn_conv_b': 8.0,
     'L1_attn_Wx': 8.0,
     'L1_attn_Wdt': 8.0,
     'L1_attn_dt_bias': 8.0,
     'L1_attn_A': 8.0,
     'L1_attn_W_out': 8.0}
    for name, (base, spread) in spreads.items():
        noise = np.random.default_rng([zlib.crc32(name.encode()), seed]).standard_normal(out[name].shape)
        drawn = base * np.exp(spread * noise) if base else spread * noise
        out[name] = jnp.asarray(drawn.astype(out[name].dtype))
    for name, factor in factors.items():
        out[name] = (out[name] * factor).astype(out[name].dtype)
    return out
```

```python
from contextlib import ExitStack

import concourse.bass as bass
from concourse import mybir

F32 = mybir.dt.float32
BF16 = mybir.dt.bfloat16
U32 = mybir.dt.uint32
ALU = mybir.AluOpType
ACT = mybir.ActivationFunctionType
AX = mybir.AxisListType

P = 128
T = 2048
D = 512
KT = D // P
W = 512
NCH = T // W
HEADS, E = 8, 8
PARTS = 3
PAIRS = PARTS * PARTS
QROWS = PAIRS * E
EXPERTS = 8
LN_EPS = 1e-5
SHIFT_A, SCALE_A, GATE_A, SHIFT_B, SCALE_B, GATE_B = range(6)

DI = 1024
DT = DI // P
NST = 16
RANK = 32
TAPS = 4
SW = 256
SCH = T // SW
NG = 4
RMS_EPS = 1e-6

MH, MD, MM = 16, 32, 128


def sb_alloc(ctx, nc):
    def sb(name, shape, dt=F32):
        return ctx.enter_context(nc.sbuf_tensor(name, shape, dt))
    return sb


def sem_alloc(ctx, nc, prefix):
    def sem(name):
        return ctx.enter_context(nc.semaphore(prefix + "_" + name))
    return sem


class LayerNorm:

    def __init__(self, nc, ctx, prefix, width, consts, psum, banks, scale, shift):
        sb, sem = sb_alloc(ctx, nc), sem_alloc(ctx, nc, prefix)
        self.nc, self.width, self.tiles = nc, width, width // P
        self.c = consts
        self.centred = sb(prefix + "_centred", [P, KT, width])
        self.square = sb(prefix + "_square", [P, KT, width])
        self.sd = sb(prefix + "_sd", [P, self.tiles])
        self.rstd = sb(prefix + "_rstd", [P, self.tiles])
        self.h = sb(prefix + "_h", [P, KT, width])
        self.ps_mean = psum[:, banks[0], 0:width]
        self.ps_var = psum[:, banks[1], 0:self.tiles]
        self.ps_rstd = psum[:, banks[2], 0:width]
        self.scale, self.shift = scale, shift
        self.mean_done, self.centred_done = sem("mean_done"), sem("centred_done")
        self.square_done, self.var_done = sem("square_done"), sem("var_done")
        self.sd_done, self.rstd_done = sem("sd_done"), sem("rstd_done")
        self.bcast_done, self.norm_done, self.h_done = sem("bcast_done"), sem("norm_done"), sem("h_done")

    def tensor(self, pe, i, x):
        nc = self.nc
        for k in range(KT):
            last = nc.tensor.matmul(self.ps_mean, self.c.inv_d[:], x[:, k, :], start=(k == 0), stop=(k == KT - 1))
        last.then_inc(self.mean_done, 1)
        pe.wait_ge(self.square_done, i + 1)
        for t in range(self.tiles):
            for k in range(KT):
                last = nc.tensor.matmul(self.ps_var[:, t:t + 1], self.square[:, k, t * P:(t + 1) * P],
                                        self.c.inv_d[:, 0:1], start=(k == 0), stop=(k == KT - 1))
        last.then_inc(self.var_done, 1)
        pe.wait_ge(self.rstd_done, i + 1)
        for t in range(self.tiles):
            last = nc.tensor.matmul(self.ps_rstd[:, t * P:(t + 1) * P], self.rstd[:, t:t + 1].to_broadcast([P, P]),
                                    self.c.ident[:], start=True, stop=True)
        last.then_inc(self.bcast_done, 1)

    def vector(self, dve, i, x):
        nc = self.nc
        w = self.width
        dve.wait_ge(self.mean_done, i + 1)
        dve.wait_ge(self.h_done, i * KT)
        nc.vector.tensor_tensor(self.centred[:], x, self.ps_mean.unsqueeze(1).to_broadcast([P, KT, w]),
                                ALU.subtract).then_inc(self.centred_done, 1)
        dve.wait_ge(self.sd_done, i + 1)
        nc.vector.reciprocal(self.rstd[:], self.sd[:]).then_inc(self.rstd_done, 1)
        dve.wait_ge(self.bcast_done, i + 1)
        nc.vector.tensor_tensor(self.centred[:], self.centred[:],
                                self.ps_rstd.unsqueeze(1).to_broadcast([P, KT, w]), ALU.mult).then_inc(self.norm_done, 1)

    def scalar(self, act, i, h_free=None):
        nc = self.nc
        act.wait_ge(self.centred_done, i + 1)
        nc.scalar.activation(self.square[:], self.centred[:], ACT.Square).then_inc(self.square_done, 1)
        act.wait_ge(self.var_done, i + 1)
        nc.scalar.activation(self.sd[:], self.ps_var, ACT.Sqrt, bias=self.c.ln_eps[:, 0:1]).then_inc(self.sd_done, 1)
        act.wait_ge(self.norm_done, i + 1)
        if h_free is not None:
            act.wait_ge(h_free[0], h_free[1])
        for k in range(KT):
            nc.scalar.activation(self.h[:, k, :], self.centred[:, k, :], ACT.Identity, bias=self.shift[:, k:k + 1],
                                 scale=self.scale[:, k:k + 1]).then_inc(self.h_done, 1)


class Consts:
    pass


def modulation(nc, d, g):
    with ExitStack() as ctx:
        sb, sem = sb_alloc(ctx, nc), sem_alloc(ctx, nc, "mod")
        wmod = sb("mod_w", [P, 2, KT, 6 * D])
        ccol = sb("mod_c", [P, 2 * KT])
        cact = sb("mod_silu_c", [P, 2 * KT])
        sign = sb("mod_sign", [P, 2, 2, KT])
        mag = sb("mod_mag", [P, 2, 2, KT])
        psum = ctx.enter_context(nc.psum_tensor("mod_psum", [P, 2, 6 * KT], F32))
        consts_in, c_in, w_in = sem("consts_in"), sem("c_in"), [sem("w0_in"), sem("w1_in")]
        silu_done, prod_done, step = sem("silu_done"), sem("prod_done"), sem("step")
        block = ctx.enter_context(nc.Block())

        @block.sync
        def _(sp):
            for layer in range(2):
                sp.dma_start(ccol[:, layer * KT:(layer + 1) * KT], d[f"c{layer}"]).then_inc(c_in, 16)
            for layer in range(2):
                for k in range(KT):
                    sp.dma_start(wmod[:, layer, k, :], d[f"wmod{layer}"][k * P:(k + 1) * P, :]).then_inc(w_in[layer], 16)
            sp.dma_start(g.ident[:], d["ident"]).then_inc(consts_in, 16)
            sp.wait_ge(consts_in, 16)

        @block.scalar
        def _(act):
            act.wait_ge(c_in, 32)
            nc.scalar.activation(cact[:], ccol[:], ACT.Silu).then_inc(silu_done, 1)

        @block.tensor
        def _(pe):
            pe.wait_ge(silu_done, 1)
            for layer in range(2):
                pe.wait_ge(w_in[layer], 16 * KT)
                for m in range(6 * KT):
                    for k in range(KT):
                        last = nc.tensor.matmul(psum[:, layer, m:m + 1], wmod[:, layer, k, m * P:(m + 1) * P],
                                                cact[:, layer * KT + k:layer * KT + k + 1],
                                                start=(k == 0), stop=(k == KT - 1))
                last.then_inc(prod_done, 1)

        @block.vector
        def _(dve):
            nc.vector.memset(g.inv_d[:], 1.0 / D)
            nc.vector.memset(g.ones_row[:], 1.0)
            nc.vector.memset(g.ln_eps[:], LN_EPS)
            nc.vector.memset(g.rms_eps[:], RMS_EPS)
            dve.wait_ge(prod_done, 2)
            nc.vector.tensor_copy(g.mod[:].rearrange("p l s k -> p (l s k)"),
                                  psum[:].rearrange("p l m -> p (l m)")).then_inc(step, 1)
            dve.wait_ge(step, 1)
            scales = g.mod[:, :, SCALE_A::3, :]
            gates = g.mod[:, :, GATE_A::3, :]
            nc.vector.tensor_scalar(scales, scales, 1.0, None, ALU.add)
            nc.vector.tensor_scalar(sign[:], gates, 0.0, 2.0, ALU.is_ge, ALU.mult).then_inc(step, 1)
            for layer in range(2):
                gate = g.mod[:, layer, GATE_A::3, :]
                nc.vector.scalar_tensor_tensor(mag[:, layer], gate, -1.0, gate, ALU.mult, ALU.max).then_inc(step, 1)
            dve.wait_ge(step, 4)
            nc.vector.tensor_scalar(mag[:], mag[:], 0.25, None, ALU.max).then_inc(step, 1)
            dve.wait_ge(step, 5)
            for layer in range(2):
                nc.vector.scalar_tensor_tensor(g.mod[:, layer, GATE_A::3, :], sign[:, layer], -1.0, mag[:, layer],
                                               ALU.add, ALU.mult)


def qkv(nc, d, g, scratch):
    with ExitStack() as ctx:
        sb, sem = sb_alloc(ctx, nc), sem_alloc(ctx, nc, "qkv")
        x = sb("qkv_x", [P, KT, T])
        wqk = sb("qkv_wqk", [P, KT, 2 * HEADS * E])
        qkb = sb("qkv_bqk", [P, 1])
        wv = sb("qkv_wv", [P, KT, HEADS * E])
        bv = sb("qkv_bv", [1, HEADS * E])
        qk = sb("qkv_qk", [P, W])
        rest = sb("qkv_rest", [P, W])
        parts = sb("qkv_parts", [P, 2, PARTS, W], BF16)
        psum = ctx.enter_context(nc.psum_tensor("qkv_psum", [P, 8, W], F32))
        ps_qk, ps_v = psum[:, 0, :], psum[:, 1, 0:W // P * HEADS * E]
        ln = LayerNorm(nc, ctx, "ln1", W, g, psum, (4, 5, 6), g.mod[:, 0, SCALE_A], g.mod[:, 0, SHIFT_A])
        weights_in = sem("weights_in")
        x_in = [sem("x_even_in"), sem("x_odd_in")]
        qk_done, v_done = sem("qk_done"), sem("v_done")
        qk_out, v_out = sem("qk_out"), sem("v_out")
        split = sem("split")
        parts_stored = [sem("parts_even_stored"), sem("parts_odd_stored")]
        block = ctx.enter_context(nc.Block())
        xsrc = d["x"].rearrange("(k p) t -> p k t", p=P)

        @block.sync
        def _(sp):
            for i in range(NCH):
                if i >= 2:
                    sp.wait_ge(x_in[i % 2], 16 * (i // 2))
                sp.dma_start(x[:, :, i * W:(i + 1) * W], xsrc[:, :, i * W:(i + 1) * W]).then_inc(x_in[i % 2], 16)
                if i == 1:
                    sp.dma_start(wqk[:], d["wqk"].rearrange("(k p) m -> p k m", p=P)).then_inc(weights_in, 16)
                    sp.dma_start(wv[:], d["wv"].rearrange("(k p) m -> p k m", p=P)).then_inc(weights_in, 16)
                    sp.dma_start(qkb[:], d["bqk"]).then_inc(weights_in, 16)
                    sp.dma_start(bv[:], d["bv"]).then_inc(weights_in, 16)
            for i in range(NCH):
                sp.wait_ge(split, (i + 1) * 5)
                sp.dma_start(scratch.parts[:, :, i * W:(i + 1) * W].rearrange("s p t -> p s t"),
                             parts[:, i % 2]).then_inc(parts_stored[i % 2], 16)
            for b in range(2):
                sp.wait_ge(parts_stored[b], 16 * NCH // 2)

        @block.tensor
        def _(pe):
            pe.wait_ge(weights_in, 64)
            for c in range(NCH // 2):
                for b in range(2):
                    i = c * 2 + b
                    pe.wait_ge(x_in[b], c * 16 + 16)
                    ln.tensor(pe, i, x[:, :, bass.ds(i * W, W)])
                    pe.wait_ge(ln.h_done, (i + 1) * KT)
                    pe.wait_ge(qk_out, i)
                    for k in range(KT):
                        last = nc.tensor.matmul(ps_qk, wqk[:, k, :], ln.h[:, k, :], start=(k == 0), stop=(k == KT - 1))
                    last.then_inc(qk_done, 1)
                    pe.wait_ge(v_out, i)
                    for t in range(W // P):
                        out = ps_v[:, t * HEADS * E:(t + 1) * HEADS * E]
                        for k in range(KT):
                            nc.tensor.matmul(out, ln.h[:, k, t * P:(t + 1) * P], wv[:, k, :], start=(k == 0), stop=False)
                        last = nc.tensor.matmul(out, g.ones_row[0:1, 0:P], bv[0:1, :], start=False, stop=True)
                    last.then_inc(v_done, 1)

        @block.vector
        def _(dve):
            for c in range(NCH // 2):
                for b in range(2):
                    i = c * 2 + b
                    dve.wait_ge(x_in[b], c * 16 + 16)
                    ln.vector(dve, i, x[:, :, bass.ds(i * W, W)])
                    dve.wait_ge(qk_out, i + 1)
                    dve.wait_ge(parts_stored[b], c * 16)
                    nc.vector.tensor_copy(parts[:, b, 0, :], qk[:]).then_inc(split, 1)
                    dve.wait_ge(split, i * 5 + 1)
                    nc.vector.tensor_tensor(rest[:], qk[:], parts[:, b, 0, :], ALU.subtract).then_inc(split, 1)
                    dve.wait_ge(split, i * 5 + 2)
                    nc.vector.tensor_copy(parts[:, b, 1, :], rest[:]).then_inc(split, 1)
                    dve.wait_ge(split, i * 5 + 3)
                    nc.vector.tensor_tensor(rest[:], rest[:], parts[:, b, 1, :], ALU.subtract).then_inc(split, 1)
                    dve.wait_ge(split, i * 5 + 4)
                    nc.vector.tensor_copy(parts[:, b, 2, :], rest[:]).then_inc(split, 1)

        @block.scalar
        def _(act):
            for c in range(NCH // 2):
                for b in range(2):
                    i = c * 2 + b
                    ln.scalar(act, i, h_free=(v_done, i))
                    act.wait_ge(qk_done, i + 1)
                    act.wait_ge(split, i * 5)
                    nc.scalar.activation(qk[:], ps_qk, ACT.Identity, bias=qkb[:, 0:1]).then_inc(qk_out, 1)
                    act.wait_ge(v_done, i + 1)
                    nc.scalar.copy(g.v[:, bass.ds(i * (W // P * HEADS * E), W // P * HEADS * E)], ps_v).then_inc(v_out, 1)


def attention(nc, d, g, scratch):
    KTILES = T // P
    QC = T // W
    UNITS = KTILES * 2
    RING = 4
    MAXES = KTILES * QC
    MB = 3
    VC = 32
    SUM = E
    with ExitStack() as ctx:
        sb, sem = sb_alloc(ctx, nc), sem_alloc(ctx, nc, "att")
        qst = sb("att_q", [P, HEADS * T], BF16)
        kst = sb("att_k", [P, HEADS * T], BF16)
        vcur = sb("att_v", [P, 2, KTILES, VC])
        probs = sb("att_probs", [P, RING, 2 * W])
        osb = sb("att_out", [P, 2, W])
        rowmax = sb("att_rowmax", [P, MAXES])
        negmax = sb("att_negmax", [P, KTILES])
        negpart = sb("att_negpart", [P, 2, 32], BF16)
        negturn = sb("att_negturn", [P, 2, 32], BF16)
        sums = sb("att_sums", [P, HEADS, T // P])
        rec = sb("att_rec", [P, HEADS, T // P])
        psum = ctx.enter_context(nc.psum_tensor("att_psum", [P, 8, W], F32))
        ps_s = [psum[:, 2 * s:2 * s + 2, :] for s in range(2)]
        ps_o, ps_m = psum[:, 4, :], [psum[:, 5 + s, :] for s in range(MB)]
        stacks_in, v_ones = sem("stacks_in"), sem("v_ones")
        scored, exp_done, pv_done = sem("scored"), sem("exp_done"), sem("pv_done")
        v_ready, o_out = sem("v_ready"), sem("o_out")
        max_scored, max_done, neg_step = sem("max_scored"), sem("max_done"), sem("neg_step")
        neg_stored, neg_in = sem("neg_stored"), sem("neg_in")
        o_stored = [sem("o_even_stored"), sem("o_odd_stored")]
        sums_in, rec_done, rec_stored = sem("sums_in"), sem("rec_done"), sem("rec_stored")
        NEG = 5
        block = ctx.enter_context(nc.Block())

        def head_steps(hh):
            return [bass.ds(hh * T + t * P, P) for t in range(KTILES)], [bass.ds(hh * T + j * W, W) for j in range(QC)]

        @block.sync
        def _(sp):
            sp.dma_start(kst[QROWS:QROWS + 2, :], d["ones"]).then_inc(stacks_in, 16)
            for a in range(PARTS):
                for b in range(PARTS):
                    r = (a * PARTS + b) * E
                    for st, part, row in ((qst, a, 0), (kst, b, HEADS * E)):
                        sp.dma_start(st[r:r + E, :].rearrange("e (h t) -> e h t", h=HEADS),
                                     scratch.parts[part, row:row + HEADS * E, :].rearrange("(h e) t -> e h t", e=E)
                                     ).then_inc(stacks_in, 16)

            def shift_rows(hh):
                sp.wait_ge(neg_step, (hh + 1) * NEG)
                for q in range(4):
                    sp.dma_start(scratch.neg[hh][:, :, q, :].rearrange("s t p -> t s p"),
                                 negturn[32 * q:32 * q + KTILES, :, :]).then_inc(neg_stored, 16)
                sp.wait_ge(neg_stored, (hh + 1) * 64)
                sp.dma_start(qst[QROWS:QROWS + 2, bass.ds(hh * T, T)],
                             scratch.neg[hh].rearrange("s t q p -> s (t q p)")).then_inc(neg_in, 16)

            def store_head(hh, b):
                sp.wait_ge(o_out, hh + 3)
                for j in range(QC):
                    sp.dma_start(scratch.num[bass.ds(hh * E, E), j * W:(j + 1) * W],
                                 osb[32 * j:32 * j + E, b, :]).then_inc(o_stored[b], 16)
                    sp.dma_start(scratch.den[bass.ds(hh, 1), j * W:(j + 1) * W],
                                 osb[32 * j + SUM:32 * j + SUM + 1, b, :]).then_inc(o_stored[b], 16)

            sp.wait_ge(stacks_in, 16 * (2 * PAIRS + 1))
            shift_rows(0)
            for hh in range(HEADS):
                if hh + 1 < HEADS:
                    shift_rows(hh + 1)
                store_head(hh, hh % 2)
            for b in range(2):
                sp.wait_ge(o_stored[b], HEADS // 2 * 2 * QC * 16)
            sp.dma_start(sums[:], scratch.den.rearrange("h (p b) -> p h b", p=P)).then_inc(sums_in, 16)
            sp.wait_ge(rec_done, 1)
            sp.dma_start(scratch.rec.rearrange("h (p b) -> p h b", p=P), rec[:]).then_inc(rec_stored, 16)
            sp.wait_ge(rec_stored, 16)

        @block.gpsimd
        def _(pool):
            nc.gpsimd.memset(vcur[:], 0.0).then_inc(v_ones, 1)
            pool.wait_ge(v_ones, 1)
            nc.gpsimd.memset(vcur[:, :, :, SUM:SUM + 1], 1.0).then_inc(v_ones, 1)
            vall = g.v[:].rearrange("p (t c) -> p t c", c=HEADS * E)

            def head(hh, b):
                pool.wait_ge(o_out, hh + 1)
                nc.gpsimd.tensor_copy(vcur[:, b, :, 0:E], vall[:, :, bass.ds(hh * E, E)]).then_inc(v_ready, 1)

            for c in range(HEADS // 2):
                for b in range(2):
                    head(c * 2 + b, b)

        @block.tensor
        def _(pe):
            def max_scores(hm, qt):
                tile, chunk = head_steps(hm)
                for kc in range(QC):
                    m = qt * QC + kc
                    if m == 0:
                        pe.wait_ge(max_done, hm * MAXES)
                    elif not (isinstance(hm, int) and hm * MAXES + m < MB):
                        pe.wait_ge(max_done, hm * MAXES + (m - MB + 1))
                    nc.tensor.matmul(ps_m[m % MB], qst[0:QROWS, tile[qt]], kst[0:QROWS, chunk[kc]],
                                     start=True, stop=True).then_inc(max_scored, 1)

            def scores(hh, kt):
                tile, chunk = head_steps(hh)
                for half in range(2):
                    u = 2 * kt + half
                    pe.wait_ge(exp_done, hh * UNITS + u + 1)
                    for j in range(2):
                        last = nc.tensor.matmul(ps_s[half][:, j, :], kst[0:QROWS + 2, tile[kt]],
                                                qst[0:QROWS + 2, chunk[2 * half + j]], start=True, stop=True)
                    last.then_inc(scored, 1)

            def weighted(hh, b, kt):
                pe.wait_ge(exp_done, hh * UNITS + 2 * kt + 4)
                if kt == 0:
                    pe.wait_ge(v_ready, hh + 1)
                    pe.wait_ge(o_out, hh + 2)
                for j in range(QC):
                    u = 2 * kt + j // 2
                    mm = nc.tensor.matmul(ps_o[32 * j:32 * j + VC, :], vcur[:, b, kt, :],
                                          probs[:, u % RING, (j % 2) * W:(j % 2 + 1) * W],
                                          start=(kt == 0), stop=(kt == KTILES - 1))
                    if j % 2:
                        mm.then_inc(pv_done, 1)

            def head(hh, b, next_max, before=None):
                pe.wait_ge(neg_in, (hh + 1) * 16)
                for kt in range(KTILES):
                    scores(hh, kt)
                    if kt == 0 and before is not None:
                        weighted(*before)
                    if kt > 0:
                        weighted(hh, b, kt - 1)
                    if next_max is not None:
                        max_scores(next_max, kt)
                return hh, b, KTILES - 1

            pe.wait_ge(v_ones, 2)
            pe.wait_ge(stacks_in, 16 * (2 * PAIRS + 1))
            for qt in range(KTILES):
                max_scores(0, qt)
            for c in range(HEADS // 2 - 1):
                before = None
                for b in range(2):
                    before = head(c * 2 + b, b, c * 2 + b + 1, before)
                weighted(*before)
            before = head(HEADS - 2, 0, HEADS - 1)
            before = head(HEADS - 1, 1, None, before)
            weighted(*before)

        @block.scalar
        def _(act):
            act.sem_inc(exp_done, 2)
            act.sem_inc(o_out, 2)
            act.sem_inc(pv_done, RING)

            def out(hh, b, c):
                act.wait_ge(pv_done, (hh + 1) * UNITS + RING)
                act.wait_ge(o_stored[b], c * (2 * QC * 16))
                nc.scalar.copy(osb[:, b, :], ps_o).then_inc(o_out, 1)

            def head(hh, before=None):
                for u in range(UNITS):
                    act.wait_ge(scored, hh * UNITS + u + 1)
                    act.wait_ge(pv_done, hh * UNITS + u + 1)
                    nc.scalar.activation(probs[:, u % RING, :].rearrange("p (j t) -> p j t", j=2), ps_s[u % 2],
                                         ACT.Exp).then_inc(exp_done, 1)
                    if u == 1 and before is not None:
                        out(*before)

            for c in range(HEADS // 2):
                head(c * 2)
                head(c * 2 + 1, (c * 2, 0, c))
                out(c * 2 + 1, 1, c)

        @block.vector
        def _(dve):
            nc.vector.memset(negpart[:], 0.0)

            def row_max(hm):
                for m in range(MAXES):
                    dve.wait_ge(max_scored, hm * MAXES + m + 1)
                    nc.vector.tensor_reduce(rowmax[:, m:m + 1], ps_m[m % MB], AX.X, ALU.max).then_inc(max_done, 1)
                dve.wait_ge(max_done, (hm + 1) * MAXES)
                nc.vector.tensor_reduce(negmax[:], rowmax[:].rearrange("p (t c) -> p t c", c=QC), AX.X, ALU.max,
                                        negate=True).then_inc(neg_step, 1)
                dve.wait_ge(neg_step, hm * NEG + 1)
                nc.vector.tensor_copy(negpart[:, 0, 0:KTILES], negmax[:]).then_inc(neg_step, 1)
                dve.wait_ge(neg_step, hm * NEG + 2)
                nc.vector.tensor_tensor(negmax[:], negmax[:], negpart[:, 0, 0:KTILES], ALU.subtract).then_inc(neg_step, 1)
                dve.wait_ge(neg_step, hm * NEG + 3)
                nc.vector.tensor_copy(negpart[:, 1, 0:KTILES], negmax[:]).then_inc(neg_step, 1)
                dve.wait_ge(neg_step, hm * NEG + 4)
                dve.wait_ge(neg_stored, hm * 64)
                nc.vector.transpose(negturn[:].rearrange("p s c -> p (s c)"),
                                    negpart[:].rearrange("p s c -> p (s c)")).then_inc(neg_step, 1)

            for hm in range(HEADS):
                row_max(hm)
            dve.wait_ge(sums_in, 16)
            nc.vector.reciprocal(rec[:], sums[:]).then_inc(rec_done, 1)


def experts(nc, d, g, scratch):
    GT = W // P
    STEPS = 6
    with ExitStack() as ctx:
        sb, sem = sb_alloc(ctx, nc), sem_alloc(ctx, nc, "moe")
        wo = sb("moe_wo", [HEADS * E + 1, D])
        wg = sb("moe_wg", [P, KT, EXPERTS])
        bg = sb("moe_bg", [1, EXPERTS])
        we = sb("moe_we", [P, EXPERTS, KT, D])
        be = sb("moe_be", [EXPERTS, D])
        pick = sb("moe_pick", [EXPERTS, EXPERTS, P])
        iota = sb("moe_iota", [P, EXPERTS])
        x = sb("moe_x", [P, 2, KT, W])
        num = sb("moe_num", [HEADS * E, 2, W])
        rec = sb("moe_rec", [HEADS * E, 2, W])
        att = sb("moe_att", [HEADS * E + 1, W])
        x1 = sb("moe_x1", [P, KT, W])
        x2 = sb("moe_x2", [P, KT, W])
        logit = sb("moe_logit", [P, GT, EXPERTS])
        top = sb("moe_top", [P, GT])
        chosen = sb("moe_chosen", [P, GT])
        onehot = sb("moe_onehot", [P, GT, EXPERTS])
        turned = sb("moe_turned", [EXPERTS, W])
        masked = sb("moe_masked", [P, 2, KT, W])
        psum = ctx.enter_context(nc.psum_tensor("moe_psum", [P, 8, W], F32))
        ln = LayerNorm(nc, ctx, "ln2", W, g, psum, (4, 5, 6), g.mod[:, 0, SCALE_B], g.mod[:, 0, SHIFT_B])
        acc = [psum[:, m, :] for m in range(KT)]
        ps_gate, ps_turn = psum[:, 7, 0:GT * EXPERTS], psum[0:EXPERTS, 5, :]
        ps_mask = [psum[:, 4, :], psum[:, 6, :]]
        weights_in, experts_in = sem("weights_in"), sem("experts_in")
        in_done = [sem("even_in"), sem("odd_in")]
        att_ready, wo_done, x1_done = sem("att_ready"), sem("wo_done"), sem("x1_done")
        gate_done, pick_step, chosen_done = sem("gate_done"), sem("pick_step"), sem("chosen_done")
        turn_done, turned_out, mask_done, masked_done = sem("turn_done"), sem("turned_out"), sem("mask_done"), sem("masked_done")
        expert_done, x2_done, x2_stored = sem("expert_done"), sem("x2_done"), sem("x2_stored")
        block = ctx.enter_context(nc.Block())
        xsrc = d["x"].rearrange("(k p) t -> p k t", p=P)
        xdst = scratch.x2.rearrange("(k p) t -> p k t", p=P)

        @block.sync
        def _(sp):
            sp.dma_start(wo[:], d["wo"]).then_inc(weights_in, 16)
            sp.dma_start(wg[:], d["wg"].rearrange("(k p) m -> p k m", p=P)).then_inc(weights_in, 16)
            sp.dma_start(bg[:], d["bg"]).then_inc(weights_in, 16)
            sp.dma_start(be[:], d["be"]).then_inc(weights_in, 16)
            sp.dma_start(pick[:], d["pick"].rearrange("e (f m) -> e f m", f=EXPERTS)).then_inc(weights_in, 16)
            sp.dma_start(iota[:], d["iota"]).then_inc(weights_in, 16)

            def load(i, b):
                sp.dma_start(num[:, b, :], scratch.num[:, bass.ds(i * W, W)]).then_inc(in_done[b], 16)
                sp.dma_start(rec[:, b, :], scratch.rec[:, bass.ds(i * W, W)].unsqueeze(1).to_broadcast([HEADS, E, W])
                             ).then_inc(in_done[b], 16)
                sp.dma_start(x[:, b], xsrc[:, :, bass.ds(i * W, W)]).then_inc(in_done[b], 16)

            def store(i):
                sp.wait_ge(x2_done, (i + 1) * KT)
                sp.dma_start(xdst[:, :, bass.ds(i * W, W)], x2[:]).then_inc(x2_stored, 16)

            load(0, 0)
            load(1, 1)
            for e in range(EXPERTS):
                sp.dma_start(we[:, e], d["we"][e].rearrange("(k p) m -> p k m", p=P)).then_inc(experts_in, 16)
            for i in range(2):
                store(i)
                load(i + 2, i)
            for i in range(2, NCH):
                store(i)
            sp.wait_ge(x2_stored, 16 * NCH)

        @block.tensor
        def _(pe):
            pe.wait_ge(weights_in, 96)
            for c in range(NCH // 2):
                for b in range(2):
                    i = c * 2 + b
                    pe.wait_ge(att_ready, i + 1)
                    pe.wait_ge(x2_done, i * KT)
                    for m in range(KT):
                        nc.tensor.matmul(acc[m], wo[:, m * P:(m + 1) * P], att[:], start=True, stop=True).then_inc(wo_done, 1)
                    pe.wait_ge(x1_done, (i + 1) * KT)
                    ln.tensor(pe, i, x1[:])
                    pe.wait_ge(ln.h_done, (i + 1) * KT)
                    for t in range(GT):
                        out = ps_gate[:, t * EXPERTS:(t + 1) * EXPERTS]
                        for k in range(KT):
                            nc.tensor.matmul(out, ln.h[:, k, t * P:(t + 1) * P], wg[:, k, :], start=(k == 0), stop=False)
                        last = nc.tensor.matmul(out, g.ones_row[0:1, 0:P], bg[0:1, :], start=False, stop=True)
                    last.then_inc(gate_done, 1)
                    pe.wait_ge(chosen_done, i + 1)
                    for t in range(GT):
                        last = nc.tensor.transpose(ps_turn[:, t * P:(t + 1) * P], onehot[:, t, :], g.ident[:])
                    last.then_inc(turn_done, 1)
                    pe.wait_ge(turned_out, i + 1)

                    def mask(e):
                        if e >= 2:
                            pe.wait_ge(masked_done, i * EXPERTS + e - 1)
                        nc.tensor.matmul(ps_mask[e % 2], pick[:, e, :], turned[:], start=True, stop=True).then_inc(mask_done, 1)

                    mask(0)
                    mask(1)
                    for m in range(KT):
                        nc.tensor.matmul(acc[m], be[:, m * P:(m + 1) * P], turned[:], start=True, stop=False)
                    if b == 0:
                        pe.wait_ge(experts_in, 16 * EXPERTS)
                    for e in range(EXPERTS):
                        pe.wait_ge(masked_done, i * EXPERTS + e + 1)
                        for m in range(KT):
                            for k in range(KT):
                                last = nc.tensor.matmul(acc[m], we[:, e, k, m * P:(m + 1) * P], masked[:, e % 2, k, :],
                                                        start=False, stop=(e == EXPERTS - 1 and k == KT - 1))
                        last.then_inc(expert_done, 1)
                        if e + 2 < EXPERTS:
                            mask(e + 2)

        @block.vector
        def _(dve):
            nc.vector.memset(att[HEADS * E:HEADS * E + 1, :], 1.0)
            dve.wait_ge(weights_in, 96)
            for c in range(NCH // 2):
                for b in range(2):
                    i = c * 2 + b
                    dve.wait_ge(in_done[b], c * 48 + 48)
                    dve.wait_ge(wo_done, i * KT)
                    nc.vector.scalar_tensor_tensor(att[0:HEADS * E, :], num[:, b, :], float((HEADS * E) ** -0.5), rec[:, b, :],
                                                   ALU.mult, ALU.mult).then_inc(att_ready, 1)
                    for m in range(KT):
                        dve.wait_ge(wo_done, i * KT + m + 1)
                        nc.vector.scalar_tensor_tensor(x1[:, m, :], acc[m], g.mod[:, 0, GATE_A, m:m + 1], x[:, b, m, :],
                                                       ALU.mult, ALU.add).then_inc(x1_done, 1)
                    dve.wait_ge(x1_done, (i + 1) * KT)
                    ln.vector(dve, i, x1[:])
                    dve.wait_ge(gate_done, i + 1)
                    nc.vector.tensor_copy(logit[:].rearrange("p t e -> p (t e)"), ps_gate).then_inc(pick_step, 1)
                    dve.wait_ge(pick_step, i * STEPS + 1)
                    nc.vector.tensor_reduce(top[:], logit[:], AX.X, ALU.max).then_inc(pick_step, 1)
                    dve.wait_ge(pick_step, i * STEPS + 2)
                    nc.vector.tensor_tensor(logit[:], logit[:], top[:].unsqueeze(2).to_broadcast([P, GT, EXPERTS]),
                                            ALU.is_equal).then_inc(pick_step, 1)
                    dve.wait_ge(pick_step, i * STEPS + 3)
                    nc.vector.scalar_tensor_tensor(logit[:], logit[:], -float(EXPERTS), iota[:].unsqueeze(1).to_broadcast([P, GT, EXPERTS]),
                                                   ALU.mult, ALU.add).then_inc(pick_step, 1)
                    dve.wait_ge(pick_step, i * STEPS + 4)
                    nc.vector.tensor_reduce(chosen[:], logit[:], AX.X, ALU.min).then_inc(pick_step, 1)
                    dve.wait_ge(pick_step, i * STEPS + 5)
                    nc.vector.tensor_scalar(chosen[:], chosen[:], float(EXPERTS), None, ALU.add).then_inc(pick_step, 1)
                    dve.wait_ge(pick_step, i * STEPS + 6)
                    nc.vector.tensor_tensor(onehot[:], iota[:].unsqueeze(1).to_broadcast([P, GT, EXPERTS]),
                                            chosen[:].unsqueeze(2).to_broadcast([P, GT, EXPERTS]), ALU.is_equal).then_inc(chosen_done, 1)
                    for e in range(EXPERTS):
                        dve.wait_ge(mask_done, i * EXPERTS + e + 1)
                        if e >= 2:
                            dve.wait_ge(expert_done, i * EXPERTS + e - 1)
                        nc.vector.tensor_tensor(masked[:, e % 2], ln.h[:], ps_mask[e % 2].unsqueeze(1).to_broadcast([P, KT, W]),
                                                ALU.mult).then_inc(masked_done, 1)
                    dve.wait_ge(expert_done, (i + 1) * EXPERTS)
                    dve.wait_ge(x2_stored, i * 16)
                    for m in range(KT):
                        nc.vector.scalar_tensor_tensor(x2[:, m, :], acc[m], g.mod[:, 0, GATE_B, m:m + 1], x1[:, m, :],
                                                       ALU.mult, ALU.add).then_inc(x2_done, 1)

        @block.scalar
        def _(act):
            for c in range(NCH // 2):
                for b in range(2):
                    i = c * 2 + b
                    ln.scalar(act, i, h_free=(masked_done, i * EXPERTS))
                    act.wait_ge(turn_done, i + 1)
                    nc.scalar.copy(turned[:], ps_turn).then_inc(turned_out, 1)


def state_space(nc, d, g, scratch):
    ST = SW // P
    ROWS = RANK + 2 * NST
    GROUPS = NST // NG
    with ExitStack() as ctx:
        sb, sem = sb_alloc(ctx, nc), sem_alloc(ctx, nc, "ssm")
        win = sb("ssm_win", [P, KT, 2 * DI])
        wout = sb("ssm_wout", [P, DT, D])
        wx = sb("ssm_wx", [P, DT, ROWS])
        wdt = sb("ssm_wdt", [RANK, DI])
        convw = sb("ssm_convw", [P, DT, TAPS])
        convb = sb("ssm_convb", [P, DT])
        dtb = sb("ssm_dtb", [P, DT])
        amat = sb("ssm_a", [P, DT, NST])
        dpar = sb("ssm_d", [P, DT])
        lnw = sb("ssm_lnw", [ROWS, 1])
        group = sb("ssm_group", [ROWS, 3])
        conv = sb("ssm_conv", [P, DT, TAPS, P])
        skip = sb("ssm_skip", [P, DT, P])
        x = sb("ssm_x", [P, KT, SW])
        upre = sb("ssm_upre", [P, DT, SW + TAPS - 1])
        u = sb("ssm_u", [P, DT, SW])
        delta = sb("ssm_delta", [P, DT, SW])
        gate = sb("ssm_gate", [P, DT, SW])
        sp_sb = sb("ssm_proj", [ROWS, SW])
        sq = sb("ssm_square", [ROWS, SW])
        rsd = sb("ssm_rsd", [P, ST, 3])
        rinv = sb("ssm_rinv", [P, ST, 3])
        rwide = sb("ssm_rwide", [P, ST, ROWS])
        normed = sb("ssm_normed", [ROWS, SW])
        bc = sb("ssm_bc", [P, 2, NST, SW])
        state = sb("ssm_state", [P, DT, NST])
        decay = sb("ssm_decay", [P, 2, NG, SW])
        scan = sb("ssm_scan", [P, 2, NG, SW])
        x3 = sb("ssm_x3", [P, KT, SW])
        psum = ctx.enter_context(nc.psum_tensor("ssm_psum", [P, 8, W], F32))
        ln = LayerNorm(nc, ctx, "ln3", SW, g, psum, (4, 5, 6), g.mod[:, 1, SCALE_A], g.mod[:, 1, SHIFT_A])
        ps_y = psum[:, 0:4, :].rearrange("p b (s t) -> p (b s) t", s=2)
        ps_a = [psum[:, 4, 0:SW], psum[:, 6, 0:SW]]
        ps_b = [psum[:, 5, 0:SW], psum[:, 7, 0:SW]]
        ps_stat = psum[:, 5, 0:ST * 3]
        weights_in, x_in, x3_done, x3_stored = sem("weights_in"), sem("x_in"), sem("x3_done"), sem("x3_stored")
        diag_done = sem("diag_done")
        proj_done, upre_out, conv_done, u_done = sem("proj_done"), sem("upre_out"), sem("conv_done"), sem("u_done")
        halo = sem("halo")
        wx_done, sq_done, stat_done, rsd_done, rms_step, rb_done, normed_done = (
            sem("wx_done"), sem("sq_done"), sem("stat_done"), sem("rsd_done"), sem("rms_step"), sem("rb_done"), sem("normed_done"))
        bc_stored, bc_in = sem("bc_stored"), sem("bc_in")
        wdt_done, abs_done, exp_done, soft_done, relu_done, delta_done, du_done = (
            sem("wdt_done"), sem("abs_done"), sem("expneg_done"), sem("soft_done"), sem("relu_done"), sem("delta_done"), sem("du_done"))
        skip_done, gate_mm, gate_out = sem("skip_done"), sem("gate_mm"), sem("gate_out")
        decay_done, drive_done, scan_done, carry_done, read_done, sum_done = (
            sem("decay_done"), sem("drive_done"), sem("scan_done"), sem("carry_done"), sem("read_done"), sem("sum_done"))
        y_done, out_mm = sem("y_done"), sem("out_mm")
        tmp = ln.square
        block = ctx.enter_context(nc.Block())
        xsrc = scratch.x2.rearrange("(k p) t -> p k t", p=P)
        xdst = scratch.x3.rearrange("(k p) t -> p k t", p=P)
        UNITS = GROUPS * DT
        HALF = DT // 2

        @block.sync
        def _(sp):
            sp.dma_start(x[:], xsrc[:, :, 0:SW]).then_inc(x_in, 16)
            small = [(wx, d["wx"].rearrange("(k p) m -> p k m", p=P)), (wdt, d["wdt"]), (convw, d["convw"]), (convb, d["convb"]),
                     (dtb, d["dtb"]), (amat, d["a"]), (dpar, d["d"]), (lnw, d["lnw"]), (group, d["group"]),
                     (win, d["win"].rearrange("(k p) m -> p k m", p=P)), (wout, d["wout"].rearrange("(k p) m -> p k m", p=P))]
            for dst, src in small:
                sp.dma_start(dst[:], src).then_inc(weights_in, 16)
            def rows_and_store(c):
                sp.wait_ge(normed_done, c + 1)
                sp.dma_start(scratch.bc, normed[RANK:ROWS, :]).then_inc(bc_stored, 16)
                sp.wait_ge(bc_stored, c * 16 + 16)
                sp.wait_ge(read_done, c * UNITS)
                sp.dma_start(bc[:].rearrange("p s n t -> p (s n) t"),
                             scratch.bc.unsqueeze(0).to_broadcast([P, 2 * NST, SW])).then_inc(bc_in, 16)
                sp.wait_ge(x3_done, (c + 1) * KT)
                sp.dma_start(xdst[:, :, bass.ds(c * SW, SW)], x3[:]).then_inc(x3_stored, 16)

            for c in range(SCH):
                rows_and_store(c)
                if c + 1 < SCH:
                    sp.dma_start(x[:], xsrc[:, :, (c + 1) * SW:(c + 2) * SW]).then_inc(x_in, 16)
            sp.wait_ge(x3_stored, 16 * SCH)

        @block.gpsimd
        def _(pool):
            pool.wait_ge(weights_in, 176)
            nc.gpsimd.memset(state[:], 0.0).then_inc(halo, 1)
            nc.gpsimd.memset(upre[:], 0.0).then_inc(halo, 1)
            for t in range(DT):
                for k in range(TAPS):
                    nc.gpsimd.tensor_scalar(conv[:, t, k, :], g.ident[:], convw[:, t, k:k + 1], 0.0, ALU.mult, ALU.add).then_inc(diag_done, 1)
                nc.gpsimd.tensor_scalar(skip[:, t, :], g.ident[:], dpar[:, t:t + 1], 0.0, ALU.mult, ALU.add).then_inc(diag_done, 1)
            for c in range(SCH):
                for t in range(DT):
                    pool.wait_ge(delta_done, c * DT + t + 1)
                    pool.wait_ge(skip_done, c * DT + t + 1)
                    nc.gpsimd.tensor_tensor(u[:, t, :], delta[:, t, :], u[:, t, :], ALU.mult).then_inc(du_done, 1)
                pool.wait_ge(bc_in, c * 16 + 16)
                for q in range(UNITS):
                    pool.wait_ge(scan_done, (c * UNITS + q + 1) * NG)
                    pool.wait_ge(carry_done, c * UNITS + q + 1)
                    gr = q // DT
                    nc.gpsimd.tensor_tensor(scan[:, q % 2], scan[:, q % 2], bc[:, 1, gr * NG:(gr + 1) * NG, :],
                                            ALU.mult).then_inc(read_done, 1)

        @block.tensor
        def _(pe):
            pe.wait_ge(weights_in, 176)
            pe.wait_ge(diag_done, DT * (TAPS + 1))
            pe.wait_ge(halo, 2)
            for c in range(SCH):
                pe.wait_ge(x_in, c * 16 + 16)
                pe.wait_ge(x3_done, c * KT)
                ln.tensor(pe, c, x[:])
                pe.wait_ge(ln.h_done, (c + 1) * KT)

                def conv_tile(t):
                    pe.wait_ge(upre_out, c * DT + t + 1)
                    if t >= 2:
                        pe.wait_ge(u_done, c * DT + t - 1)
                    for k in range(TAPS):
                        last = nc.tensor.matmul(ps_b[t % 2], conv[:, t, k, :], upre[:, t, k:k + SW], start=(k == 0), stop=(k == TAPS - 1))
                    last.then_inc(conv_done, 1)

                for t in range(DT):
                    if t >= 2:
                        pe.wait_ge(upre_out, c * DT + t - 1)
                    for k in range(KT):
                        last = nc.tensor.matmul(ps_a[t % 2], win[:, k, t * P:(t + 1) * P], ln.h[:, k, :], start=(k == 0), stop=(k == KT - 1))
                    last.then_inc(proj_done, 1)
                    if t > 0:
                        conv_tile(t - 1)
                conv_tile(DT - 1)
                pe.wait_ge(u_done, (c + 1) * DT)
                for t in range(DT):
                    last = nc.tensor.matmul(ps_a[0][0:ROWS, :], wx[:, t, :], u[:, t, :], start=(t == 0), stop=(t == DT - 1))
                last.then_inc(wx_done, 1)
                pe.wait_ge(sq_done, c * 2 + 2)
                for t in range(ST):
                    last = nc.tensor.matmul(ps_stat[:, 3 * t:3 * t + 3], sq[:, t * P:(t + 1) * P], group[:], start=True, stop=True)
                last.then_inc(stat_done, 1)
                pe.wait_ge(rms_step, c * 4 + 4)
                for t in range(ST):
                    last = nc.tensor.matmul(ps_a[1][0:ROWS, t * P:(t + 1) * P], rwide[:, t, :], g.ident[:], start=True, stop=True)
                last.then_inc(rb_done, 1)
                for t in range(DT):
                    nc.tensor.matmul(ps_y[:, t, :], skip[:, t, :], u[:, t, :], start=(t % 2 == 0), stop=False,
                                     skip_group_check=True).then_inc(skip_done, 1)
                pe.wait_ge(normed_done, c + 1)
                for t in range(DT):
                    if t >= 2:
                        pe.wait_ge(relu_done, c * DT + t - 1)
                        pe.wait_ge(abs_done, c * DT + t - 1)
                    nc.tensor.matmul(ps_a[t % 2], wdt[:, t * P:(t + 1) * P], normed[0:RANK, :], start=True, stop=True).then_inc(wdt_done, 1)
                for t in range(DT):
                    if t >= 2:
                        pe.wait_ge(gate_out, c * DT + t - 1)
                    for k in range(KT):
                        last = nc.tensor.matmul(ps_b[t % 2], win[:, k, DI + t * P:DI + (t + 1) * P], ln.h[:, k, :],
                                                start=(k == 0), stop=(k == KT - 1))
                    last.then_inc(gate_mm, 1)
                for q in range(UNITS):
                    gr, t = q // DT, q % DT
                    pe.wait_ge(read_done, c * UNITS + q + 1)
                    for n in range(NG):
                        last = nc.tensor.matmul(ps_y[:, t, :], g.ident[:], scan[:, q % 2, n, :], start=False,
                                                stop=(gr == GROUPS - 1 and n == NG - 1), skip_group_check=True)
                    last.then_inc(sum_done, 1)
                for m in range(KT):
                    pe.wait_ge(y_done, c + 1)
                    if m >= 2:
                        pe.wait_ge(x3_done, c * KT + m - 1)
                    for t in range(DT):
                        last = nc.tensor.matmul(ps_a[m % 2], wout[:, t, m * P:(m + 1) * P], u[:, t, :], start=(t == 0), stop=(t == DT - 1))
                    last.then_inc(out_mm, 1)

        @block.scalar
        def _(act):
            act.wait_ge(weights_in, 176)
            for c in range(SCH):
                ln.scalar(act, c, h_free=(gate_mm, c * DT))
                for t in range(DT):
                    act.wait_ge(conv_done, c * DT + t + 1)
                    act.wait_ge(out_mm, c * KT)
                    nc.scalar.activation(u[:, t, :], ps_b[t % 2], ACT.Silu, bias=convb[:, t:t + 1]).then_inc(u_done, 1)
                act.wait_ge(wx_done, c + 1)
                nc.scalar.activation(sq[:], ps_a[0][0:ROWS, :], ACT.Square).then_inc(sq_done, 1)
                nc.scalar.copy(sp_sb[:], ps_a[0][0:ROWS, :]).then_inc(sq_done, 1)
                act.wait_ge(stat_done, c + 1)
                nc.scalar.activation(rsd[:].rearrange("p t s -> p (t s)"), ps_stat, ACT.Sqrt, bias=g.rms_eps[:, 0:1]).then_inc(rsd_done, 1)
                for t in range(DT):
                    act.wait_ge(wdt_done, c * DT + t + 1)
                    nc.scalar.activation(delta[:, t, :], ps_a[t % 2], ACT.Abs, bias=dtb[:, t:t + 1]).then_inc(abs_done, 1)
                act.wait_ge(abs_done, (c + 1) * DT)
                nc.scalar.activation(delta[:], delta[:], ACT.Exp, scale=-1.0).then_inc(exp_done, 1)
                act.wait_ge(exp_done, c + 1)
                nc.scalar.activation(delta[:], delta[:], ACT.Ln, bias=1.0).then_inc(soft_done, 1)
                for t in range(DT):
                    act.wait_ge(gate_mm, c * DT + t + 1)
                    act.wait_ge(y_done, c)
                    nc.scalar.activation(gate[:, t, :], ps_b[t % 2], ACT.Silu).then_inc(gate_out, 1)
                for q in range(UNITS):
                    gr, t = q // DT, q % DT
                    act.wait_ge(delta_done, (c + 1) * DT)
                    if q >= 2:
                        act.wait_ge(scan_done, (c * UNITS + q - 1) * NG)
                    for n in range(NG):
                        s = gr * NG + n
                        nc.scalar.activation(decay[:, q % 2, n, :], delta[:, t, :], ACT.Exp,
                                             scale=amat[:, t, s:s + 1]).then_inc(decay_done, 1)

        @block.vector
        def _(dve):
            dve.wait_ge(weights_in, 176)
            dve.wait_ge(halo, 2)
            for c in range(SCH):
                dve.wait_ge(x_in, c * 16 + 16)
                ln.vector(dve, c, x[:])
                dve.wait_ge(conv_done, c * DT)
                nc.vector.tensor_copy(upre[:, :, 0:TAPS - 1], upre[:, :, SW:SW + TAPS - 1]).then_inc(halo, 1)
                dve.wait_ge(halo, c + 3)
                for t in range(DT):
                    dve.wait_ge(proj_done, c * DT + t + 1)
                    nc.vector.tensor_copy(upre[:, t, TAPS - 1:], ps_a[t % 2]).then_inc(upre_out, 1)
                dve.wait_ge(rsd_done, c + 1)
                nc.vector.reciprocal(rinv[:], rsd[:]).then_inc(rms_step, 1)
                dve.wait_ge(rms_step, c * 4 + 1)
                for s, (at, n) in enumerate(((0, RANK), (RANK, NST), (RANK + NST, NST))):
                    nc.vector.tensor_copy(rwide[:, :, at:at + n], rinv[:, :, s:s + 1].to_broadcast([P, ST, n])).then_inc(rms_step, 1)
                dve.wait_ge(rb_done, c + 1)
                dve.wait_ge(bc_stored, c * 16)
                nc.vector.scalar_tensor_tensor(normed[:], sp_sb[:], lnw[:, 0:1], ps_a[1][0:ROWS, :], ALU.mult,
                                               ALU.mult).then_inc(normed_done, 1)
                for t in range(DT):
                    dve.wait_ge(wdt_done, c * DT + t + 1)
                    dve.wait_ge(abs_done, c * DT + t + 1)
                    nc.vector.tensor_scalar(decay[:].rearrange("p s n t -> p (s n) t")[:, t, :], ps_a[t % 2], dtb[:, t:t + 1], 0.0,
                                            ALU.add, ALU.max).then_inc(relu_done, 1)
                dve.wait_ge(soft_done, c + 1)
                dve.wait_ge(relu_done, (c + 1) * DT)
                for t in range(DT):
                    nc.vector.tensor_tensor(delta[:, t, :], delta[:, t, :], decay[:].rearrange("p s n t -> p (s n) t")[:, t, :],
                                            ALU.add).then_inc(delta_done, 1)
                dve.wait_ge(bc_in, c * 16 + 16)
                for q in range(UNITS):
                    gr, t = q // DT, q % DT
                    dve.wait_ge(du_done, c * DT + t + 1)
                    if q >= 2:
                        dve.wait_ge(sum_done, c * UNITS + q - 1)
                    nc.vector.tensor_tensor(scan[:, q % 2], u[:, t, :].unsqueeze(1).to_broadcast([P, NG, SW]),
                                            bc[:, 0, gr * NG:(gr + 1) * NG, :], ALU.mult).then_inc(drive_done, 1)
                    dve.wait_ge(drive_done, c * UNITS + q + 1)
                    if gr == 0:
                        dve.wait_ge(carry_done, c * UNITS)
                    for n in range(NG):
                        s = gr * NG + n
                        dve.wait_ge(decay_done, (c * UNITS + q) * NG + n + 1)
                        nc.vector.tensor_tensor_scan(scan[:, q % 2, n, :], decay[:, q % 2, n, :], scan[:, q % 2, n, :],
                                                     state[:, t, s:s + 1], ALU.mult, ALU.add).then_inc(scan_done, 1)
                    dve.wait_ge(scan_done, (c * UNITS + q + 1) * NG)
                    nc.vector.tensor_copy(state[:, t, gr * NG:(gr + 1) * NG], scan[:, q % 2, :, SW - 1]).then_inc(carry_done, 1)
                dve.wait_ge(sum_done, (c + 1) * UNITS)
                dve.wait_ge(gate_out, (c + 1) * DT)
                nc.vector.tensor_tensor(u[:], gate[:], ps_y, ALU.mult).then_inc(y_done, 1)
                dve.wait_ge(x3_stored, c * 16)
                for m in range(KT):
                    dve.wait_ge(out_mm, c * KT + m + 1)
                    nc.vector.scalar_tensor_tensor(x3[:, m, :], ps_a[m % 2], g.mod[:, 1, GATE_A, m:m + 1], x[:, m, :],
                                                   ALU.mult, ALU.add).then_inc(x3_done, 1)


def permuted_mlp(nc, d, g, scratch, out):
    MODS = (SCALE_B, SHIFT_B, GATE_B)
    with ExitStack() as ctx:
        sb, sem = sb_alloc(ctx, nc), sem_alloc(ctx, nc, "mlp")
        perm = sb("mlp_perm", [P, KT], U32)
        rows = sb("mlp_rows", [P, NCH, KT], U32)
        x = sb("mlp_x", [P, KT, T])
        modp = sb("mlp_mod", [P, KT, 4])
        modcols = sb("mlp_modcols", [P, KT, 4])
        up = sb("mlp_up", [P, KT, MM])
        down = sb("mlp_down", [P, MH, MD])
        hid = sb("mlp_hid", [P, 4, W])
        y = sb("mlp_y", [P, 2, KT, W])
        psum = ctx.enter_context(nc.psum_tensor("mlp_psum", [P, 8, W], F32))
        scale = sb("mlp_scale", [P, KT])
        shift = sb("mlp_shift", [P, KT])
        ln = LayerNorm(nc, ctx, "ln4", W, g, psum, (4, 5, 6), scale, shift)
        ps_up = [psum[:, b, :] for b in (4, 5, 6, 7)]
        ps_y = [psum[:, k, :] for k in range(KT)]
        weights_in, perm_in, x_in, mod_set, mod_stored, mod_in, cols_done = (
            sem("weights_in"), sem("perm_in"), sem("x_in"), sem("mod_set"), sem("mod_stored"), sem("mod_in"), sem("cols_done"))
        rows_done = sem("rows_done")
        up_done, hid_done, down_done, y_done = sem("up_done"), sem("hid_done"), sem("down_done"), sem("y_done")
        y_stored = [sem("y_even_stored"), sem("y_odd_stored")]
        block = ctx.enter_context(nc.Block())

        @block.sync
        def _(sp):
            sp.dma_start(up[:], d["up"].rearrange("p (k m) -> p k m", k=KT)).then_inc(weights_in, 16)
            sp.dma_start(down[:], d["down"].rearrange("p (h e) -> p h e", h=MH)).then_inc(weights_in, 16)
            sp.wait_ge(mod_set, 4)
            sp.dma_start(scratch.modb.rearrange("(k p) s -> p k s", p=P), modcols[:]).then_inc(mod_stored, 16)

        @block.gpsimd
        def _(pool):
            pool.dma_start(perm[:], d["perm"]).then_inc(perm_in, 16)
            pool.wait_ge(perm_in, 16)
            for k in range(KT):
                pool.indirect_dma_start(x[:, k, :], None, scratch.x3, bass.IndirectOffsetOnAxis(ap=perm[:, k:k + 1], axis=0)).then_inc(x_in, 16)
            pool.wait_ge(mod_stored, 16)
            for k in range(KT):
                pool.indirect_dma_start(modp[:, k, :], None, scratch.modb, bass.IndirectOffsetOnAxis(ap=perm[:, k:k + 1], axis=0)).then_inc(mod_in, 16)
            pool.wait_ge(rows_done, NCH)
            for i in range(NCH):
                for k in range(KT):
                    pool.wait_ge(y_done, i * KT + k + 1)
                    pool.indirect_dma_start(out, bass.IndirectOffsetOnAxis(ap=rows[:, i, k:k + 1], axis=0), y[:, i % 2, k, :], None
                                            ).then_inc(y_stored[i % 2], 16)
            for b in range(2):
                pool.wait_ge(y_stored[b], 16 * KT * NCH // 2)

        @block.tensor
        def _(pe):
            pe.wait_ge(weights_in, 32)
            pe.wait_ge(x_in, 16 * KT)
            for c in range(NCH // 2):
                for b in range(2):
                    i = c * 2 + b
                    pe.wait_ge(hid_done, i * MH)
                    ln.tensor(pe, i, x[:, :, bass.ds(i * W, W)])
                    pe.wait_ge(ln.h_done, (i + 1) * KT)

                    def down_head(h):
                        pe.wait_ge(hid_done, i * MH + h + 1)
                        if h < KT * 4 and h % 4 == 0:
                            pe.wait_ge(y_done, i * KT)
                        r = MD * (h % 4)
                        nc.tensor.matmul(ps_y[h // 4][r:r + MD, :], down[:, h, :], hid[:, h % 4, :], start=True, stop=True).then_inc(down_done, 1)

                    for h in range(MH):
                        r = MD * (h % 4)
                        if h >= 4:
                            pe.wait_ge(hid_done, i * MH + h - 3)
                        nc.tensor.matmul(ps_up[h % 4], up[r:r + MD, h // 4, :], ln.h[r:r + MD, h // 4, :], start=True, stop=True).then_inc(up_done, 1)
                        if h >= 2:
                            down_head(h - 2)
                    down_head(MH - 2)
                    down_head(MH - 1)

        @block.scalar
        def _(act):
            act.wait_ge(cols_done, 2)
            for c in range(NCH // 2):
                for b in range(2):
                    i = c * 2 + b
                    ln.scalar(act, i, h_free=(up_done, i * MH))
                    for h in range(MH):
                        act.wait_ge(up_done, i * MH + h + 1)
                        if h < 4:
                            act.wait_ge(down_done, i * MH)
                        else:
                            act.wait_ge(down_done, i * MH + h - 3)
                        nc.scalar.activation(hid[:, h % 4, :], ps_up[h % 4], ACT.Gelu).then_inc(hid_done, 1)

        @block.vector
        def _(dve):
            nc.vector.memset(modcols[:], 0.0).then_inc(mod_set, 1)
            dve.wait_ge(mod_set, 1)
            for s, which in enumerate(MODS):
                nc.vector.tensor_copy(modcols[:, :, s], g.mod[:, 1, which, :]).then_inc(mod_set, 1)
            dve.wait_ge(perm_in, 16)
            for i in range(NCH):
                nc.vector.tensor_scalar(rows[:, i, :], perm[:], float(i * D), None, ALU.add).then_inc(rows_done, 1)
            dve.wait_ge(mod_in, 16 * KT)
            nc.vector.tensor_copy(scale[:], modp[:, :, 0]).then_inc(cols_done, 1)
            nc.vector.tensor_copy(shift[:], modp[:, :, 1]).then_inc(cols_done, 1)
            dve.wait_ge(x_in, 16 * KT)
            for c in range(NCH // 2):
                for b in range(2):
                    i = c * 2 + b
                    ln.vector(dve, i, x[:, :, bass.ds(i * W, W)])
                    dve.wait_ge(y_stored[b], c * 16 * KT)
                    for k in range(KT):
                        dve.wait_ge(down_done, i * MH + (k + 1) * 4)
                        nc.vector.scalar_tensor_tensor(y[:, b, k, :], ps_y[k], modp[:, k, 2:3], x[:, k, bass.ds(i * W, W)],
                                                       ALU.mult, ALU.add).then_inc(y_done, 1)


STAGES = 6


def build(nc, d, out, stages=STAGES):
    scratch = Consts()
    scratch.parts = nc.dram_tensor("parts", [PARTS, 2 * HEADS * E, T], BF16).ap()
    neg = nc.dram_tensor("negmax_rows", [HEADS, 2, T // P, 4, 32], BF16).ap()

    class Rows:
        def __getitem__(self, hh):
            return neg[bass.ds(hh, 1)].rearrange("o s t q p -> (o s) t q p")
    scratch.neg = Rows()
    scratch.num = nc.dram_tensor("att_num", [HEADS * E, T], F32).ap()
    scratch.den = nc.dram_tensor("att_den", [HEADS, T], F32).ap()
    scratch.rec = nc.dram_tensor("att_den_inv", [HEADS, T], F32).ap()
    scratch.x2 = nc.dram_tensor("x_layer0", [D, T], F32).ap()
    scratch.bc = nc.dram_tensor("bc_rows", [2 * NST, SW], F32).ap()
    scratch.x3 = nc.dram_tensor("x_after_ssm", [D, T], F32).ap()
    scratch.modb = nc.dram_tensor("mod_rows", [D, 4], F32).ap()
    with ExitStack() as ctx:
        sb = sb_alloc(ctx, nc)
        g = Consts()
        g.ident = sb("ident", [P, P])
        g.inv_d = sb("inv_d", [P, P])
        g.ones_row = sb("ones_row", [1, W])
        g.ln_eps = sb("ln_eps", [P, 1])
        g.rms_eps = sb("rms_eps", [P, 1])
        g.mod = sb("mod", [P, 2, 6, KT])
        modulation(nc, d, g)
        with ExitStack() as layer0:
            g.v = layer0.enter_context(nc.sbuf_tensor("v_tokens", [P, T // P * HEADS * E], F32))
            if stages > 1:
                qkv(nc, d, g, scratch)
            if stages > 2:
                attention(nc, d, g, scratch)
        if stages > 3:
            experts(nc, d, g, scratch)
        if stages > 4:
            state_space(nc, d, g, scratch)
        if stages > 5:
            permuted_mlp(nc, d, g, scratch, out)


def layouts(a):
    import numpy as np

    def cols(v, n):
        return np.ascontiguousarray(v.reshape(n, P).T)

    def by_part(w):
        return np.ascontiguousarray(np.moveaxis(w.reshape((HEADS, E, 2) + w.shape[1:]), 2, 0)).reshape(w.shape)

    t = lambda w: np.ascontiguousarray(w.T)
    f = np.float32
    up = a["L1_ffn_up"].reshape(KT, 4, MD, MM)
    group = np.zeros((RANK + 2 * NST, 3), f)
    group[:RANK, 0], group[RANK:RANK + NST, 1], group[RANK + NST:, 2] = 1.0 / RANK, 1.0 / NST, 1.0 / NST
    pick = np.zeros((EXPERTS, EXPERTS, P), f)
    pick[np.arange(EXPERTS), np.arange(EXPERTS)] = 1.0
    return {
        "ones": np.ones((2, HEADS * T), mybir.dt.np(BF16)),
        "x": t(a["L0_attn_x"].reshape(T, D)),
        "wqk": t(by_part(a["L0_attn_Wqk_w"])), "bqk": by_part(a["L0_attn_Wqk_b"])[:, None].copy(),
        "wv": t(a["L0_attn_Wv_w"]), "bv": a["L0_attn_Wv_b"][None].copy(),
        "wo": np.concatenate([a["L0_attn_Wo_w"].T, a["L0_attn_Wo_b"][None]]),
        "wg": t(a["L0_ffn_gate_w"]), "bg": a["L0_ffn_gate_b"][None].copy(),
        "we": np.ascontiguousarray(a["L0_ffn_expert_w"].transpose(0, 2, 1)), "be": a["L0_ffn_expert_b"],
        "c0": cols(a["L0_c"], KT), "c1": cols(a["L1_c"], KT), "wmod0": a["L0_wmod"], "wmod1": a["L1_wmod"],
        "win": t(a["L1_attn_W_in"]), "wout": t(a["L1_attn_W_out"]), "wx": t(a["L1_attn_Wx"]), "wdt": t(a["L1_attn_Wdt"]),
        "convw": np.ascontiguousarray(a["L1_attn_conv_w"].reshape(DT, P, TAPS).transpose(1, 0, 2)),
        "convb": cols(a["L1_attn_conv_b"], DT), "dtb": cols(a["L1_attn_dt_bias"], DT), "d": cols(a["L1_attn_D_param"], DT),
        "a": np.ascontiguousarray(a["L1_attn_A"].reshape(DT, P, NST).transpose(1, 0, 2)),
        "lnw": np.concatenate([a["L1_attn_dt_ln_w"], a["L1_attn_b_ln_w"], a["L1_attn_c_ln_w"]])[:, None].copy(),
        "up": np.ascontiguousarray(up.transpose(1, 2, 0, 3)).reshape(P, KT * MM),
        "down": np.ascontiguousarray(a["L1_ffn_down"].transpose(1, 0, 2)).reshape(P, MH * MD),
        "perm": np.ascontiguousarray(a["L1_ffn_perm"].reshape(KT, P).T).view(np.uint32),
        "ident": np.eye(P, dtype=f), "group": group, "pick": pick.reshape(EXPERTS, EXPERTS * P),
        "iota": np.tile(np.arange(EXPERTS, dtype=f), (P, 1)),
    }


def kernel(**inputs):
    import numpy as np
    import concourse.bacc as bacc
    from concourse.bass_utils import run_bass_kernel_spmd

    nc = bacc.Bacc("TRN2", target_bir_lowering=False, num_devices=1)
    arrays = layouts({k: np.asarray(v) for k, v in inputs.items()})
    d = {k: nc.dram_tensor("in_" + k, a.shape, mybir.dt.from_np(a.dtype), kind="ExternalInput").ap() for k, a in arrays.items()}
    out = nc.dram_tensor("out", [NCH * D, W], F32, kind="ExternalOutput").ap()
    build(nc, d, out)
    r = run_bass_kernel_spmd(nc, [{"in_" + k: a for k, a in arrays.items()}], core_ids=[0])
    y = r.results[0]["out"].reshape(NCH, D, W)
    return np.ascontiguousarray(y.transpose(0, 2, 1)).reshape(1, T, D)
```

```python
from contextlib import ExitStack

import concourse.bass as bass
from concourse import mybir

F32 = mybir.dt.float32
BF16 = mybir.dt.bfloat16
U32 = mybir.dt.uint32
ALU = mybir.AluOpType
ACT = mybir.ActivationFunctionType
AX = mybir.AxisListType

P = 128
T = 2048
D = 512
KT = D // P
W = 512
NCH = T // W
HEADS, E = 8, 8
PARTS = 3
PAIRS = PARTS * PARTS
QROWS = PAIRS * E
EXPERTS = 8
LN_EPS = 1e-5
SHIFT_A, SCALE_A, GATE_A, SHIFT_B, SCALE_B, GATE_B = range(6)

DI = 1024
DT = DI // P
NST = 16
RANK = 32
TAPS = 4
SW = 256
SCH = T // SW
NG = 4
SLOTS = 3
RMS_EPS = 1e-6

MH, MD, MM = 16, 32, 128


def sb_alloc(ctx, nc):
    def sb(name, shape, dt=F32):
        return ctx.enter_context(nc.sbuf_tensor(name, shape, dt))
    return sb


def sem_alloc(ctx, nc, prefix):
    def sem(name):
        return ctx.enter_context(nc.semaphore(prefix + "_" + name))
    return sem


class LayerNorm:

    def __init__(self, nc, ctx, prefix, width, consts, psum, banks, scale, shift):
        sb, sem = sb_alloc(ctx, nc), sem_alloc(ctx, nc, prefix)
        self.nc, self.width, self.tiles = nc, width, width // P
        self.c = consts
        self.centred = sb(prefix + "_centred", [P, KT, width])
        self.square = sb(prefix + "_square", [P, KT, width])
        self.sd = sb(prefix + "_sd", [P, self.tiles])
        self.rstd = sb(prefix + "_rstd", [P, self.tiles])
        self.h = sb(prefix + "_h", [P, KT, width])
        self.ps_mean = psum[:, banks[0], 0:width]
        self.ps_var = psum[:, banks[1], 0:self.tiles]
        self.ps_rstd = psum[:, banks[2], 0:width]
        self.scale, self.shift = scale, shift
        self.mean_done, self.centred_done = sem("mean_done"), sem("centred_done")
        self.square_done, self.var_done = sem("square_done"), sem("var_done")
        self.sd_done, self.rstd_done = sem("sd_done"), sem("rstd_done")
        self.bcast_done, self.norm_done, self.h_done = sem("bcast_done"), sem("norm_done"), sem("h_done")

    def tensor(self, pe, i, x):
        nc = self.nc
        for k in range(KT):
            last = nc.tensor.matmul(self.ps_mean, self.c.inv_d[:], x[:, k, :], start=(k == 0), stop=(k == KT - 1))
        last.then_inc(self.mean_done, 1)
        pe.wait_ge(self.square_done, i + 1)
        for t in range(self.tiles):
            for k in range(KT):
                last = nc.tensor.matmul(self.ps_var[:, t:t + 1], self.square[:, k, t * P:(t + 1) * P],
                                        self.c.inv_d[:, 0:1], start=(k == 0), stop=(k == KT - 1))
        last.then_inc(self.var_done, 1)
        pe.wait_ge(self.rstd_done, i + 1)
        for t in range(self.tiles):
            last = nc.tensor.matmul(self.ps_rstd[:, t * P:(t + 1) * P], self.rstd[:, t:t + 1].to_broadcast([P, P]),
                                    self.c.ident[:], start=True, stop=True)
        last.then_inc(self.bcast_done, 1)

    def vector(self, dve, i, x):
        nc = self.nc
        w = self.width
        dve.wait_ge(self.mean_done, i + 1)
        dve.wait_ge(self.h_done, i * KT)
        nc.vector.tensor_tensor(self.centred[:], x, self.ps_mean.unsqueeze(1).to_broadcast([P, KT, w]),
                                ALU.subtract).then_inc(self.centred_done, 1)
        dve.wait_ge(self.sd_done, i + 1)
        nc.vector.reciprocal(self.rstd[:], self.sd[:]).then_inc(self.rstd_done, 1)
        dve.wait_ge(self.bcast_done, i + 1)
        nc.vector.tensor_tensor(self.centred[:], self.centred[:],
                                self.ps_rstd.unsqueeze(1).to_broadcast([P, KT, w]), ALU.mult).then_inc(self.norm_done, 1)

    def scalar(self, act, i, h_free=None):
        nc = self.nc
        act.wait_ge(self.centred_done, i + 1)
        nc.scalar.activation(self.square[:], self.centred[:], ACT.Square).then_inc(self.square_done, 1)
        act.wait_ge(self.var_done, i + 1)
        nc.scalar.activation(self.sd[:], self.ps_var, ACT.Sqrt, bias=self.c.ln_eps[:, 0:1]).then_inc(self.sd_done, 1)
        act.wait_ge(self.norm_done, i + 1)
        if h_free is not None:
            act.wait_ge(h_free[0], h_free[1])
        for k in range(KT):
            nc.scalar.activation(self.h[:, k, :], self.centred[:, k, :], ACT.Identity, bias=self.shift[:, k:k + 1],
                                 scale=self.scale[:, k:k + 1]).then_inc(self.h_done, 1)


class Consts:
    pass


def modulation(nc, d, g):
    with ExitStack() as ctx:
        sb, sem = sb_alloc(ctx, nc), sem_alloc(ctx, nc, "mod")
        wmod = sb("mod_w", [P, 2, KT, 6 * D])
        ccol = sb("mod_c", [P, 2 * KT])
        cact = sb("mod_silu_c", [P, 2 * KT])
        sign = sb("mod_sign", [P, 2, 2, KT])
        mag = sb("mod_mag", [P, 2, 2, KT])
        psum = ctx.enter_context(nc.psum_tensor("mod_psum", [P, 2, 6 * KT], F32))
        consts_in, c_in, w_in = sem("consts_in"), sem("c_in"), [sem("w0_in"), sem("w1_in")]
        silu_done, prod_done, step = sem("silu_done"), sem("prod_done"), sem("step")
        block = ctx.enter_context(nc.Block())

        @block.sync
        def _(sp):
            for layer in range(2):
                sp.dma_start(ccol[:, layer * KT:(layer + 1) * KT], d[f"c{layer}"]).then_inc(c_in, 16)
            for layer in range(2):
                for k in range(KT):
                    sp.dma_start(wmod[:, layer, k, :], d[f"wmod{layer}"][k * P:(k + 1) * P, :]).then_inc(w_in[layer], 16)
            sp.dma_start(g.ident[:], d["ident"]).then_inc(consts_in, 16)
            sp.wait_ge(consts_in, 16)

        @block.scalar
        def _(act):
            act.wait_ge(c_in, 32)
            nc.scalar.activation(cact[:], ccol[:], ACT.Silu).then_inc(silu_done, 1)

        @block.tensor
        def _(pe):
            pe.wait_ge(silu_done, 1)
            for layer in range(2):
                pe.wait_ge(w_in[layer], 16 * KT)
                for m in range(6 * KT):
                    for k in range(KT):
                        last = nc.tensor.matmul(psum[:, layer, m:m + 1], wmod[:, layer, k, m * P:(m + 1) * P],
                                                cact[:, layer * KT + k:layer * KT + k + 1],
                                                start=(k == 0), stop=(k == KT - 1))
                last.then_inc(prod_done, 1)

        @block.vector
        def _(dve):
            nc.vector.memset(g.inv_d[:], 1.0 / D)
            nc.vector.memset(g.ones_row[:], 1.0)
            nc.vector.memset(g.ln_eps[:], LN_EPS)
            nc.vector.memset(g.rms_eps[:], RMS_EPS)
            dve.wait_ge(prod_done, 2)
            nc.vector.tensor_copy(g.mod[:].rearrange("p l s k -> p (l s k)"),
                                  psum[:].rearrange("p l m -> p (l m)")).then_inc(step, 1)
            dve.wait_ge(step, 1)
            scales = g.mod[:, :, SCALE_A::3, :]
            gates = g.mod[:, :, GATE_A::3, :]
            nc.vector.tensor_scalar(scales, scales, 1.0, None, ALU.add)
            nc.vector.tensor_scalar(sign[:], gates, 0.0, 2.0, ALU.is_ge, ALU.mult).then_inc(step, 1)
            for layer in range(2):
                gate = g.mod[:, layer, GATE_A::3, :]
                nc.vector.scalar_tensor_tensor(mag[:, layer], gate, -1.0, gate, ALU.mult, ALU.max).then_inc(step, 1)
            dve.wait_ge(step, 4)
            nc.vector.tensor_scalar(mag[:], mag[:], 0.25, None, ALU.max).then_inc(step, 1)
            dve.wait_ge(step, 5)
            for layer in range(2):
                nc.vector.scalar_tensor_tensor(g.mod[:, layer, GATE_A::3, :], sign[:, layer], -1.0, mag[:, layer],
                                               ALU.add, ALU.mult)


def qkv(nc, d, g, scratch):
    with ExitStack() as ctx:
        sb, sem = sb_alloc(ctx, nc), sem_alloc(ctx, nc, "qkv")
        x = sb("qkv_x", [P, KT, T])
        wqk = sb("qkv_wqk", [P, KT, 2 * HEADS * E])
        qkb = sb("qkv_bqk", [P, 1])
        wv = sb("qkv_wv", [P, KT, HEADS * E])
        bv = sb("qkv_bv", [1, HEADS * E])
        qk = sb("qkv_qk", [P, W])
        rest = sb("qkv_rest", [P, W])
        parts = sb("qkv_parts", [P, 2, PARTS, W], BF16)
        psum = ctx.enter_context(nc.psum_tensor("qkv_psum", [P, 8, W], F32))
        ps_qk, ps_v = psum[:, 0, :], psum[:, 1, 0:W // P * HEADS * E]
        ln = LayerNorm(nc, ctx, "ln1", W, g, psum, (4, 5, 6), g.mod[:, 0, SCALE_A], g.mod[:, 0, SHIFT_A])
        weights_in = sem("weights_in")
        x_in = [sem("x_even_in"), sem("x_odd_in")]
        qk_done, v_done = sem("qk_done"), sem("v_done")
        qk_out, v_out = sem("qk_out"), sem("v_out")
        split = sem("split")
        parts_stored = [sem("parts_even_stored"), sem("parts_odd_stored")]
        block = ctx.enter_context(nc.Block())
        xsrc = d["x"].rearrange("(k p) t -> p k t", p=P)

        @block.sync
        def _(sp):
            for i in range(NCH):
                if i >= 2:
                    sp.wait_ge(x_in[i % 2], 16 * (i // 2))
                sp.dma_start(x[:, :, i * W:(i + 1) * W], xsrc[:, :, i * W:(i + 1) * W]).then_inc(x_in[i % 2], 16)
                if i == 1:
                    sp.dma_start(wqk[:], d["wqk"].rearrange("(k p) m -> p k m", p=P)).then_inc(weights_in, 16)
                    sp.dma_start(wv[:], d["wv"].rearrange("(k p) m -> p k m", p=P)).then_inc(weights_in, 16)
                    sp.dma_start(qkb[:], d["bqk"]).then_inc(weights_in, 16)
                    sp.dma_start(bv[:], d["bv"]).then_inc(weights_in, 16)
            for i in range(NCH):
                sp.wait_ge(split, (i + 1) * 5)
                sp.dma_start(scratch.parts[:, :, i * W:(i + 1) * W].rearrange("s p t -> p s t"),
                             parts[:, i % 2]).then_inc(parts_stored[i % 2], 16)
            for b in range(2):
                sp.wait_ge(parts_stored[b], 16 * NCH // 2)

        @block.tensor
        def _(pe):
            pe.wait_ge(weights_in, 64)
            for c in range(NCH // 2):
                for b in range(2):
                    i = c * 2 + b
                    pe.wait_ge(x_in[b], c * 16 + 16)
                    ln.tensor(pe, i, x[:, :, bass.ds(i * W, W)])
                    pe.wait_ge(ln.h_done, (i + 1) * KT)
                    pe.wait_ge(qk_out, i)
                    for k in range(KT):
                        last = nc.tensor.matmul(ps_qk, wqk[:, k, :], ln.h[:, k, :], start=(k == 0), stop=(k == KT - 1))
                    last.then_inc(qk_done, 1)
                    pe.wait_ge(v_out, i)
                    for t in range(W // P):
                        out = ps_v[:, t * HEADS * E:(t + 1) * HEADS * E]
                        for k in range(KT):
                            nc.tensor.matmul(out, ln.h[:, k, t * P:(t + 1) * P], wv[:, k, :], start=(k == 0), stop=False)
                        last = nc.tensor.matmul(out, g.ones_row[0:1, 0:P], bv[0:1, :], start=False, stop=True)
                    last.then_inc(v_done, 1)

        @block.vector
        def _(dve):
            for c in range(NCH // 2):
                for b in range(2):
                    i = c * 2 + b
                    dve.wait_ge(x_in[b], c * 16 + 16)
                    ln.vector(dve, i, x[:, :, bass.ds(i * W, W)])
                    dve.wait_ge(qk_out, i + 1)
                    dve.wait_ge(parts_stored[b], c * 16)
                    nc.vector.tensor_copy(parts[:, b, 0, :], qk[:]).then_inc(split, 1)
                    dve.wait_ge(split, i * 5 + 1)
                    nc.vector.tensor_tensor(rest[:], qk[:], parts[:, b, 0, :], ALU.subtract).then_inc(split, 1)
                    dve.wait_ge(split, i * 5 + 2)
                    nc.vector.tensor_copy(parts[:, b, 1, :], rest[:]).then_inc(split, 1)
                    dve.wait_ge(split, i * 5 + 3)
                    nc.vector.tensor_tensor(rest[:], rest[:], parts[:, b, 1, :], ALU.subtract).then_inc(split, 1)
                    dve.wait_ge(split, i * 5 + 4)
                    nc.vector.tensor_copy(parts[:, b, 2, :], rest[:]).then_inc(split, 1)

        @block.scalar
        def _(act):
            for c in range(NCH // 2):
                for b in range(2):
                    i = c * 2 + b
                    ln.scalar(act, i, h_free=(v_done, i))
                    act.wait_ge(qk_done, i + 1)
                    act.wait_ge(split, i * 5)
                    nc.scalar.activation(qk[:], ps_qk, ACT.Identity, bias=qkb[:, 0:1]).then_inc(qk_out, 1)
                    act.wait_ge(v_done, i + 1)
                    nc.scalar.copy(g.v[:, bass.ds(i * (W // P * HEADS * E), W // P * HEADS * E)], ps_v).then_inc(v_out, 1)


def attention(nc, d, g, scratch):
    KTILES = T // P
    QC = T // W
    UNITS = KTILES * 2
    RING = 4
    MAXES = KTILES * QC
    MB = 3
    VC = 32
    SUM = E
    with ExitStack() as ctx:
        sb, sem = sb_alloc(ctx, nc), sem_alloc(ctx, nc, "att")
        qst = sb("att_q", [P, HEADS * T], BF16)
        kst = sb("att_k", [P, HEADS * T], BF16)
        vcur = sb("att_v", [P, 2, KTILES, VC])
        probs = sb("att_probs", [P, RING, 2 * W])
        osb = sb("att_out", [P, 2, W])
        rowmax = sb("att_rowmax", [P, MAXES])
        negmax = sb("att_negmax", [P, KTILES])
        negpart = sb("att_negpart", [P, 2, 32], BF16)
        negturn = sb("att_negturn", [P, 2, 32], BF16)
        sums = sb("att_sums", [P, HEADS, T // P])
        rec = sb("att_rec", [P, HEADS, T // P])
        psum = ctx.enter_context(nc.psum_tensor("att_psum", [P, 8, W], F32))
        ps_s = [psum[:, 2 * s:2 * s + 2, :] for s in range(2)]
        ps_o, ps_m = psum[:, 4, :], [psum[:, 5 + s, :] for s in range(MB)]
        stacks_in, v_ones = sem("stacks_in"), sem("v_ones")
        scored, exp_done, pv_done = sem("scored"), sem("exp_done"), sem("pv_done")
        v_ready, o_out = sem("v_ready"), sem("o_out")
        max_scored, max_done, neg_step = sem("max_scored"), sem("max_done"), sem("neg_step")
        neg_stored, neg_in = sem("neg_stored"), sem("neg_in")
        o_stored = [sem("o_even_stored"), sem("o_odd_stored")]
        sums_in, rec_done, rec_stored = sem("sums_in"), sem("rec_done"), sem("rec_stored")
        NEG = 5
        block = ctx.enter_context(nc.Block())

        def head_steps(hh):
            return [bass.ds(hh * T + t * P, P) for t in range(KTILES)], [bass.ds(hh * T + j * W, W) for j in range(QC)]

        @block.sync
        def _(sp):
            sp.dma_start(kst[QROWS:QROWS + 2, :], d["ones"]).then_inc(stacks_in, 16)
            for a in range(PARTS):
                for b in range(PARTS):
                    r = (a * PARTS + b) * E
                    for st, part, row in ((qst, a, 0), (kst, b, HEADS * E)):
                        sp.dma_start(st[r:r + E, :].rearrange("e (h t) -> e h t", h=HEADS),
                                     scratch.parts[part, row:row + HEADS * E, :].rearrange("(h e) t -> e h t", e=E)
                                     ).then_inc(stacks_in, 16)

            def shift_rows(hh):
                sp.wait_ge(neg_step, (hh + 1) * NEG)
                for q in range(4):
                    sp.dma_start(scratch.neg[hh][:, :, q, :].rearrange("s t p -> t s p"),
                                 negturn[32 * q:32 * q + KTILES, :, :]).then_inc(neg_stored, 16)
                sp.wait_ge(neg_stored, (hh + 1) * 64)
                sp.dma_start(qst[QROWS:QROWS + 2, bass.ds(hh * T, T)],
                             scratch.neg[hh].rearrange("s t q p -> s (t q p)")).then_inc(neg_in, 16)

            def store_head(hh, b):
                sp.wait_ge(o_out, hh + 3)
                for j in range(QC):
                    sp.dma_start(scratch.num[bass.ds(hh * E, E), j * W:(j + 1) * W],
                                 osb[32 * j:32 * j + E, b, :]).then_inc(o_stored[b], 16)
                    sp.dma_start(scratch.den[bass.ds(hh, 1), j * W:(j + 1) * W],
                                 osb[32 * j + SUM:32 * j + SUM + 1, b, :]).then_inc(o_stored[b], 16)

            sp.wait_ge(stacks_in, 16 * (2 * PAIRS + 1))
            shift_rows(0)
            for hh in range(HEADS):
                if hh + 1 < HEADS:
                    shift_rows(hh + 1)
                store_head(hh, hh % 2)
            for b in range(2):
                sp.wait_ge(o_stored[b], HEADS // 2 * 2 * QC * 16)
            sp.dma_start(sums[:], scratch.den.rearrange("h (p b) -> p h b", p=P)).then_inc(sums_in, 16)
            sp.wait_ge(rec_done, 1)
            sp.dma_start(scratch.rec.rearrange("h (p b) -> p h b", p=P), rec[:]).then_inc(rec_stored, 16)
            sp.wait_ge(rec_stored, 16)

        @block.gpsimd
        def _(pool):
            nc.gpsimd.memset(vcur[:], 0.0).then_inc(v_ones, 1)
            pool.wait_ge(v_ones, 1)
            nc.gpsimd.memset(vcur[:, :, :, SUM:SUM + 1], 1.0).then_inc(v_ones, 1)
            vall = g.v[:].rearrange("p (t c) -> p t c", c=HEADS * E)

            def head(hh, b):
                pool.wait_ge(o_out, hh + 1)
                nc.gpsimd.tensor_copy(vcur[:, b, :, 0:E], vall[:, :, bass.ds(hh * E, E)]).then_inc(v_ready, 1)

            for c in range(HEADS // 2):
                for b in range(2):
                    head(c * 2 + b, b)

        @block.tensor
        def _(pe):
            def max_scores(hm, qt):
                tile, chunk = head_steps(hm)
                for kc in range(QC):
                    m = qt * QC + kc
                    if m == 0:
                        pe.wait_ge(max_done, hm * MAXES)
                    elif not (isinstance(hm, int) and hm * MAXES + m < MB):
                        pe.wait_ge(max_done, hm * MAXES + (m - MB + 1))
                    nc.tensor.matmul(ps_m[m % MB], qst[0:QROWS, tile[qt]], kst[0:QROWS, chunk[kc]],
                                     start=True, stop=True).then_inc(max_scored, 1)

            def scores(hh, kt):
                tile, chunk = head_steps(hh)
                for half in range(2):
                    u = 2 * kt + half
                    pe.wait_ge(exp_done, hh * UNITS + u + 1)
                    for j in range(2):
                        last = nc.tensor.matmul(ps_s[half][:, j, :], kst[0:QROWS + 2, tile[kt]],
                                                qst[0:QROWS + 2, chunk[2 * half + j]], start=True, stop=True)
                    last.then_inc(scored, 1)

            def weighted(hh, b, kt):
                pe.wait_ge(exp_done, hh * UNITS + 2 * kt + 4)
                if kt == 0:
                    pe.wait_ge(v_ready, hh + 1)
                    pe.wait_ge(o_out, hh + 2)
                for j in range(QC):
                    u = 2 * kt + j // 2
                    mm = nc.tensor.matmul(ps_o[32 * j:32 * j + VC, :], vcur[:, b, kt, :],
                                          probs[:, u % RING, (j % 2) * W:(j % 2 + 1) * W],
                                          start=(kt == 0), stop=(kt == KTILES - 1))
                    if j % 2:
                        mm.then_inc(pv_done, 1)

            def head(hh, b, next_max, before=None):
                pe.wait_ge(neg_in, (hh + 1) * 16)
                for kt in range(KTILES):
                    scores(hh, kt)
                    if kt == 0 and before is not None:
                        weighted(*before)
                    if kt > 0:
                        weighted(hh, b, kt - 1)
                    if next_max is not None:
                        max_scores(next_max, kt)
                return hh, b, KTILES - 1

            pe.wait_ge(v_ones, 2)
            pe.wait_ge(stacks_in, 16 * (2 * PAIRS + 1))
            for qt in range(KTILES):
                max_scores(0, qt)
            for c in range(HEADS // 2 - 1):
                before = None
                for b in range(2):
                    before = head(c * 2 + b, b, c * 2 + b + 1, before)
                weighted(*before)
            before = head(HEADS - 2, 0, HEADS - 1)
            before = head(HEADS - 1, 1, None, before)
            weighted(*before)

        @block.scalar
        def _(act):
            act.sem_inc(exp_done, 2)
            act.sem_inc(o_out, 2)
            act.sem_inc(pv_done, RING)

            def out(hh, b, c):
                act.wait_ge(pv_done, (hh + 1) * UNITS + RING)
                act.wait_ge(o_stored[b], c * (2 * QC * 16))
                nc.scalar.copy(osb[:, b, :], ps_o).then_inc(o_out, 1)

            def head(hh, before=None):
                for u in range(UNITS):
                    act.wait_ge(scored, hh * UNITS + u + 1)
                    act.wait_ge(pv_done, hh * UNITS + u + 1)
                    nc.scalar.activation(probs[:, u % RING, :].rearrange("p (j t) -> p j t", j=2), ps_s[u % 2],
                                         ACT.Exp).then_inc(exp_done, 1)
                    if u == 1 and before is not None:
                        out(*before)

            for c in range(HEADS // 2):
                head(c * 2)
                head(c * 2 + 1, (c * 2, 0, c))
                out(c * 2 + 1, 1, c)

        @block.vector
        def _(dve):
            nc.vector.memset(negpart[:], 0.0)

            def row_max(hm):
                for m in range(MAXES):
                    dve.wait_ge(max_scored, hm * MAXES + m + 1)
                    nc.vector.tensor_reduce(rowmax[:, m:m + 1], ps_m[m % MB], AX.X, ALU.max).then_inc(max_done, 1)
                dve.wait_ge(max_done, (hm + 1) * MAXES)
                nc.vector.tensor_reduce(negmax[:], rowmax[:].rearrange("p (t c) -> p t c", c=QC), AX.X, ALU.max,
                                        negate=True).then_inc(neg_step, 1)
                dve.wait_ge(neg_step, hm * NEG + 1)
                nc.vector.tensor_copy(negpart[:, 0, 0:KTILES], negmax[:]).then_inc(neg_step, 1)
                dve.wait_ge(neg_step, hm * NEG + 2)
                nc.vector.tensor_tensor(negmax[:], negmax[:], negpart[:, 0, 0:KTILES], ALU.subtract).then_inc(neg_step, 1)
                dve.wait_ge(neg_step, hm * NEG + 3)
                nc.vector.tensor_copy(negpart[:, 1, 0:KTILES], negmax[:]).then_inc(neg_step, 1)
                dve.wait_ge(neg_step, hm * NEG + 4)
                dve.wait_ge(neg_stored, hm * 64)
                nc.vector.transpose(negturn[:].rearrange("p s c -> p (s c)"),
                                    negpart[:].rearrange("p s c -> p (s c)")).then_inc(neg_step, 1)

            for hm in range(HEADS):
                row_max(hm)
            dve.wait_ge(sums_in, 16)
            nc.vector.reciprocal(rec[:], sums[:]).then_inc(rec_done, 1)


def experts(nc, d, g, scratch):
    GT = W // P
    STEPS = 6
    with ExitStack() as ctx:
        sb, sem = sb_alloc(ctx, nc), sem_alloc(ctx, nc, "moe")
        wo = sb("moe_wo", [HEADS * E + 1, D])
        wg = sb("moe_wg", [P, KT, EXPERTS])
        bg = sb("moe_bg", [1, EXPERTS])
        we = sb("moe_we", [P, EXPERTS, KT, D])
        be = sb("moe_be", [EXPERTS, D])
        pick = sb("moe_pick", [EXPERTS, EXPERTS, P])
        iota = sb("moe_iota", [P, EXPERTS])
        x = sb("moe_x", [P, 2, KT, W])
        num = sb("moe_num", [HEADS * E, 2, W])
        rec = sb("moe_rec", [HEADS * E, 2, W])
        att = sb("moe_att", [HEADS * E + 1, W])
        x1 = sb("moe_x1", [P, KT, W])
        x2 = sb("moe_x2", [P, KT, W])
        logit = sb("moe_logit", [P, GT, EXPERTS])
        top = sb("moe_top", [P, GT])
        chosen = sb("moe_chosen", [P, GT])
        onehot = sb("moe_onehot", [P, GT, EXPERTS])
        turned = sb("moe_turned", [EXPERTS, W])
        masked = sb("moe_masked", [P, 2, KT, W])
        psum = ctx.enter_context(nc.psum_tensor("moe_psum", [P, 8, W], F32))
        ln = LayerNorm(nc, ctx, "ln2", W, g, psum, (4, 5, 6), g.mod[:, 0, SCALE_B], g.mod[:, 0, SHIFT_B])
        acc = [psum[:, m, :] for m in range(KT)]
        ps_gate, ps_turn = psum[:, 7, 0:GT * EXPERTS], psum[0:EXPERTS, 5, :]
        ps_mask = [psum[:, 4, :], psum[:, 6, :]]
        weights_in, experts_in = sem("weights_in"), sem("experts_in")
        in_done = [sem("even_in"), sem("odd_in")]
        att_ready, wo_done, x1_done = sem("att_ready"), sem("wo_done"), sem("x1_done")
        gate_done, pick_step, chosen_done = sem("gate_done"), sem("pick_step"), sem("chosen_done")
        turn_done, turned_out, mask_done, masked_done = sem("turn_done"), sem("turned_out"), sem("mask_done"), sem("masked_done")
        expert_done, x2_done, x2_stored = sem("expert_done"), sem("x2_done"), sem("x2_stored")
        block = ctx.enter_context(nc.Block())
        xsrc = d["x"].rearrange("(k p) t -> p k t", p=P)
        xdst = scratch.x2.rearrange("(k p) t -> p k t", p=P)

        @block.sync
        def _(sp):
            sp.dma_start(wo[:], d["wo"]).then_inc(weights_in, 16)
            sp.dma_start(wg[:], d["wg"].rearrange("(k p) m -> p k m", p=P)).then_inc(weights_in, 16)
            sp.dma_start(bg[:], d["bg"]).then_inc(weights_in, 16)
            sp.dma_start(be[:], d["be"]).then_inc(weights_in, 16)
            sp.dma_start(pick[:], d["pick"].rearrange("e (f m) -> e f m", f=EXPERTS)).then_inc(weights_in, 16)
            sp.dma_start(iota[:], d["iota"]).then_inc(weights_in, 16)

            def load(i, b):
                sp.dma_start(num[:, b, :], scratch.num[:, bass.ds(i * W, W)]).then_inc(in_done[b], 16)
                sp.dma_start(rec[:, b, :], scratch.rec[:, bass.ds(i * W, W)].unsqueeze(1).to_broadcast([HEADS, E, W])
                             ).then_inc(in_done[b], 16)
                sp.dma_start(x[:, b], xsrc[:, :, bass.ds(i * W, W)]).then_inc(in_done[b], 16)

            def store(i):
                sp.wait_ge(x2_done, (i + 1) * KT)
                sp.dma_start(xdst[:, :, bass.ds(i * W, W)], x2[:]).then_inc(x2_stored, 16)

            load(0, 0)
            load(1, 1)
            for e in range(EXPERTS):
                sp.dma_start(we[:, e], d["we"][e].rearrange("(k p) m -> p k m", p=P)).then_inc(experts_in, 16)
            for i in range(2):
                store(i)
                load(i + 2, i)
            for i in range(2, NCH):
                store(i)
            sp.wait_ge(x2_stored, 16 * NCH)

        @block.tensor
        def _(pe):
            pe.wait_ge(weights_in, 96)
            for c in range(NCH // 2):
                for b in range(2):
                    i = c * 2 + b
                    pe.wait_ge(att_ready, i + 1)
                    pe.wait_ge(x2_done, i * KT)
                    for m in range(KT):
                        nc.tensor.matmul(acc[m], wo[:, m * P:(m + 1) * P], att[:], start=True, stop=True).then_inc(wo_done, 1)
                    pe.wait_ge(x1_done, (i + 1) * KT)
                    ln.tensor(pe, i, x1[:])
                    pe.wait_ge(ln.h_done, (i + 1) * KT)
                    for t in range(GT):
                        out = ps_gate[:, t * EXPERTS:(t + 1) * EXPERTS]
                        for k in range(KT):
                            nc.tensor.matmul(out, ln.h[:, k, t * P:(t + 1) * P], wg[:, k, :], start=(k == 0), stop=False)
                        last = nc.tensor.matmul(out, g.ones_row[0:1, 0:P], bg[0:1, :], start=False, stop=True)
                    last.then_inc(gate_done, 1)
                    pe.wait_ge(chosen_done, i + 1)
                    for t in range(GT):
                        last = nc.tensor.transpose(ps_turn[:, t * P:(t + 1) * P], onehot[:, t, :], g.ident[:])
                    last.then_inc(turn_done, 1)
                    pe.wait_ge(turned_out, i + 1)

                    def mask(e):
                        if e >= 2:
                            pe.wait_ge(masked_done, i * EXPERTS + e - 1)
                        nc.tensor.matmul(ps_mask[e % 2], pick[:, e, :], turned[:], start=True, stop=True).then_inc(mask_done, 1)

                    mask(0)
                    mask(1)
                    for m in range(KT):
                        nc.tensor.matmul(acc[m], be[:, m * P:(m + 1) * P], turned[:], start=True, stop=False)
                    if b == 0:
                        pe.wait_ge(experts_in, 16 * EXPERTS)
                    for e in range(EXPERTS):
                        pe.wait_ge(masked_done, i * EXPERTS + e + 1)
                        for m in range(KT):
                            for k in range(KT):
                                last = nc.tensor.matmul(acc[m], we[:, e, k, m * P:(m + 1) * P], masked[:, e % 2, k, :],
                                                        start=False, stop=(e == EXPERTS - 1 and k == KT - 1))
                        last.then_inc(expert_done, 1)
                        if e + 2 < EXPERTS:
                            mask(e + 2)

        @block.vector
        def _(dve):
            nc.vector.memset(att[HEADS * E:HEADS * E + 1, :], 1.0)
            dve.wait_ge(weights_in, 96)
            for c in range(NCH // 2):
                for b in range(2):
                    i = c * 2 + b
                    dve.wait_ge(in_done[b], c * 48 + 48)
                    dve.wait_ge(wo_done, i * KT)
                    nc.vector.scalar_tensor_tensor(att[0:HEADS * E, :], num[:, b, :], float((HEADS * E) ** -0.5), rec[:, b, :],
                                                   ALU.mult, ALU.mult).then_inc(att_ready, 1)
                    for m in range(KT):
                        dve.wait_ge(wo_done, i * KT + m + 1)
                        nc.vector.scalar_tensor_tensor(x1[:, m, :], acc[m], g.mod[:, 0, GATE_A, m:m + 1], x[:, b, m, :],
                                                       ALU.mult, ALU.add).then_inc(x1_done, 1)
                    dve.wait_ge(x1_done, (i + 1) * KT)
                    ln.vector(dve, i, x1[:])
                    dve.wait_ge(gate_done, i + 1)
                    nc.vector.tensor_copy(logit[:].rearrange("p t e -> p (t e)"), ps_gate).then_inc(pick_step, 1)
                    dve.wait_ge(pick_step, i * STEPS + 1)
                    nc.vector.tensor_reduce(top[:], logit[:], AX.X, ALU.max).then_inc(pick_step, 1)
                    dve.wait_ge(pick_step, i * STEPS + 2)
                    nc.vector.tensor_tensor(logit[:], logit[:], top[:].unsqueeze(2).to_broadcast([P, GT, EXPERTS]),
                                            ALU.is_equal).then_inc(pick_step, 1)
                    dve.wait_ge(pick_step, i * STEPS + 3)
                    nc.vector.scalar_tensor_tensor(logit[:], logit[:], -float(EXPERTS), iota[:].unsqueeze(1).to_broadcast([P, GT, EXPERTS]),
                                                   ALU.mult, ALU.add).then_inc(pick_step, 1)
                    dve.wait_ge(pick_step, i * STEPS + 4)
                    nc.vector.tensor_reduce(chosen[:], logit[:], AX.X, ALU.min).then_inc(pick_step, 1)
                    dve.wait_ge(pick_step, i * STEPS + 5)
                    nc.vector.tensor_scalar(chosen[:], chosen[:], float(EXPERTS), None, ALU.add).then_inc(pick_step, 1)
                    dve.wait_ge(pick_step, i * STEPS + 6)
                    nc.vector.tensor_tensor(onehot[:], iota[:].unsqueeze(1).to_broadcast([P, GT, EXPERTS]),
                                            chosen[:].unsqueeze(2).to_broadcast([P, GT, EXPERTS]), ALU.is_equal).then_inc(chosen_done, 1)
                    for e in range(EXPERTS):
                        dve.wait_ge(mask_done, i * EXPERTS + e + 1)
                        if e >= 2:
                            dve.wait_ge(expert_done, i * EXPERTS + e - 1)
                        nc.vector.tensor_tensor(masked[:, e % 2], ln.h[:], ps_mask[e % 2].unsqueeze(1).to_broadcast([P, KT, W]),
                                                ALU.mult).then_inc(masked_done, 1)
                    dve.wait_ge(expert_done, (i + 1) * EXPERTS)
                    dve.wait_ge(x2_stored, i * 16)
                    for m in range(KT):
                        nc.vector.scalar_tensor_tensor(x2[:, m, :], acc[m], g.mod[:, 0, GATE_B, m:m + 1], x1[:, m, :],
                                                       ALU.mult, ALU.add).then_inc(x2_done, 1)

        @block.scalar
        def _(act):
            for c in range(NCH // 2):
                for b in range(2):
                    i = c * 2 + b
                    ln.scalar(act, i, h_free=(masked_done, i * EXPERTS))
                    act.wait_ge(turn_done, i + 1)
                    nc.scalar.copy(turned[:], ps_turn).then_inc(turned_out, 1)


def state_space(nc, d, g, scratch):
    ROWS = RANK + 2 * NST
    ST = SW // P
    GROUPS = NST // NG
    J = P // 32
    UNITS = DT * GROUPS
    STEP_EXP = J * GROUPS
    HALF = DT // 2
    with ExitStack() as ctx:
        sb, sem = sb_alloc(ctx, nc), sem_alloc(ctx, nc, "ssm")
        win = sb("ssm_win", [P, KT, 2 * DI])
        wout = sb("ssm_wout", [P, DT, D])
        wx = sb("ssm_wx", [P, DT, ROWS])
        wdt = sb("ssm_wdt", [RANK, DI])
        convw = sb("ssm_convw", [P, DT, TAPS])
        convb = sb("ssm_convb", [P, DT])
        dtb = sb("ssm_dtb", [P, DT])
        amat = sb("ssm_a", [P, DT, GROUPS, J])
        dpar = sb("ssm_d", [P, DT])
        lnw = sb("ssm_lnw", [ROWS, 1])
        group = sb("ssm_group", [ROWS, 3])
        select = sb("ssm_select", [P, 32])
        conv = sb("ssm_conv", [P, DT, TAPS, P])
        x = sb("ssm_x", [P, KT, SW])
        xres = sb("ssm_xres", [P, KT, SW])
        logv = sb("ssm_logv", [P, ST])
        rstd = sb("ssm_rstd", [P, ST])
        h = sb("ssm_h", [P, 2, KT, SW])
        halo = sb("ssm_halo", [P, DT, TAPS - 1])
        upre = sb("ssm_upre", [P, 2, SW + TAPS - 1])
        u = sb("ssm_u", [P, 2, DT, SW])
        gate = sb("ssm_gate", [P, DT, SW])
        proj = sb("ssm_proj", [ROWS, SW])
        rms = sb("ssm_rms", [P, ST, 3])
        rwide = sb("ssm_rwide", [P, ST, ROWS])
        normed = sb("ssm_normed", [ROWS, SW])
        bc = sb("ssm_bc", [P, 2, 2, GROUPS, SW])
        soft = sb("ssm_soft", [P, DT - 2, SW])
        delta = sb("ssm_delta", [P, DT, SW])
        du = sb("ssm_du", [P, 2, SW])
        rep = sb("ssm_rep", [P, 2, 2, J, SW])
        decay = sb("ssm_decay", [P, SLOTS, J, SW])
        scan = sb("ssm_scan", [P, SLOTS, J, SW])
        state = sb("ssm_state", [P, DT, GROUPS, J])
        y = sb("ssm_y", [P, 2, DT, SW])
        psum = ctx.enter_context(nc.psum_tensor("ssm_psum", [P, 8, W], F32))
        ps_y = [psum[:, s, 0:SW] for s in (0, 1)]
        ps_p = [psum[:, s, 0:SW] for s in (2, 3)]
        ps_c = [psum[:, s, 0:SW] for s in (4, 5)]
        ps_z = psum[:, 6, :].rearrange("p (i t) -> p i t", i=2)
        ps_n, ps_v = psum[:, 7, 0:SW], psum[:, 7, SW:SW + 8]
        scale, shift, gates = g.mod[:, 1, SCALE_A], g.mod[:, 1, SHIFT_A], g.mod[:, 1, GATE_A]
        (weights_in, diag_done, zeroed, x_in, mean_done, centred_done, square_done, var_done, logv_done, rstd_done, bcast_done,
         norm_done, h_done, halo_in, halo_saved, proj_done, upre_out, conv_done, conv_out, u_done, wx_done, proj_out, stat_done, rlog_done,
         rms_done, rwide_done, rb_done, normed_done, bc_stored, wdt_done, abs_done, expneg_done, soft_done, relu_done,
         delta_done, du_done, drive_stored, decay_done, input_done, scan_done, carry_done, read_done, sum_done, yraw_done,
         gate_mm, gate_out, gate_done, ygate_done, out_mm, x3_done, x3_stored, xres_in) = (sem(n) for n in (
             "weights_in diag_done zeroed x_in mean_done centred_done square_done var_done logv_done rstd_done bcast_done "
             "norm_done h_done halo_in halo_saved proj_done upre_out conv_done conv_out u_done wx_done proj_out stat_done rlog_done "
             "rms_done rwide_done rb_done normed_done bc_stored wdt_done abs_done expneg_done soft_done relu_done "
             "delta_done du_done drive_stored decay_done input_done scan_done carry_done read_done sum_done yraw_done "
             "gate_mm gate_out gate_done ygate_done out_mm x3_done x3_stored xres_in").split())
        rep_in = [sem("rep_even_in"), sem("rep_odd_in")]
        bc_in = [sem("bc_even_in"), sem("bc_odd_in")]
        block = ctx.enter_context(nc.Block())
        xsrc = scratch.x2.rearrange("(k p) t -> p k t", p=P)
        xdst = scratch.x3.rearrange("(k p) t -> p k t", p=P)

        PROJ = {0: 0, 1: 1, 3: 2, 4: 3, 6: 4, 7: 5, 9: 6, 10: 7}
        CARRY = {q + 2: i for q, i in PROJ.items()}
        U_COPY = {q + 4: i for q, i in PROJ.items()}
        SAVE = {q + 5: i for q, i in PROJ.items()}
        CONV = {q + 2: i for q, i in PROJ.items()}
        CONV_OUT = {q + 6: i for q, i in PROJ.items()}
        GATE = {11: 0, 12: 1, 14: 2, 15: 3, 17: 4, 18: 5, 20: 6, 21: 7}
        GATE_OUT = {q + 4: i for q, i in GATE.items()}
        SILU, WX, PROJ_OUT, STAT, RMS, RMS_WIDE, RB, NORMED, GATE_SILU = 16, 15, 19, 17, 21, 21, 19, 22, 27
        Z = {21: 0, 24: 1, 26: 2, 28: 3}
        ABS = {25: 0, 28: 1, 30: 2, 31: 3}
        RELU = {25: 0, 27: 1, 29: 2, 31: 3}
        LOG, DELTA = {27: 0, 31: 1}, 28
        MEAN, CENTRED, SQUARE, VAR, RSTD, BCAST, NORM, H_OUT = 21, 23, 25, 23, 27, 25, 28, 30
        OUT = 24
        RESIDUAL = {OUT + 4 + 2 * m: m for m in range(KT)}
        PAIRS_Z = DT // 2
        BATCH = ((0, 2), (2, DT))

        def soft_of(batch):
            t0, t1 = BATCH[batch]
            at = (t0 - 2) % (DT - 2)
            return soft[:, at:at + t1 - t0]

        def ahead(c, t):
            return (c, t + 2) if t + 2 < DT else (c + 1, t + 2 - DT)

        @block.sync
        def _(sp):
            def load_x(c):
                sp.wait_ge(h_done, c)
                sp.dma_start(x[:], xsrc[:, :, c * SW:(c + 1) * SW]).then_inc(x_in, 16)

            def bc_rows(c):
                sp.wait_ge(normed_done, c + 1)
                sp.dma_start(scratch.bc, normed[RANK:ROWS, :]).then_inc(bc_stored, 16)
                sp.wait_ge(bc_stored, 16 * (c + 1))
                if c >= 2:
                    sp.wait_ge(read_done, (c - 1) * UNITS)
                src = scratch.bc.rearrange("(s k n) t -> n s k t", s=2, n=NG)
                for n in range(NG):
                    sp.dma_start(bc[32 * n:32 * n + 32, c % 2], src[n].unsqueeze(0).to_broadcast([32, 2, GROUPS, SW])).then_inc(bc_in[c % 2], 16)

            def repeat(c, t):
                s = c * DT + t
                sp.wait_ge(du_done, s + 1)
                sp.dma_start(scratch.drive[s % 2, 0], delta[:, t, :]).then_inc(drive_stored, 16)
                sp.dma_start(scratch.drive[s % 2, 1], du[:, s % 2]).then_inc(drive_stored, 16)
                sp.wait_ge(drive_stored, 32 * (s + 1))
                if s >= 2:
                    sp.wait_ge(decay_done, (s - 1) * STEP_EXP)
                    sp.wait_ge(input_done, (s - 1) * GROUPS)
                src = scratch.drive[s % 2].rearrange("q (j i) t -> i q j t", j=J)
                for n in range(NG):
                    sp.dma_start(rep[32 * n:32 * n + 32, s % 2], src).then_inc(rep_in[s % 2], 16)

            def load_residual(c):
                if c >= 1:
                    sp.wait_ge(x3_stored, 16 * c)
                sp.dma_start(xres[:], xsrc[:, :, c * SW:(c + 1) * SW]).then_inc(xres_in, 16)

            def store(c):
                sp.wait_ge(x3_done, (c + 1) * KT)
                sp.dma_start(xdst[:, :, c * SW:(c + 1) * SW], xres[:]).then_inc(x3_stored, 16)

            load_x(0)
            for dst, src in ((win, d["win"].rearrange("(k p) m -> p k m", p=P)), (convw, d["convw"]), (convb, d["convb"]),
                             (wx, d["wx"].rearrange("(k p) m -> p k m", p=P)), (group, d["group"]), (lnw, d["lnw"]),
                             (wdt, d["wdt"]), (dtb, d["dtb"]), (amat, d["a"]), (dpar, d["d"]), (select, d["select"]),
                             (wout, d["wout"].rearrange("(k p) m -> p k m", p=P))):
                sp.dma_start(dst[:], src).then_inc(weights_in, 16)
            load_x(1)
            bc_rows(0)
            repeat(0, 0)
            repeat(0, 1)
            for c in range(SCH):
                for t in range(DT):
                    if t == 1 and c >= 2:
                        store(c - 2)
                    if t == 1 and c + 2 < SCH:
                        load_x(c + 2)
                    if t == 2 and c >= 1:
                        load_residual(c - 1)
                    c2, t2 = ahead(c, t)
                    if t == DT - 2 and c + 1 < SCH:
                        bc_rows(c + 1)
                    if c2 < SCH:
                        repeat(c2, t2)
            store(SCH - 2)
            load_residual(SCH - 1)
            store(SCH - 1)
            sp.wait_ge(x3_stored, 16 * SCH)

        @block.gpsimd
        def _(pool):
            nc.gpsimd.memset(state[:], 0.0).then_inc(zeroed, 1)
            nc.gpsimd.memset(halo[:], 0.0).then_inc(zeroed, 1)
            pool.wait_ge(weights_in, 16 * 12)
            for t in range(DT):
                for k in range(TAPS):
                    nc.gpsimd.tensor_scalar(conv[:, t, k, :], g.ident[:], convw[:, t, k:k + 1], 0.0, ALU.mult, ALU.add).then_inc(diag_done, 1)

            def drive_input(c, t):
                s = c * DT + t
                pool.wait_ge(delta_done, 2 * c + (1 if t < BATCH[0][1] else 2))
                pool.wait_ge(u_done, c + 1)
                if s >= 2:
                    pool.wait_ge(drive_stored, (s - 1) * 32)
                nc.gpsimd.tensor_tensor(du[:, s % 2], delta[:, t, :], u[:, c % 2, t, :], ALU.mult).then_inc(du_done, 1)

            def gate_y(c, part):
                pool.wait_ge(yraw_done, c * DT + 2 * part + 2)
                pool.wait_ge(gate_done, c + 1)
                sl = slice(2 * part, 2 * part + 2)
                nc.gpsimd.tensor_tensor(y[:, c % 2, sl], y[:, c % 2, sl], gate[:, sl], ALU.mult).then_inc(ygate_done, 1)

            drive_input(0, 0)
            drive_input(0, 1)
            for c in range(SCH):
                for q in range(UNITS):
                    t, gr = q // GROUPS, q % GROUPS
                    Q = c * UNITS + q
                    if c >= 1 and 3 <= q < 7:
                        gate_y(c - 1, q - 3)
                    if q == 0:
                        pool.wait_ge(bc_in[c % 2], 64 * (c // 2 + 1))
                    pool.wait_ge(scan_done, (Q + 1) * J)
                    pool.wait_ge(carry_done, Q + 1)
                    nc.gpsimd.tensor_tensor(scan[:, Q % SLOTS], scan[:, Q % SLOTS],
                                            bc[:, c % 2, 1, gr, :].unsqueeze(1).to_broadcast([P, J, SW]), ALU.mult).then_inc(read_done, 1)
                    if gr == 3:
                        c2, t2 = ahead(c, t)
                        if c2 < SCH:
                            drive_input(c2, t2)
            for part in range(HALF):
                gate_y(SCH - 1, part)

        @block.tensor
        def _(pe):
            def mean(c):
                pe.wait_ge(x_in, 16 * (c + 1))
                if c >= 1:
                    pe.wait_ge(normed_done, c)
                for k in range(KT):
                    last = nc.tensor.matmul(ps_n, g.inv_d[:], x[:, k, :], start=(k == 0), stop=(k == KT - 1))
                last.then_inc(mean_done, 1)

            def var(c):
                pe.wait_ge(square_done, c + 1)
                for t in range(ST):
                    for k in range(KT):
                        last = nc.tensor.matmul(ps_v[:, t:t + 1], h[:, c % 2, k, t * P:(t + 1) * P], g.inv_d[:, 0:1],
                                                start=(k == 0), stop=(k == KT - 1))
                last.then_inc(var_done, 1)

            def bcast(c):
                pe.wait_ge(rstd_done, c + 1)
                for t in range(ST):
                    last = nc.tensor.matmul(ps_n[:, t * P:(t + 1) * P], rstd[:, t:t + 1].to_broadcast([P, P]), g.ident[:],
                                            start=True, stop=True)
                last.then_inc(bcast_done, 1)

            def project(c, i):
                if i == 0:
                    pe.wait_ge(h_done, c + 1)
                    if c >= 2:
                        pe.wait_ge(gate_out, (c - 1) * DT)
                if i >= 2:
                    pe.wait_ge(upre_out, c * DT + i - 1)
                for k in range(KT):
                    last = nc.tensor.matmul(ps_p[i % 2], win[:, k, i * P:(i + 1) * P], h[:, c % 2, k, :], start=(k == 0), stop=(k == KT - 1))
                last.then_inc(proj_done, 1)

            def convolve(c, i):
                pe.wait_ge(upre_out, c * DT + i + 1)
                if i >= 2:
                    pe.wait_ge(conv_out, c * DT + i - 1)
                elif c >= 3:
                    pe.wait_ge(x3_done, (c - 2) * KT)
                for k in range(TAPS):
                    last = nc.tensor.matmul(ps_c[i % 2], conv[:, i, k, :], upre[:, i % 2, k:k + SW], start=(k == 0), stop=(k == TAPS - 1))
                last.then_inc(conv_done, 1)

            def rows(c):
                pe.wait_ge(u_done, c + 1)
                for t in range(DT):
                    last = nc.tensor.matmul(ps_c[0][0:ROWS, :], wx[:, t, :], u[:, c % 2, t, :], start=(t == 0), stop=(t == DT - 1))
                last.then_inc(wx_done, 1)

            def mean_square(c):
                pe.wait_ge(proj_out, 2 * c + 2)
                for t in range(ST):
                    last = nc.tensor.matmul(ps_v[:, 3 * t:3 * t + 3], normed[:, t * P:(t + 1) * P], group[:], start=True, stop=True)
                last.then_inc(stat_done, 1)

            def rms_bcast(c):
                pe.wait_ge(rwide_done, 3 * (c + 1))
                for t in range(ST):
                    last = nc.tensor.matmul(ps_n[0:ROWS, t * P:(t + 1) * P], rwide[:, t, :], g.ident[:], start=True, stop=True)
                last.then_inc(rb_done, 1)

            def step_size(c, pair):
                n = c * PAIRS_Z + pair
                if pair == 0:
                    pe.wait_ge(normed_done, c + 1)
                if n >= 1:
                    pe.wait_ge(abs_done, 2 * n)
                    pe.wait_ge(relu_done, 2 * n)
                for i in range(2):
                    t = 2 * pair + i
                    last = nc.tensor.matmul(ps_z[:, i], wdt[:, t * P:(t + 1) * P], normed[0:RANK, :], start=True, stop=True)
                last.then_inc(wdt_done, 1)

            def gate_project(c, i):
                if i >= 2:
                    pe.wait_ge(gate_out, c * DT + i - 1)
                elif c + 1 < SCH:
                    pe.wait_ge(upre_out, (c + 2) * DT)
                for k in range(KT):
                    last = nc.tensor.matmul(ps_p[i % 2], win[:, k, DI + i * P:DI + (i + 1) * P], h[:, c % 2, k, :],
                                            start=(k == 0), stop=(k == KT - 1))
                last.then_inc(gate_mm, 1)

            def output(c, m, half):
                if half == 0:
                    if m == 0:
                        pe.wait_ge(ygate_done, (c + 1) * HALF)
                        if c + 2 < SCH:
                            pe.wait_ge(conv_out, (c + 3) * DT)
                            pe.wait_ge(proj_out, 2 * (c + 3))
                    if c * KT + m >= 2:
                        pe.wait_ge(x3_done, c * KT + m - 1)
                for t in range(half * HALF, (half + 1) * HALF):
                    last = nc.tensor.matmul(ps_c[m % 2], wout[:, t, m * P:(m + 1) * P], y[:, c % 2, t, :], start=(t == 0), stop=(t == DT - 1))
                if half == 1:
                    last.then_inc(out_mm, 1)

            def sum_states(c, q):
                t, gr = q // GROUPS, q % GROUPS
                Q, s = c * UNITS + q, c * DT + t
                if gr == 0 and s >= 2:
                    pe.wait_ge(yraw_done, s - 1)
                pe.wait_ge(read_done, Q + 1)
                for j in range(J):
                    last = nc.tensor.matmul(ps_y[t % 2][32 * j:32 * j + 32, :], select[:], scan[:, Q % SLOTS, j, :],
                                            start=(gr == 0), stop=(gr == GROUPS - 1))
                last.then_inc(sum_done, 1)

            def norm_chunk(c):
                mean(c)
                var(c)
                bcast(c)

            pe.wait_ge(weights_in, 16 * 12)
            norm_chunk(0)
            pe.wait_ge(diag_done, DT * TAPS)
            for i in range(DT):
                project(0, i)
                if i >= 1:
                    convolve(0, i - 1)
            convolve(0, DT - 1)
            rows(0)
            mean_square(0)
            rms_bcast(0)
            for pair in range(PAIRS_Z):
                step_size(0, pair)
            norm_chunk(1)
            for c in range(SCH):
                for q in range(UNITS):
                    if c + 1 < SCH:
                        if q in PROJ:
                            project(c + 1, PROJ[q])
                        if q in CONV:
                            convolve(c + 1, CONV[q])
                        if q == WX:
                            rows(c + 1)
                        if q == STAT:
                            mean_square(c + 1)
                        if q == RB:
                            rms_bcast(c + 1)
                    if q in GATE:
                        gate_project(c, GATE[q])
                    if c + 2 < SCH:
                        if q == MEAN:
                            mean(c + 2)
                        if q == VAR:
                            var(c + 2)
                        if q == BCAST:
                            bcast(c + 2)
                    if c >= 1 and q >= OUT:
                        output(c - 1, (q - OUT) // 2, (q - OUT) % 2)
                    if c + 1 < SCH and q in Z:
                        step_size(c + 1, Z[q])
                    sum_states(c, q)
            for m in range(KT):
                output(SCH - 1, m, 0)
                output(SCH - 1, m, 1)

        @block.scalar
        def _(act):
            def squares(c):
                act.wait_ge(centred_done, c + 1)
                if c >= 2:
                    act.wait_ge(gate_mm, (c - 1) * DT)
                nc.scalar.activation(h[:, c % 2], x[:], ACT.Square).then_inc(square_done, 1)

            def inverse_sd(c):
                act.wait_ge(var_done, c + 1)
                nc.scalar.activation(logv[:], ps_v[:, 0:ST], ACT.Ln, bias=g.ln_eps[:, 0:1]).then_inc(logv_done, 1)
                act.wait_ge(logv_done, c + 1)
                nc.scalar.activation(rstd[:], logv[:], ACT.Exp, scale=-0.5).then_inc(rstd_done, 1)

            def modulate(c):
                act.wait_ge(norm_done, c + 1)
                for k in range(KT):
                    last = nc.scalar.activation(h[:, c % 2, k, :], x[:, k, :], ACT.Identity, bias=shift[:, k:k + 1], scale=scale[:, k:k + 1])
                last.then_inc(h_done, 1)

            def copy_u(c, i):
                act.wait_ge(proj_done, c * DT + i + 1)
                n = c * DT + i
                act.wait_ge(halo_in, n + 1)
                if n >= 2:
                    act.wait_ge(halo_saved, n - 1)
                nc.scalar.copy(upre[:, i % 2, TAPS - 1:], ps_p[i % 2]).then_inc(upre_out, 1)

            def copy_conv(c, i):
                act.wait_ge(conv_done, c * DT + i + 1)
                if i == 0 and c >= 2:
                    act.wait_ge(yraw_done, (c - 1) * DT)
                nc.scalar.activation(u[:, c % 2, i, :], ps_c[i % 2], ACT.Identity, bias=convb[:, i:i + 1]).then_inc(conv_out, 1)

            def silu_u(c):
                act.wait_ge(conv_out, (c + 1) * DT)
                nc.scalar.activation(u[:, c % 2], u[:, c % 2], ACT.Silu).then_inc(u_done, 1)

            def copy_rows(c):
                act.wait_ge(wx_done, c + 1)
                if c >= 1:
                    act.wait_ge(wdt_done, c * PAIRS_Z)
                    act.wait_ge(bc_stored, c * 16)
                nc.scalar.activation(normed[:], ps_c[0][0:ROWS, :], ACT.Square).then_inc(proj_out, 1)
                act.wait_ge(normed_done, c)
                nc.scalar.copy(proj[:], ps_c[0][0:ROWS, :]).then_inc(proj_out, 1)

            def inverse_rms(c):
                act.wait_ge(stat_done, c + 1)
                flat = rms[:].rearrange("p t s -> p (t s)")
                act.wait_ge(rwide_done, 3 * c)
                nc.scalar.activation(flat, ps_v[:, 0:3 * ST], ACT.Ln, bias=g.rms_eps[:, 0:1]).then_inc(rlog_done, 1)
                act.wait_ge(rlog_done, c + 1)
                nc.scalar.activation(flat, flat, ACT.Exp, scale=-0.5).then_inc(rms_done, 1)

            def absolute(c, pair):
                n = c * PAIRS_Z + pair
                act.wait_ge(wdt_done, n + 1)
                if pair == 0 and c >= 1:
                    act.wait_ge(delta_done, 2 * c)
                if pair == PAIRS_Z - 1:
                    act.wait_ge(delta_done, 2 * c + 1)
                for i in range(2):
                    t = 2 * pair + i
                    nc.scalar.activation(soft[:, (t - 2) % (DT - 2), :], ps_z[:, i], ACT.Abs, bias=dtb[:, t:t + 1]).then_inc(abs_done, 1)

            def log1p_exp(c, batch):
                act.wait_ge(abs_done, c * DT + BATCH[batch][1])
                nc.scalar.activation(soft_of(batch), soft_of(batch), ACT.Exp, scale=-1.0).then_inc(expneg_done, 1)
                act.wait_ge(expneg_done, 2 * c + batch + 1)
                nc.scalar.activation(soft_of(batch), soft_of(batch), ACT.Ln, bias=1.0).then_inc(soft_done, 1)

            def copy_gate(c, i):
                act.wait_ge(gate_mm, c * DT + i + 1)
                if i == 0 and c >= 1:
                    act.wait_ge(ygate_done, c * HALF)
                nc.scalar.copy(gate[:, i, :], ps_p[i % 2]).then_inc(gate_out, 1)

            def silu_gate(c):
                act.wait_ge(gate_out, (c + 1) * DT)
                nc.scalar.activation(gate[:], gate[:], ACT.Silu).then_inc(gate_done, 1)

            def decays(c, q):
                t, gr = q // GROUPS, q % GROUPS
                Q, s = c * UNITS + q, c * DT + t
                if gr == 0:
                    act.wait_ge(rep_in[s % 2], 64 * (s // 2 + 1))
                if Q >= SLOTS:
                    act.wait_ge(scan_done, (Q - SLOTS + 1) * J)
                for j in range(J):
                    nc.scalar.activation(decay[:, Q % SLOTS, j, :], rep[:, s % 2, 0, j, :], ACT.Exp,
                                         scale=amat[:, t, gr, j:j + 1]).then_inc(decay_done, 1)

            def norm_chunk(c):
                squares(c)
                inverse_sd(c)
                modulate(c)

            act.wait_ge(weights_in, 16 * 12)
            norm_chunk(0)
            for i in range(DT):
                copy_u(0, i)
                if i >= 1:
                    copy_conv(0, i - 1)
            copy_conv(0, DT - 1)
            silu_u(0)
            copy_rows(0)
            inverse_rms(0)
            absolute(0, 0)
            log1p_exp(0, 0)
            for pair in range(1, PAIRS_Z):
                absolute(0, pair)
            log1p_exp(0, 1)
            norm_chunk(1)
            for c in range(SCH):
                for q in range(UNITS):
                    if c + 1 < SCH:
                        if q in U_COPY:
                            copy_u(c + 1, U_COPY[q])
                        if q in CONV_OUT:
                            copy_conv(c + 1, CONV_OUT[q])
                        if q == SILU:
                            silu_u(c + 1)
                        if q == PROJ_OUT:
                            copy_rows(c + 1)
                        if q == RMS:
                            inverse_rms(c + 1)
                        if q in ABS:
                            absolute(c + 1, ABS[q])
                        if q in LOG:
                            log1p_exp(c + 1, LOG[q])
                    if q in GATE_OUT:
                        copy_gate(c, GATE_OUT[q])
                    if q == GATE_SILU:
                        silu_gate(c)
                    if c + 2 < SCH:
                        if q == SQUARE:
                            squares(c + 2)
                        if q == RSTD:
                            inverse_sd(c + 2)
                        if q == H_OUT:
                            modulate(c + 2)
                    decays(c, q)

        @block.vector
        def _(dve):
            def centre(c):
                dve.wait_ge(mean_done, c + 1)
                nc.vector.tensor_tensor(x[:], x[:], ps_n.unsqueeze(1).to_broadcast([P, KT, SW]), ALU.subtract).then_inc(centred_done, 1)

            def normalise(c):
                dve.wait_ge(bcast_done, c + 1)
                nc.vector.tensor_tensor(x[:], x[:], ps_n.unsqueeze(1).to_broadcast([P, KT, SW]), ALU.mult).then_inc(norm_done, 1)

            def carry_halo(c, i):
                n = c * DT + i
                if n >= 2:
                    dve.wait_ge(conv_done, n - 1)
                if c >= 1:
                    dve.wait_ge(halo_saved, n - DT + 1)
                nc.vector.tensor_copy(upre[:, i % 2, 0:TAPS - 1], halo[:, i, :]).then_inc(halo_in, 1)

            def save_halo(c, i):
                n = c * DT + i
                dve.wait_ge(upre_out, n + 1)
                dve.wait_ge(halo_in, n + 1)
                nc.vector.tensor_copy(halo[:, i, :], upre[:, i % 2, SW:SW + TAPS - 1]).then_inc(halo_saved, 1)

            def rms_wide(c):
                dve.wait_ge(rms_done, c + 1)
                for s, (at, n) in enumerate(((0, RANK), (RANK, NST), (RANK + NST, NST))):
                    nc.vector.tensor_copy(rwide[:, :, at:at + n], rms[:, :, s:s + 1].to_broadcast([P, ST, n])).then_inc(rwide_done, 1)

            def rms_norm(c):
                dve.wait_ge(rb_done, c + 1)
                nc.vector.scalar_tensor_tensor(normed[:], proj[:], lnw[:, 0:1], ps_n[0:ROWS, :], ALU.mult, ALU.mult).then_inc(normed_done, 1)

            def positive(c, pair):
                n = c * PAIRS_Z + pair
                dve.wait_ge(abs_done, 2 * (n + 1))
                if c >= 1:
                    dve.wait_ge(drive_stored, ((c - 1) * DT + 2 * pair + 2) * 32)
                for i in range(2):
                    t = 2 * pair + i
                    nc.vector.tensor_scalar(delta[:, t, :], ps_z[:, i], dtb[:, t:t + 1], 0.0, ALU.add, ALU.max).then_inc(relu_done, 1)

            def step_sizes(c, batch):
                t0, t1 = BATCH[batch]
                dve.wait_ge(relu_done, c * DT + t1)
                dve.wait_ge(soft_done, 2 * c + batch + 1)
                nc.vector.tensor_tensor(delta[:, t0:t1], delta[:, t0:t1], soft_of(batch), ALU.add).then_inc(delta_done, 1)

            def unit(c, q):
                t, gr = q // GROUPS, q % GROUPS
                Q, s = c * UNITS + q, c * DT + t
                if gr == 0:
                    dve.wait_ge(rep_in[s % 2], 64 * (s // 2 + 1))
                if q == 0:
                    dve.wait_ge(bc_in[c % 2], 64 * (c // 2 + 1))
                if Q >= SLOTS:
                    dve.wait_ge(sum_done, Q - SLOTS + 1)
                nc.vector.tensor_tensor(scan[:, Q % SLOTS], rep[:, s % 2, 1],
                                        bc[:, c % 2, 0, gr, :].unsqueeze(1).to_broadcast([P, J, SW]), ALU.mult).then_inc(input_done, 1)
                dve.wait_ge(input_done, Q + 1)
                if c >= 1:
                    dve.wait_ge(carry_done, Q - UNITS + 1)
                for j in range(J):
                    dve.wait_ge(decay_done, Q * J + j + 1)
                    nc.vector.tensor_tensor_scan(scan[:, Q % SLOTS, j, :], decay[:, Q % SLOTS, j, :], scan[:, Q % SLOTS, j, :],
                                                 state[:, t, gr, j:j + 1], ALU.mult, ALU.add).then_inc(scan_done, 1)
                dve.wait_ge(scan_done, (Q + 1) * J)
                nc.vector.tensor_copy(state[:, t, gr, :], scan[:, Q % SLOTS, :, SW - 1]).then_inc(carry_done, 1)

            def raw_y(c, t):
                s = c * DT + t
                dve.wait_ge(sum_done, (s + 1) * GROUPS)
                if c >= 2:
                    dve.wait_ge(out_mm, (c - 1) * KT)
                nc.vector.scalar_tensor_tensor(y[:, c % 2, t, :], u[:, c % 2, t, :], dpar[:, t:t + 1], ps_y[t % 2], ALU.mult, ALU.add).then_inc(yraw_done, 1)

            def residual(c, m):
                if m == 0:
                    dve.wait_ge(xres_in, 16 * (c + 1))
                dve.wait_ge(out_mm, c * KT + m + 1)
                nc.vector.scalar_tensor_tensor(xres[:, m, :], ps_c[m % 2], gates[:, m:m + 1], xres[:, m, :], ALU.mult, ALU.add).then_inc(x3_done, 1)

            def Q_step(c, q):
                return c * DT + q // GROUPS

            dve.wait_ge(weights_in, 16 * 12)
            dve.wait_ge(zeroed, 2)
            dve.wait_ge(x_in, 16)
            centre(0)
            normalise(0)
            for i in range(DT):
                carry_halo(0, i)
                save_halo(0, i)
            rms_wide(0)
            rms_norm(0)
            positive(0, 0)
            step_sizes(0, 0)
            for pair in range(1, PAIRS_Z):
                positive(0, pair)
            step_sizes(0, 1)
            dve.wait_ge(x_in, 32)
            centre(1)
            normalise(1)
            for c in range(SCH):
                for q in range(UNITS):
                    if c + 1 < SCH:
                        if q in CARRY:
                            carry_halo(c + 1, CARRY[q])
                        if q in SAVE:
                            save_halo(c + 1, SAVE[q])
                        if q == RMS_WIDE:
                            rms_wide(c + 1)
                        if q == NORMED:
                            rms_norm(c + 1)
                        if q in RELU:
                            positive(c + 1, RELU[q])
                        if q == DELTA:
                            step_sizes(c + 1, 0)
                    if c >= 1 and q == 0:
                        step_sizes(c, 1)
                    if c + 2 < SCH:
                        if q == CENTRED:
                            centre(c + 2)
                        if q == NORM:
                            normalise(c + 2)
                    if c >= 1 and q in RESIDUAL:
                        residual(c - 1, RESIDUAL[q])
                    if c >= 2 and q + UNITS in RESIDUAL:
                        residual(c - 2, RESIDUAL[q + UNITS])
                    unit(c, q)
                    if q % GROUPS == 1 and Q_step(c, q) >= 1:
                        s = Q_step(c, q) - 1
                        raw_y(s // DT, s % DT)
            raw_y(SCH - 1, DT - 1)
            for q in range(UNITS, max(RESIDUAL) + 1):
                if q in RESIDUAL:
                    residual(SCH - 2, RESIDUAL[q])
            for m in range(KT):
                residual(SCH - 1, m)


def permuted_mlp(nc, d, g, scratch, out):
    MODS = (SCALE_B, SHIFT_B, GATE_B)
    with ExitStack() as ctx:
        sb, sem = sb_alloc(ctx, nc), sem_alloc(ctx, nc, "mlp")
        perm = sb("mlp_perm", [P, KT], U32)
        rows = sb("mlp_rows", [P, NCH, KT], U32)
        x = sb("mlp_x", [P, KT, T])
        modp = sb("mlp_mod", [P, KT, 4])
        modcols = sb("mlp_modcols", [P, KT, 4])
        up = sb("mlp_up", [P, KT, MM])
        down = sb("mlp_down", [P, MH, MD])
        hid = sb("mlp_hid", [P, 4, W])
        y = sb("mlp_y", [P, 2, KT, W])
        psum = ctx.enter_context(nc.psum_tensor("mlp_psum", [P, 8, W], F32))
        scale = sb("mlp_scale", [P, KT])
        shift = sb("mlp_shift", [P, KT])
        ln = LayerNorm(nc, ctx, "ln4", W, g, psum, (4, 5, 6), scale, shift)
        ps_up = [psum[:, b, :] for b in (4, 5, 6, 7)]
        ps_y = [psum[:, k, :] for k in range(KT)]
        weights_in, perm_in, x_in, mod_set, mod_stored, mod_in, cols_done = (
            sem("weights_in"), sem("perm_in"), sem("x_in"), sem("mod_set"), sem("mod_stored"), sem("mod_in"), sem("cols_done"))
        rows_done = sem("rows_done")
        up_done, hid_done, down_done, y_done = sem("up_done"), sem("hid_done"), sem("down_done"), sem("y_done")
        y_stored = [sem("y_even_stored"), sem("y_odd_stored")]
        block = ctx.enter_context(nc.Block())

        @block.sync
        def _(sp):
            sp.dma_start(up[:], d["up"].rearrange("p (k m) -> p k m", k=KT)).then_inc(weights_in, 16)
            sp.dma_start(down[:], d["down"].rearrange("p (h e) -> p h e", h=MH)).then_inc(weights_in, 16)
            sp.wait_ge(mod_set, 4)
            sp.dma_start(scratch.modb.rearrange("(k p) s -> p k s", p=P), modcols[:]).then_inc(mod_stored, 16)

        @block.gpsimd
        def _(pool):
            pool.dma_start(perm[:], d["perm"]).then_inc(perm_in, 16)
            pool.wait_ge(perm_in, 16)
            for k in range(KT):
                pool.indirect_dma_start(x[:, k, :], None, scratch.x3, bass.IndirectOffsetOnAxis(ap=perm[:, k:k + 1], axis=0)).then_inc(x_in, 16)
            pool.wait_ge(mod_stored, 16)
            for k in range(KT):
                pool.indirect_dma_start(modp[:, k, :], None, scratch.modb, bass.IndirectOffsetOnAxis(ap=perm[:, k:k + 1], axis=0)).then_inc(mod_in, 16)
            pool.wait_ge(rows_done, NCH)
            for i in range(NCH):
                for k in range(KT):
                    pool.wait_ge(y_done, i * KT + k + 1)
                    pool.indirect_dma_start(out, bass.IndirectOffsetOnAxis(ap=rows[:, i, k:k + 1], axis=0), y[:, i % 2, k, :], None
                                            ).then_inc(y_stored[i % 2], 16)
            for b in range(2):
                pool.wait_ge(y_stored[b], 16 * KT * NCH // 2)

        @block.tensor
        def _(pe):
            pe.wait_ge(weights_in, 32)
            pe.wait_ge(x_in, 16 * KT)
            for c in range(NCH // 2):
                for b in range(2):
                    i = c * 2 + b
                    pe.wait_ge(hid_done, i * MH)
                    ln.tensor(pe, i, x[:, :, bass.ds(i * W, W)])
                    pe.wait_ge(ln.h_done, (i + 1) * KT)

                    def down_head(h):
                        pe.wait_ge(hid_done, i * MH + h + 1)
                        if h < KT * 4 and h % 4 == 0:
                            pe.wait_ge(y_done, i * KT)
                        r = MD * (h % 4)
                        nc.tensor.matmul(ps_y[h // 4][r:r + MD, :], down[:, h, :], hid[:, h % 4, :], start=True, stop=True).then_inc(down_done, 1)

                    for h in range(MH):
                        r = MD * (h % 4)
                        if h >= 4:
                            pe.wait_ge(hid_done, i * MH + h - 3)
                        nc.tensor.matmul(ps_up[h % 4], up[r:r + MD, h // 4, :], ln.h[r:r + MD, h // 4, :], start=True, stop=True).then_inc(up_done, 1)
                        if h >= 2:
                            down_head(h - 2)
                    down_head(MH - 2)
                    down_head(MH - 1)

        @block.scalar
        def _(act):
            act.wait_ge(cols_done, 2)
            for c in range(NCH // 2):
                for b in range(2):
                    i = c * 2 + b
                    ln.scalar(act, i, h_free=(up_done, i * MH))
                    for h in range(MH):
                        act.wait_ge(up_done, i * MH + h + 1)
                        if h < 4:
                            act.wait_ge(down_done, i * MH)
                        else:
                            act.wait_ge(down_done, i * MH + h - 3)
                        nc.scalar.activation(hid[:, h % 4, :], ps_up[h % 4], ACT.Gelu).then_inc(hid_done, 1)

        @block.vector
        def _(dve):
            nc.vector.memset(modcols[:], 0.0).then_inc(mod_set, 1)
            dve.wait_ge(mod_set, 1)
            for s, which in enumerate(MODS):
                nc.vector.tensor_copy(modcols[:, :, s], g.mod[:, 1, which, :]).then_inc(mod_set, 1)
            dve.wait_ge(perm_in, 16)
            for i in range(NCH):
                nc.vector.tensor_scalar(rows[:, i, :], perm[:], float(i * D), None, ALU.add).then_inc(rows_done, 1)
            dve.wait_ge(mod_in, 16 * KT)
            nc.vector.tensor_copy(scale[:], modp[:, :, 0]).then_inc(cols_done, 1)
            nc.vector.tensor_copy(shift[:], modp[:, :, 1]).then_inc(cols_done, 1)
            dve.wait_ge(x_in, 16 * KT)
            for c in range(NCH // 2):
                for b in range(2):
                    i = c * 2 + b
                    ln.vector(dve, i, x[:, :, bass.ds(i * W, W)])
                    dve.wait_ge(y_stored[b], c * 16 * KT)
                    for k in range(KT):
                        dve.wait_ge(down_done, i * MH + (k + 1) * 4)
                        nc.vector.scalar_tensor_tensor(y[:, b, k, :], ps_y[k], modp[:, k, 2:3], x[:, k, bass.ds(i * W, W)],
                                                       ALU.mult, ALU.add).then_inc(y_done, 1)


STAGES = 6


def build(nc, d, out, stages=STAGES):
    scratch = Consts()
    scratch.parts = nc.dram_tensor("parts", [PARTS, 2 * HEADS * E, T], BF16).ap()
    neg = nc.dram_tensor("negmax_rows", [HEADS, 2, T // P, 4, 32], BF16).ap()

    class Rows:
        def __getitem__(self, hh):
            return neg[bass.ds(hh, 1)].rearrange("o s t q p -> (o s) t q p")
    scratch.neg = Rows()
    scratch.num = nc.dram_tensor("att_num", [HEADS * E, T], F32).ap()
    scratch.den = nc.dram_tensor("att_den", [HEADS, T], F32).ap()
    scratch.rec = nc.dram_tensor("att_den_inv", [HEADS, T], F32).ap()
    scratch.x2 = nc.dram_tensor("x_layer0", [D, T], F32).ap()
    scratch.bc = nc.dram_tensor("bc_rows", [2 * NST, SW], F32).ap()
    scratch.drive = nc.dram_tensor("drive_rows", [2, 2, P, SW], F32).ap()
    scratch.x3 = nc.dram_tensor("x_after_ssm", [D, T], F32).ap()
    scratch.modb = nc.dram_tensor("mod_rows", [D, 4], F32).ap()
    with ExitStack() as ctx:
        sb = sb_alloc(ctx, nc)
        g = Consts()
        g.ident = sb("ident", [P, P])
        g.inv_d = sb("inv_d", [P, P])
        g.ones_row = sb("ones_row", [1, W])
        g.ln_eps = sb("ln_eps", [P, 1])
        g.rms_eps = sb("rms_eps", [P, 1])
        g.mod = sb("mod", [P, 2, 6, KT])
        modulation(nc, d, g)
        with ExitStack() as layer0:
            g.v = layer0.enter_context(nc.sbuf_tensor("v_tokens", [P, T // P * HEADS * E], F32))
            if stages > 1:
                qkv(nc, d, g, scratch)
            if stages > 2:
                attention(nc, d, g, scratch)
        if stages > 3:
            experts(nc, d, g, scratch)
        if stages > 4:
            state_space(nc, d, g, scratch)
        if stages > 5:
            permuted_mlp(nc, d, g, scratch, out)


def layouts(a):
    import numpy as np

    def cols(v, n):
        return np.ascontiguousarray(v.reshape(n, P).T)

    def by_part(w):
        return np.ascontiguousarray(np.moveaxis(w.reshape((HEADS, E, 2) + w.shape[1:]), 2, 0)).reshape(w.shape)

    t = lambda w: np.ascontiguousarray(w.T)
    f = np.float32
    up = a["L1_ffn_up"].reshape(KT, 4, MD, MM)
    group = np.zeros((RANK + 2 * NST, 3), f)
    group[:RANK, 0], group[RANK:RANK + NST, 1], group[RANK + NST:, 2] = 1.0 / RANK, 1.0 / NST, 1.0 / NST
    pick = np.zeros((EXPERTS, EXPERTS, P), f)
    pick[np.arange(EXPERTS), np.arange(EXPERTS)] = 1.0
    return {
        "ones": np.ones((2, HEADS * T), mybir.dt.np(BF16)),
        "x": t(a["L0_attn_x"].reshape(T, D)),
        "wqk": t(by_part(a["L0_attn_Wqk_w"])), "bqk": by_part(a["L0_attn_Wqk_b"])[:, None].copy(),
        "wv": t(a["L0_attn_Wv_w"]), "bv": a["L0_attn_Wv_b"][None].copy(),
        "wo": np.concatenate([a["L0_attn_Wo_w"].T, a["L0_attn_Wo_b"][None]]),
        "wg": t(a["L0_ffn_gate_w"]), "bg": a["L0_ffn_gate_b"][None].copy(),
        "we": np.ascontiguousarray(a["L0_ffn_expert_w"].transpose(0, 2, 1)), "be": a["L0_ffn_expert_b"],
        "c0": cols(a["L0_c"], KT), "c1": cols(a["L1_c"], KT), "wmod0": a["L0_wmod"], "wmod1": a["L1_wmod"],
        "win": t(a["L1_attn_W_in"]), "wout": t(a["L1_attn_W_out"]), "wx": t(a["L1_attn_Wx"]), "wdt": t(a["L1_attn_Wdt"]),
        "convw": np.ascontiguousarray(a["L1_attn_conv_w"].reshape(DT, P, TAPS).transpose(1, 0, 2)),
        "convb": cols(a["L1_attn_conv_b"], DT), "dtb": cols(a["L1_attn_dt_bias"], DT), "d": cols(a["L1_attn_D_param"], DT),
        "a": np.ascontiguousarray(a["L1_attn_A"].reshape(DT, 4, 32, NST // NG, NG).transpose(4, 2, 0, 3, 1)).reshape(P, DT, NST // NG, 4),
        "select": np.tile(np.eye(32, dtype=f), (NG, 1)),
        "lnw": np.concatenate([a["L1_attn_dt_ln_w"], a["L1_attn_b_ln_w"], a["L1_attn_c_ln_w"]])[:, None].copy(),
        "up": np.ascontiguousarray(up.transpose(1, 2, 0, 3)).reshape(P, KT * MM),
        "down": np.ascontiguousarray(a["L1_ffn_down"].transpose(1, 0, 2)).reshape(P, MH * MD),
        "perm": np.ascontiguousarray(a["L1_ffn_perm"].reshape(KT, P).T).view(np.uint32),
        "ident": np.eye(P, dtype=f), "group": group, "pick": pick.reshape(EXPERTS, EXPERTS * P),
        "iota": np.tile(np.arange(EXPERTS, dtype=f), (P, 1)),
    }


def kernel(**inputs):
    import numpy as np
    import concourse.bacc as bacc
    from concourse.bass_utils import run_bass_kernel_spmd

    nc = bacc.Bacc("TRN2", target_bir_lowering=False, num_devices=1)
    arrays = layouts({k: np.asarray(v) for k, v in inputs.items()})
    d = {k: nc.dram_tensor("in_" + k, a.shape, mybir.dt.from_np(a.dtype), kind="ExternalInput").ap() for k, a in arrays.items()}
    out = nc.dram_tensor("out", [NCH * D, W], F32, kind="ExternalOutput").ap()
    build(nc, d, out)
    r = run_bass_kernel_spmd(nc, [{"in_" + k: a for k, a in arrays.items()}], core_ids=[0])
    y = r.results[0]["out"].reshape(NCH, D, W)
    return np.ascontiguousarray(y.transpose(0, 2, 1)).reshape(1, T, D)
```

```python
from contextlib import ExitStack

import concourse.bass as bass
from concourse import mybir

F32 = mybir.dt.float32
BF16 = mybir.dt.bfloat16
U32 = mybir.dt.uint32
I32 = mybir.dt.int32
ALU = mybir.AluOpType
ACT = mybir.ActivationFunctionType
AX = mybir.AxisListType

P = 128
T = 2048
D = 512
KT = D // P
W = 512
NCH = T // W
HEADS, E = 8, 8
PARTS = 3
PAIRS = PARTS * PARTS
QROWS = PAIRS * E
PAD = slice(64, 96)
EXPERTS = 8
LN_EPS = 1e-5
SHIFT_A, SCALE_A, GATE_A, SHIFT_B, SCALE_B, GATE_B = range(6)

DI = 1024
DT = DI // P
NST = 16
RANK = 32
TAPS = 4
SW = 256
SCH = T // SW
NG = 4
SLOTS = 3
RMS_EPS = 1e-6

MH, MD, MM = 16, 32, 128


def sb_alloc(ctx, nc):
    def sb(name, shape, dt=F32):
        return ctx.enter_context(nc.sbuf_tensor(name, shape, dt))
    return sb


def sem_alloc(ctx, nc, prefix, used=None):
    def sem(name):
        made = ctx.enter_context(nc.semaphore(prefix + "_" + name))
        if used is not None:
            used.append(made)
        return made
    return sem


class LayerNorm:

    def __init__(self, nc, ctx, prefix, consts, psum, stat_bank, x, centred, scale, shift):
        sb, sem = sb_alloc(ctx, nc), sem_alloc(ctx, nc, prefix, consts.used)
        self.nc, self.c, self.x, self.centred = nc, consts, x, centred
        self.scale, self.shift = scale, shift
        self.square = sb(prefix + "_square", [P, NCH, KT, W])
        self.sd = sb(prefix + "_sd", [P, W])
        self.rstd = sb(prefix + "_rstd", [P, NCH, W // P])
        self.h = sb(prefix + "_h", [P, 2, KT, W])
        self.ps_mean = [psum[:, i, :] for i in range(NCH)]
        self.ps_var, self.ps_sd = psum[:, stat_bank, :], psum[:, stat_bank + 1, :]
        (self.mean_done, self.centred_done, self.square_done, self.sd_set, self.var_done, self.sd_done, self.turn_done, self.rstd_done, self.spread_done,
         self.norm_done, self.h_done) = (sem(n) for n in (
             "mean_done centred_done square_done sd_set var_done sd_done turn_done rstd_done spread_done norm_done h_done").split())

    def mean(self, pe, i):
        nc = self.nc
        for k in range(KT):
            last = nc.tensor.matmul(self.ps_mean[i], self.c.inv_d[:], self.x[:, k, i * W:(i + 1) * W], start=(k == 0), stop=(k == KT - 1))
        last.then_inc(self.mean_done, 1)

    def mean_part(self, pe, k):
        for i in range(NCH):
            last = self.nc.tensor.matmul(self.ps_mean[i], self.c.inv_d[:], self.x[:, k, i * W:(i + 1) * W], start=(k == 0), stop=(k == KT - 1))
            if k == KT - 1:
                last.then_inc(self.mean_done, 1)

    def centre(self, dve, i):
        nc, sl = self.nc, slice(i * W, (i + 1) * W)
        dve.wait_ge(self.mean_done, i + 1)
        nc.vector.tensor_tensor(self.centred[:, :, sl], self.x[:, :, sl], self.ps_mean[i].unsqueeze(1).to_broadcast([P, KT, W]),
                                ALU.subtract).then_inc(self.centred_done, 1)

    def squares(self, act, i):
        nc = self.nc
        act.wait_ge(self.centred_done, i + 1)
        nc.scalar.activation(self.square[:, i], self.centred[:, :, i * W:(i + 1) * W], ACT.Square).then_inc(self.square_done, 1)

    def variance(self, pe):
        pe.wait_ge(self.square_done, NCH)
        for k in range(KT):
            for i in range(NCH):
                last = self.nc.tensor.matmul(self.ps_var[32 * i:32 * i + 1, :], self.c.inv_d[:, 0:1], self.square[:, i, k, :],
                                             start=(k == 0), stop=(k == KT - 1))
        last.then_inc(self.var_done, 1)

    def clear(self, dve):
        self.nc.vector.memset(self.sd[:], 0.0).then_inc(self.sd_set, 1)

    def deviation(self, act):
        act.wait_ge(self.var_done, 1)
        act.wait_ge(self.sd_set, 1)
        for i in range(NCH):
            r = slice(32 * i, 32 * i + 1)
            self.nc.scalar.activation(self.sd[r, :], self.ps_var[r, :], ACT.Sqrt, bias=self.c.ln_eps[r, 0:1]).then_inc(self.sd_done, 1)

    def turn(self, pe):
        pe.wait_ge(self.sd_done, NCH)
        for t in range(W // P):
            last = self.nc.tensor.transpose(self.ps_sd[:, t * P:(t + 1) * P], self.sd[:, t * P:(t + 1) * P], self.c.ident[:])
        last.then_inc(self.turn_done, 1)

    def inverse(self, dve):
        dve.wait_ge(self.turn_done, 1)
        turned = self.ps_sd.rearrange("p (t i c) -> p i t c", i=NCH, c=32)
        self.nc.vector.reciprocal(self.rstd[:], turned[:, :, :, 0]).then_inc(self.rstd_done, 1)

    def spread(self, pe, i):
        nc = self.nc
        pe.wait_ge(self.rstd_done, 1)
        for t in range(W // P):
            last = nc.tensor.matmul(self.ps_mean[i][:, t * P:(t + 1) * P], self.rstd[:, i, t:t + 1].to_broadcast([P, P]),
                                    self.c.ident[:], start=True, stop=True)
        last.then_inc(self.spread_done, 1)

    def normalise(self, dve, i):
        nc, sl = self.nc, slice(i * W, (i + 1) * W)
        dve.wait_ge(self.spread_done, i + 1)
        nc.vector.tensor_tensor(self.centred[:, :, sl], self.centred[:, :, sl], self.ps_mean[i].unsqueeze(1).to_broadcast([P, KT, W]),
                                ALU.mult).then_inc(self.norm_done, 1)

    def modulate(self, act, i):
        nc = self.nc
        act.wait_ge(self.norm_done, i + 1)
        for k in range(KT):
            last = nc.scalar.activation(self.h[:, i % 2, k, :], self.centred[:, k, i * W:(i + 1) * W], ACT.Identity,
                                        bias=self.shift[:, k:k + 1], scale=self.scale[:, k:k + 1])
        last.then_inc(self.h_done, 1)


class Consts:
    pass


class Modulation:

    def __init__(self, nc, ctx, layer, d, g, wmod, psum, bank):
        sb, sem = sb_alloc(ctx, nc), sem_alloc(ctx, nc, f"mod{layer}", g.used)
        self.nc, self.layer, self.d, self.g = nc, layer, d, g
        name = f"mod{layer}_"
        self.wmod = wmod
        self.ccol = sb(name + "c", [P, KT])
        self.cact = sb(name + "silu_c", [P, KT])
        self.row = sb(name + "row", [P, 2, D])
        self.sign = sb(name + "sign", [P, 2, KT])
        self.mag = sb(name + "mag", [P, 2, KT])
        self.ps_row = [psum[:, bank + half, :] for half in range(2)]
        self.ps_col = psum[:, bank + 2:bank + 4, :]
        self.c_in, self.w_in, self.row_set, self.silu_done, self.prod_done, self.row_out, self.col_done, self.step = (sem(n) for n in (
            "c_in", "w_in", "row_set", "silu_done", "prod_done", "row_out", "col_done", "step"))
        self.STEPS = 8

    @staticmethod
    def place(s):
        return slice(32 * (s % 4), 32 * (s % 4) + 1), s // 4

    def load_c(self, sp):
        sp.dma_start(self.ccol[:], self.d[f"c{self.layer}"]).then_inc(self.c_in, 16)

    def load(self, sp):
        for k in range(KT):
            sp.dma_start(self.wmod[:, k, :], self.d[f"wmod{self.layer}"][k * P:(k + 1) * P, :]).then_inc(self.w_in, 16)

    def silu(self, act):
        act.wait_ge(self.c_in, 16)
        self.nc.scalar.activation(self.cact[:], self.ccol[:], ACT.Silu).then_inc(self.silu_done, 1)

    def products(self, pe):
        pe.wait_ge(self.silu_done, 1)
        pe.wait_ge(self.w_in, 16 * KT)
        for k in range(KT):
            for s in range(6):
                p, half = self.place(s)
                last = self.nc.tensor.matmul(self.ps_row[half][p, :], self.cact[:, k:k + 1], self.wmod[:, k, s * D:(s + 1) * D],
                                             start=(k == 0), stop=(k == KT - 1))
        last.then_inc(self.prod_done, 1)

    def rows(self, act):
        act.wait_ge(self.prod_done, 1)
        act.wait_ge(self.row_set, 1)
        for s in range(6):
            p, half = self.place(s)
            self.nc.scalar.copy(self.row[p, half], self.ps_row[half][p, :]).then_inc(self.row_out, 1)

    def columns(self, pe):
        pe.wait_ge(self.row_out, 6)
        for half in range(2):
            for k in range(KT):
                last = self.nc.tensor.transpose(self.ps_col[:, half, k * P:(k + 1) * P], self.row[:, half, k * P:(k + 1) * P], self.g.ident[:])
        last.then_inc(self.col_done, 1)

    def clear(self, dve):
        self.nc.vector.memset(self.row[:], 0.0).then_inc(self.row_set, 1)

    def finish(self, dve):
        nc, step = self.nc, self.step
        mod = self.g.mod[:, self.layer]
        dve.wait_ge(self.col_done, 1)
        for half, n in enumerate((4, 2)):
            turned = self.ps_col[:, half].rearrange("p (k s c) -> p s k c", s=4, c=32)
            nc.vector.tensor_copy(mod[:, 4 * half:4 * half + n, :], turned[:, 0:n, :, 0]).then_inc(step, 1)
        dve.wait_ge(step, 2)
        scales, gates = mod[:, SCALE_A::3, :], mod[:, GATE_A::3, :]
        nc.vector.tensor_scalar(scales, scales, 1.0, None, ALU.add).then_inc(step, 1)
        nc.vector.tensor_scalar(self.sign[:], gates, 0.0, 2.0, ALU.is_ge, ALU.mult).then_inc(step, 1)
        nc.vector.scalar_tensor_tensor(self.mag[:], gates, -1.0, gates, ALU.mult, ALU.max).then_inc(step, 1)
        dve.wait_ge(step, 5)
        nc.vector.tensor_scalar(self.mag[:], self.mag[:], 0.25, None, ALU.max).then_inc(step, 1)
        dve.wait_ge(step, 6)
        nc.vector.tensor_scalar(self.sign[:], self.sign[:], -1.0, None, ALU.add).then_inc(step, 1)
        dve.wait_ge(step, 7)
        nc.vector.tensor_tensor(gates, self.sign[:], self.mag[:], ALU.mult).then_inc(step, 1)


def qkv(nc, d, g, scratch):
    with ExitStack() as ctx:
        sb, sem = sb_alloc(ctx, nc), sem_alloc(ctx, nc, "qkv", g.used)
        x = sb("qkv_x", [P, KT, T])
        wqk = sb("qkv_wqk", [P, KT, 2 * HEADS * E])
        qkb = sb("qkv_bqk", [P, 1])
        wv = sb("qkv_wv", [P, KT, HEADS * E])
        bv = sb("qkv_bv", [1, HEADS * E])
        qk = sb("qkv_qk", [P, 2, W])
        rest = sb("qkv_rest", [P, W])
        parts = sb("qkv_parts", [P, 2, PARTS, W], BF16)
        psum = ctx.enter_context(nc.psum_tensor("qkv_psum", [P, 8, W], F32))
        ps_qk, ps_v = [psum[:, b, :] for b in (4, 5)], [psum[:, b, 0:W // P * HEADS * E] for b in (6, 7)]
        wmod = sb("qkv_wmod", [P, KT, 6 * D])
        mods = [Modulation(nc, ctx, 0, d, g, wmod, psum, 4), Modulation(nc, ctx, 1, d, g, wmod, psum, 0)]
        consts_in, consts_set = sem("consts_in"), sem("consts_set")
        ln = LayerNorm(nc, ctx, "ln1", g, psum, 6, x, x, g.mod[:, 0, SCALE_A], g.mod[:, 0, SHIFT_A])
        weights_in = sem("weights_in")
        x_in = [sem(f"x{i}_in") for i in range(NCH)]
        qk_done, v_done = sem("qk_done"), sem("v_done")
        qk_out, v_out = sem("qk_out"), sem("v_out")
        split = sem("split")
        parts_stored = [sem("parts_even_stored"), sem("parts_odd_stored")]
        zeros_set, first_in = sem("zeros_set"), sem("first_in")
        block = ctx.enter_context(nc.Block())
        xsrc = d["x"].rearrange("(k p) t -> p k t", p=P)
        SPLITS = 5

        @block.sync
        def _(sp):
            for mod in mods:
                mod.load_c(sp)
            for i in range(NCH):
                if i >= 1:
                    sp.wait_ge(x_in[i - 1], 16)
                sp.dma_start(x[:, :, i * W:(i + 1) * W], xsrc[:, :, i * W:(i + 1) * W]).then_inc(x_in[i], 16)
            sp.dma_start(g.ident[:], d["ident"]).then_inc(consts_in, 16)
            mods[0].load(sp)
            sp.dma_start(wqk[:], d["wqk"].rearrange("(k p) m -> p k m", p=P)).then_inc(weights_in, 16)
            sp.dma_start(wv[:], d["wv"].rearrange("(k p) m -> p k m", p=P)).then_inc(weights_in, 16)
            sp.dma_start(qkb[:], d["bqk"]).then_inc(weights_in, 16)
            sp.dma_start(bv[:], d["bv"]).then_inc(weights_in, 16)
            sp.wait_ge(mods[0].prod_done, 1)
            mods[1].load(sp)
            for i in range(NCH):
                sp.wait_ge(split, (i + 1) * SPLITS)
                sp.dma_start(scratch.parts[:, :, i * W:(i + 1) * W].rearrange("s p t -> p s t"),
                             parts[:, i % 2]).then_inc(parts_stored[i % 2], 16)
            for b in range(2):
                sp.wait_ge(parts_stored[b], 16 * NCH // 2)
            sp.wait_ge(zeros_set, 2)
            for a in range(PARTS):
                rows = slice(a * PARTS * E, (a + 1) * PARTS * E)
                sp.dma_start(g.q0[rows, :], scratch.parts[a, 0:E, :].unsqueeze(0).to_broadcast([PARTS, E, T])).then_inc(first_in, 16)
                sp.dma_start(g.k0[rows, :], scratch.parts[:, HEADS * E:HEADS * E + E, :]).then_inc(first_in, 16)
            sp.wait_ge(first_in, 2 * PARTS * 16)

        @block.tensor
        def _(pe):
            pe.wait_ge(consts_set, 4)
            for i in range(NCH):
                pe.wait_ge(x_in[i], 16)
                ln.mean(pe, i)
            ln.variance(pe)
            pe.wait_ge(consts_in, 16)
            ln.turn(pe)
            for i in range(NCH):
                ln.spread(pe, i)
            mods[0].products(pe)
            mods[0].columns(pe)
            pe.wait_ge(weights_in, 64)
            pe.wait_ge(mods[0].step, 2)
            for i in range(NCH):
                h = ln.h[:, i % 2]
                pe.wait_ge(ln.h_done, i + 1)
                if i >= 2:
                    pe.wait_ge(qk_out, i - 1)
                for k in range(KT):
                    last = nc.tensor.matmul(ps_qk[i % 2], wqk[:, k, :], h[:, k, :], start=(k == 0), stop=(k == KT - 1))
                last.then_inc(qk_done, 1)
                if i >= 2:
                    pe.wait_ge(v_out, i - 1)
                for t in range(W // P):
                    out = ps_v[i % 2][:, t * HEADS * E:(t + 1) * HEADS * E]
                    for k in range(KT):
                        nc.tensor.matmul(out, h[:, k, t * P:(t + 1) * P], wv[:, k, :], start=(k == 0), stop=False)
                    last = nc.tensor.matmul(out, g.ones_row[0:1, 0:P], bv[0:1, :], start=False, stop=True)
                last.then_inc(v_done, 1)
            pe.wait_ge(ln.norm_done, NCH)
            mods[1].products(pe)
            mods[1].columns(pe)

        @block.vector
        def _(dve):
            for const, value in ((g.inv_d, 1.0 / D), (g.ones_row, 1.0), (g.ln_eps, LN_EPS), (g.rms_eps, RMS_EPS)):
                nc.vector.memset(const[:], value).then_inc(consts_set, 1)
            for mod in mods:
                mod.clear(dve)
            ln.clear(dve)
            for st in (g.q0, g.k0):
                nc.vector.memset(st[PAD, :], 0.0).then_inc(zeros_set, 1)

            def split_parts(i):
                b = i % 2
                dve.wait_ge(qk_out, i + 1)
                if i >= 2:
                    dve.wait_ge(parts_stored[b], i // 2 * 16)
                if i >= 1:
                    dve.wait_ge(split, i * SPLITS)
                nc.vector.tensor_copy(parts[:, b, 0, :], qk[:, b]).then_inc(split, 1)
                dve.wait_ge(split, i * SPLITS + 1)
                nc.vector.tensor_tensor(rest[:], qk[:, b], parts[:, b, 0, :], ALU.subtract).then_inc(split, 1)
                dve.wait_ge(split, i * SPLITS + 2)
                nc.vector.tensor_copy(parts[:, b, 1, :], rest[:]).then_inc(split, 1)
                dve.wait_ge(split, i * SPLITS + 3)
                nc.vector.tensor_tensor(rest[:], rest[:], parts[:, b, 1, :], ALU.subtract).then_inc(split, 1)
                dve.wait_ge(split, i * SPLITS + 4)
                nc.vector.tensor_copy(parts[:, b, 2, :], rest[:]).then_inc(split, 1)

            for i in range(NCH):
                dve.wait_ge(x_in[i], 16)
                ln.centre(dve, i)
            ln.inverse(dve)
            for i in range(NCH):
                ln.normalise(dve, i)
                if i == 1:
                    mods[0].finish(dve)
                if i >= 2:
                    split_parts(i - 2)
            split_parts(NCH - 2)
            split_parts(NCH - 1)
            mods[1].finish(dve)

        @block.scalar
        def _(act):
            def out(i):
                act.wait_ge(qk_done, i + 1)
                if i >= 2:
                    act.wait_ge(split, (i - 1) * SPLITS)
                nc.scalar.activation(qk[:, i % 2], ps_qk[i % 2], ACT.Identity, bias=qkb[:, 0:1]).then_inc(qk_out, 1)
                act.wait_ge(v_done, i + 1)
                n = W // P * HEADS * E
                nc.scalar.copy(g.v[:, i * n:(i + 1) * n], ps_v[i % 2]).then_inc(v_out, 1)

            for mod in mods:
                mod.silu(act)
            for i in range(NCH):
                ln.squares(act, i)
            act.wait_ge(consts_set, 4)
            ln.deviation(act)
            mods[0].rows(act)
            act.wait_ge(mods[0].step, mods[0].STEPS)
            act.wait_ge(weights_in, 64)
            for i in range(NCH):
                if i >= 2:
                    act.wait_ge(v_done, i - 1)
                ln.modulate(act, i)
                if i >= 1:
                    out(i - 1)
            out(NCH - 1)
            mods[1].rows(act)


def attention(nc, d, g, scratch):
    KTILES = T // P
    QC = T // W
    UNITS = KTILES * 2
    RING = 4
    MAXES = KTILES * QC
    MB = 3
    VC = 32
    SUM = E
    FIRST = KTILES
    FIRST_MAXES = 2 * FIRST
    AHEAD = 18
    STACK_LOADS = (2 * PAIRS + 1) * 16
    LOWEST = -3.4028234e38
    with ExitStack() as ctx:
        sb, sem = sb_alloc(ctx, nc), sem_alloc(ctx, nc, "att")
        qst = sb("att_q", [P, (HEADS - 1) * T], BF16)
        kst = sb("att_k", [P, (HEADS - 1) * T], BF16)
        vcur = sb("att_v", [P, 2, KTILES, VC])
        probs = sb("att_probs", [P, RING, 2 * W])
        osb = sb("att_out", [P, 2, W])
        rowmax = sb("att_rowmax", [P, MAXES])
        running = sb("att_running", [P, FIRST_MAXES, W])
        negmax = sb("att_negmax", [P, KTILES])
        negpart = sb("att_negpart", [P, 2, 32], BF16)
        negturn = sb("att_negturn", [P, 2, 32], BF16)
        sums = sb("att_sums", [P, HEADS, T // P])
        rec = sb("att_rec", [P, HEADS, T // P])
        psum = ctx.enter_context(nc.psum_tensor("att_psum", [P, 8, W], F32))
        ps_s = [psum[:, 2 * s:2 * s + 2, :] for s in range(2)]
        ps_o, ps_m = psum[:, 4, :], [psum[:, 5 + s, :] for s in range(MB)]
        stacks_in, v_ones = sem("stacks_in"), sem("v_ones")
        scored, exp_done, pv_done = sem("scored"), sem("exp_done"), sem("pv_done")
        v_ready, o_out = sem("v_ready"), sem("o_out")
        max_scored, max_done, neg_step = sem("max_scored"), sem("max_done"), sem("neg_step")
        neg_stored, neg_in = sem("neg_stored"), sem("neg_in")
        o_stored = [sem("o_even_stored"), sem("o_odd_stored")]
        sums_moved, rec_done = sem("sums_moved"), sem("rec_done")
        NEG = 5
        block = ctx.enter_context(nc.Block())

        def head_steps(hh):
            q, k, at = (qst, kst, (hh - 1) * T) if hh else (g.q0, g.k0, 0)
            return q, k, [slice(at + t * P, at + (t + 1) * P) for t in range(KTILES)], [slice(at + j * W, at + (j + 1) * W) for j in range(QC)]

        @block.sync
        def _(sp):

            for semaphore in g.used:
                sp.sem_clear(semaphore)
            sp.dma_start(kst[QROWS:QROWS + 2, :], d["ones"][:, T:]).then_inc(stacks_in, 16)
            for a in range(PARTS):
                for b in range(PARTS):
                    r = (a * PARTS + b) * E
                    for st, part, row in ((qst, a, E), (kst, b, (HEADS + 1) * E)):
                        sp.dma_start(st[r:r + E, :].rearrange("e (h t) -> e h t", h=HEADS - 1),
                                     scratch.parts[part, row:row + (HEADS - 1) * E, :].rearrange("(h e) t -> e h t", e=E)
                                     ).then_inc(stacks_in, 16)

            def shift_rows(hh):
                sp.wait_ge(neg_step, (hh + 1) * NEG)
                for q in range(4):
                    sp.dma_start(scratch.neg[hh][:, :, q, :].rearrange("s t p -> t s p"),
                                 negturn[32 * q:32 * q + KTILES, :, :]).then_inc(neg_stored, 16)
                sp.wait_ge(neg_stored, (hh + 1) * 64)
                q, _, tile, _ = head_steps(hh)
                sp.dma_start(q[QROWS:QROWS + 2, tile[0].start:tile[0].start + T],
                             scratch.neg[hh].rearrange("s t q p -> s (t q p)")).then_inc(neg_in, 16)

            def store_head(hh, b):
                sp.wait_ge(o_out, hh + 3)
                for j in range(QC):
                    sp.dma_start(scratch.num[bass.ds(hh * E, E), j * W:(j + 1) * W],
                                 osb[32 * j:32 * j + E, b, :]).then_inc(o_stored[b], 16)
                    sp.dma_start(scratch.den[bass.ds(hh, 1), j * W:(j + 1) * W],
                                 osb[32 * j + SUM:32 * j + SUM + 1, b, :]).then_inc(o_stored[b], 16)

            sp.wait_ge(max_done, FIRST_MAXES)
            sp.dma_start(g.k0[QROWS:QROWS + 2, :], d["ones"][:, 0:T]).then_inc(neg_in, 16)
            sp.wait_ge(neg_in, 16)
            shift_rows(0)
            for hh in range(HEADS):
                if hh + 1 < HEADS:
                    shift_rows(hh + 1)
                store_head(hh, hh % 2)
            for b in range(2):
                sp.wait_ge(o_stored[b], HEADS // 2 * 2 * QC * 16)
            sp.dma_start(sums[:], scratch.den.rearrange("h (p b) -> p h b", p=P)).then_inc(sums_moved, 16)
            sp.wait_ge(rec_done, 1)
            sp.dma_start(scratch.rec.rearrange("h (p b) -> p h b", p=P), rec[:]).then_inc(sums_moved, 16)
            sp.wait_ge(sums_moved, 32)

        @block.gpsimd
        def _(pool):
            nc.gpsimd.memset(vcur[:], 0.0).then_inc(v_ones, 1)
            pool.wait_ge(v_ones, 1)
            nc.gpsimd.memset(vcur[:, :, :, SUM:SUM + 1], 1.0).then_inc(v_ones, 1)
            vall = g.v[:].rearrange("p (t c) -> p t c", c=HEADS * E)

            def head(hh, b):
                pool.wait_ge(o_out, hh + 1)
                nc.gpsimd.tensor_copy(vcur[:, b, :, 0:E], vall[:, :, bass.ds(hh * E, E)]).then_inc(v_ready, 1)

            for c in range(HEADS // 2):
                for b in range(2):
                    head(c * 2 + b, b)

        @block.tensor
        def _(pe):
            def max_scores(count):
                for _ in range(min(count, FIRST_MAXES + (HEADS - 1) * MAXES - len(max_issued))):
                    n = len(max_issued)
                    if n < FIRST_MAXES:
                        hm, m = 0, n // 2 * QC + 2 + n % 2
                    else:
                        hm, m = 1 + (n - FIRST_MAXES) // MAXES, (n - FIRST_MAXES) % MAXES
                    if n == FIRST_MAXES:
                        pe.wait_ge(stacks_in, STACK_LOADS)
                    q, k, tile, chunk = head_steps(hm)
                    rows = slice(0, PAD.stop if n < FIRST_MAXES else QROWS)
                    if n >= MB:
                        pe.wait_ge(max_done, n - MB + 1)
                    nc.tensor.matmul(ps_m[n % MB], q[rows, tile[m // QC]], k[rows, chunk[m % QC]],
                                     start=True, stop=True).then_inc(max_scored, 1)
                    max_issued.append(n)

            def copied_scores(t):
                q, k, tile, chunk = head_steps(0)
                pe.wait_ge(exp_done, t + 1)
                for j in range(2):
                    last = nc.tensor.matmul(ps_s[t % 2][:, j, :], q[0:PAD.stop, tile[t]], k[0:PAD.stop, chunk[j]],
                                            start=True, stop=True)
                last.then_inc(scored, 1)

            def scores(hh, kt, half):
                q, k, tile, chunk = head_steps(hh)
                u = 2 * kt + half
                pe.wait_ge(exp_done, FIRST + hh * UNITS + u + 1)
                for j in range(2):
                    last = nc.tensor.matmul(ps_s[half][:, j, :], k[0:QROWS + 2, tile[kt]],
                                            q[0:QROWS + 2, chunk[2 * half + j]], start=True, stop=True)
                last.then_inc(scored, 1)

            def weighted(hh, b, kt):
                pe.wait_ge(exp_done, FIRST + hh * UNITS + 2 * kt + 4)
                if kt == 0:
                    pe.wait_ge(v_ready, hh + 1)
                    pe.wait_ge(o_out, hh + 2)
                for j in range(QC):
                    u = 2 * kt + j // 2
                    mm = nc.tensor.matmul(ps_o[32 * j:32 * j + VC, :], vcur[:, b, kt, :],
                                          probs[:, u % RING, (j % 2) * W:(j % 2 + 1) * W],
                                          start=(kt == 0), stop=(kt == KTILES - 1))
                    if j % 2:
                        mm.then_inc(pv_done, 1)

            max_issued = []

            def head(hh, b, before):
                pe.wait_ge(neg_in, (hh + 2) * 16)
                for kt in range(KTILES):
                    scores(hh, kt, 0)
                    max_scores(1)
                    scores(hh, kt, 1)
                    max_scores(QC - 3)
                    if kt == 0 and before is not None:
                        weighted(*before)
                    if kt > 0:
                        weighted(hh, b, kt - 1)
                    max_scores(2)
                return hh, b, KTILES - 1

            for t in range(FIRST):
                copied_scores(t)
                max_scores(2)
            max_scores(AHEAD)
            pe.wait_ge(v_ones, 2)
            before = None
            for hh in range(HEADS):
                before = head(hh, hh % 2, before)
            weighted(*before)

        @block.scalar
        def _(act):
            act.sem_inc(exp_done, 2)
            act.sem_inc(o_out, 2)
            act.sem_inc(pv_done, RING)

            def out(hh, b, c):
                act.wait_ge(pv_done, (hh + 1) * UNITS + RING)
                act.wait_ge(o_stored[b], c * (2 * QC * 16))
                nc.scalar.copy(osb[:, b, :], ps_o).then_inc(o_out, 1)

            def head(hh, before=None):
                for u in range(UNITS):
                    act.wait_ge(scored, FIRST + hh * UNITS + u + 1)
                    act.wait_ge(pv_done, hh * UNITS + u + 1)
                    nc.scalar.activation(probs[:, u % RING, :].rearrange("p (j t) -> p j t", j=2), ps_s[u % 2],
                                         ACT.Exp).then_inc(exp_done, 1)
                    if u == 1 and before is not None:
                        out(*before)

            for t in range(FIRST):
                act.wait_ge(scored, t + 1)
                if t >= RING:
                    act.wait_ge(max_done, 2 * (t - RING + 1))
                nc.scalar.copy(probs[:, t % RING, :].rearrange("p (j t) -> p j t", j=2), ps_s[t % 2]).then_inc(exp_done, 1)
            before = None
            for hh in range(HEADS):
                head(hh, before)
                before = hh, hh % 2, hh // 2
            out(*before)

        @block.vector
        def _(dve):
            nc.vector.memset(negpart[:], 0.0)

            def row_max(hm):
                columns = QC if hm else 2
                first = FIRST_MAXES + (hm - 1) * MAXES if hm else 0
                for m in range(KTILES * columns):
                    n = first + m
                    dve.wait_ge(max_scored, n + 1)
                    if hm:
                        nc.vector.tensor_reduce(rowmax[:, m:m + 1], ps_m[n % MB], AX.X, ALU.max).then_inc(max_done, 1)
                    else:
                        dve.wait_ge(exp_done, m // 2 + 3)
                        nc.vector.tensor_tensor_scan(running[:, m], ps_m[n % MB], probs[:, m // 2 % RING, m % 2 * W:(m % 2 + 1) * W],
                                                     LOWEST, ALU.max, ALU.max).then_inc(max_done, 1)
                dve.wait_ge(max_done, first + KTILES * columns)
                found = rowmax[:] if hm else running[:, :, W - 1]
                nc.vector.tensor_reduce(negmax[:], found.rearrange("p (t c) -> p t c", c=columns),
                                        AX.X, ALU.max, negate=True).then_inc(neg_step, 1)
                dve.wait_ge(neg_step, hm * NEG + 1)
                nc.vector.tensor_copy(negpart[:, 0, 0:KTILES], negmax[:]).then_inc(neg_step, 1)
                dve.wait_ge(neg_step, hm * NEG + 2)
                nc.vector.tensor_tensor(negmax[:], negmax[:], negpart[:, 0, 0:KTILES], ALU.subtract).then_inc(neg_step, 1)
                dve.wait_ge(neg_step, hm * NEG + 3)
                nc.vector.tensor_copy(negpart[:, 1, 0:KTILES], negmax[:]).then_inc(neg_step, 1)
                dve.wait_ge(neg_step, hm * NEG + 4)
                dve.wait_ge(neg_stored, hm * 64)
                nc.vector.transpose(negturn[:].rearrange("p s c -> p (s c)"),
                                    negpart[:].rearrange("p s c -> p (s c)")).then_inc(neg_step, 1)

            for hm in range(HEADS):
                row_max(hm)
            dve.wait_ge(sums_moved, 16)
            nc.vector.reciprocal(rec[:], sums[:]).then_inc(rec_done, 1)


def experts(nc, d, g, scratch):
    TT = T // P
    TILES = TT + EXPERTS - 1
    A_BANKS, LAG = 3, 7
    LOADS, YSLOTS, BACKS = 4, 3, 4
    ROW = {w: i for i, w in enumerate((GATE_A, SCALE_B, SHIFT_B, GATE_B))}
    DVE_TILES = range(1, TT, 4)
    FILLED = 96
    with ExitStack() as ctx:
        sb, sem = sb_alloc(ctx, nc), sem_alloc(ctx, nc, "moe")
        wo = sb("moe_wo", [HEADS * E + 1, D])
        wos = sb("moe_wo_gated", [FILLED, D])
        wg = sb("moe_wg", [P, KT, EXPERTS])
        bg = sb("moe_bg", [P, EXPERTS])
        be = sb("moe_be", [EXPERTS, D])
        bes = sb("moe_be_gated", [EXPERTS, D])
        we = sb("moe_we", [P, EXPERTS, KT, D])
        order = sb("moe_order", [P, 2, P])
        first = sb("moe_first", [P, EXPERTS, TT])
        iota = sb("moe_iota", [P, EXPERTS])
        starts = sb("moe_starts", [P, TT])
        tiles = sb("moe_tiles", [P, TILES])
        rows = sb("moe_rows", [P, len(ROW), D])
        att = sb("moe_att", [FILLED, T])
        rec = sb("moe_rec", [HEADS * E, T])
        turned = rec[0:EXPERTS, :]
        x = sb("moe_x", [P, TT, D])
        h = sb("moe_h", [P, TT, D])
        back = h
        ht = sb("moe_ht", [P, 2, D])
        stat = sb("moe_stat", [P, TT, 6])
        meanvar = sb("moe_meanvar", [P, TT, 2])
        sd = sb("moe_sd", [P, TT])
        rstd = sb("moe_rstd", [P, TT])
        logit = sb("moe_logit", [P, TT, EXPERTS])
        top = sb("moe_top", [P, TT])
        chosen = sb("moe_chosen", [P, TT])
        onehot = sb("moe_onehot", [P, TT, EXPERTS])
        total = sb("moe_total", [P, EXPERTS, TT])
        upto = sb("moe_upto", [P, EXPERTS, TT])
        place = sb("moe_place", [P, EXPERTS, TT])
        count = sb("moe_count", [P, EXPERTS])
        ends = sb("moe_ends", [P, EXPERTS])
        base = sb("moe_base", [P, EXPERTS])
        past = sb("moe_past", [P, TILES, EXPERTS])
        owner = sb("moe_owner", [P, TILES])
        owner_int = sb("moe_owner_int", [P, TILES], I32)
        pos = sb("moe_pos", [P, TT])
        pos_int = sb("moe_pos_int", [P, TT], U32)
        zeros = sb("moe_zeros", [P, D])
        srt = sb("moe_sorted", [P, LOADS, D])
        y = sb("moe_y", [P, YSLOTS, D])
        x2t = sb("moe_x2t", [P, KT, W])
        psum = ctx.enter_context(nc.psum_tensor("moe_psum", [P, 8, W], F32))
        ps_rows = [psum[:, b, :] for b in (4, 5, 6, 7)]
        ps_a = [psum[:, b, :] for b in range(A_BANKS)]
        ps_gate = psum[:, 3, 0:TT * EXPERTS]
        ps_ht = [psum[:, b, :] for b in (4, 5)]
        ps_before, ps_total = psum[:, 6, 0:TT * EXPERTS], psum[:, 7, 0:TT * EXPERTS]
        ps_turn = [psum[0:EXPERTS, b, :] for b in range(NCH)]
        ps_bias = [psum[:, b, :] for b in (4, 5)]
        ps_st = [psum[:, b, :] for b in (0, 1)]
        ps_y = [psum[:, b, :] for b in (2, 3, 6)]
        ps_x2 = [psum[:, b, :] for b in (4, 5, 7)]
        weights_in, att_in, experts_in, zeros_set, zeroed = (sem(n) for n in (
            "weights_in", "att_in", "experts_in", "zeros_set", "zeroed"))
        x_in = [sem("x_even_in"), sem("x_odd_in")]
        rows_mm, rows_out, gated, ones_set, att_ready = (sem(n) for n in ("rows_mm", "rows_out", "gated", "ones_set", "att_ready"))
        att_mm, x1_done, stat_done, var_done, sd_done, rstd_done, norm_done, scaled, centred, h_done, ht_mm, ht_out, gate_mm = (sem(n) for n in (
            "att_mm x1_done stat_done var_done sd_done rstd_done norm_done scaled centred h_done ht_mm ht_out gate_mm").split())
        pick, chosen_done, count_mm, place_step, place_done, owner_done = (sem(n) for n in (
            "pick chosen_done count_mm place_step place_done owner_done").split())
        turn_mm, turned_out, bias_mm, biased = (sem(n) for n in "turn_mm turned_out bias_mm biased".split())
        scattered, st_mm, st_out, y_mm, y_done = (sem(n) for n in "scattered st_mm st_out y_mm y_done".split())
        srt_in = [sem(f"sorted{i}_in") for i in range(LOADS)]
        y_stored = [sem(f"y{i}_stored") for i in range(YSLOTS)]
        back_in = [sem(f"back{i}_in") for i in range(BACKS)]
        x2_done, x2_mm, x2_out, x2_stored = (sem(n) for n in "x2_done x2_mm x2_out x2_stored".split())
        block = ctx.enter_context(nc.Block())
        xdst = scratch.x2.rearrange("(k p) t -> p k t", p=P)
        CONSTS = ((wo, "wo"), (be, "be"), (order, "order"), (first, "first"), (iota, "iota"), (starts, "starts"), (tiles, "tiles"))

        @block.sync
        def _(sp):
            sp.dma_start(att[0:HEADS * E, :], scratch.num).then_inc(att_in, 16)
            sp.dma_start(rec[:], scratch.rec.unsqueeze(1).to_broadcast([HEADS, E, T])).then_inc(att_in, 16)
            sp.dma_start(wg[:], d["wg"].rearrange("(k p) m -> p k m", p=P)).then_inc(weights_in, 16)
            sp.dma_start(bg[:], d["bg"].to_broadcast([P, EXPERTS])).then_inc(weights_in, 16)
            for dst, name in CONSTS:
                sp.dma_start(dst[:], d[name]).then_inc(weights_in, 16)
            for i in range(NCH):
                if i >= 2:
                    sp.wait_ge(x_in[i % 2], 16 * (i // 2))
                sp.dma_start(x[:, i * TT // NCH:(i + 1) * TT // NCH], d["xt"][i * W:(i + 1) * W, :].rearrange("(t p) f -> p t f", p=P)).then_inc(x_in[i % 2], 16)
            for b in range(2):
                sp.wait_ge(x_in[b], 16 * NCH // 2)
            sp.wait_ge(zeros_set, 1)
            sp.dma_start(scratch.sorted_h.rearrange("(j p) f -> p j f", p=P), zeros[:].unsqueeze(1).to_broadcast([P, TILES, D])).then_inc(zeroed, 16)
            for e in range(EXPERTS):
                sp.dma_start(we[:, e], d["we"][e].rearrange("(k p) m -> p k m", p=P)).then_inc(experts_in, 16)
            sp.wait_ge(scattered, 16 * TT)
            for j in range(TILES):
                if j >= LOADS:
                    sp.wait_ge(st_mm, j - LOADS + 1)
                sp.dma_start(srt[:, j % LOADS], scratch.sorted_h[j * P:(j + 1) * P, :]).then_inc(srt_in[j % LOADS], 16)
            for i in range(NCH):
                sp.wait_ge(x2_out, (i + 1) * TT // NCH)
                sp.dma_start(xdst[:, :, i * W:(i + 1) * W], x2t[:]).then_inc(x2_stored, 16)
            sp.wait_ge(x2_stored, 16 * NCH)

        @block.gpsimd
        def _(pool):
            pool.wait_ge(rows_out, len(ROW))
            modulated = 0
            for t in range(TT):
                pool.wait_ge(norm_done, t + 1)
                if t in DVE_TILES:
                    pool.wait_ge(h_done, t)
                    pool.sem_inc(h_done, 1)
                    continue
                nc.gpsimd.tensor_tensor(h[:, t], h[:, t], rows[:, ROW[SCALE_B]], ALU.mult).then_inc(scaled, 1)
                modulated += 1
                pool.wait_ge(scaled, modulated)
                nc.gpsimd.tensor_tensor(h[:, t], h[:, t], rows[:, ROW[SHIFT_B]], ALU.add).then_inc(h_done, 1)
            pool.wait_ge(zeroed, 16)
            pool.wait_ge(place_done, 1)
            pool.wait_ge(h_done, TT)
            for t in range(TT):
                pool.indirect_dma_start(scratch.sorted_h, bass.IndirectOffsetOnAxis(ap=pos_int[:, t:t + 1], axis=0), h[:, t], None).then_inc(scattered, 16)
            pool.wait_ge(scattered, 16 * TT)
            for s in range(YSLOTS):
                pool.wait_ge(y_stored[s], 16 * len(range(s, TILES, YSLOTS)))
            for t in range(TT):
                if t >= BACKS:
                    pool.wait_ge(back_in[t % BACKS], 16 * (t // BACKS))
                pool.indirect_dma_start(back[:, t], None, scratch.sorted_y, bass.IndirectOffsetOnAxis(ap=pos_int[:, t:t + 1], axis=0)
                                        ).then_inc(back_in[t % BACKS], 16)

        @block.tensor
        def _(pe):
            for i, which in enumerate(ROW):
                for k in range(KT):
                    last = nc.tensor.matmul(ps_rows[i][:, k * P:(k + 1) * P], g.mod[:, 0, which, k:k + 1].to_broadcast([P, P]), g.ident[:],
                                            start=True, stop=True)
                last.then_inc(rows_mm, 1)
            pe.wait_ge(weights_in, 16 * (len(CONSTS) + 2))
            pe.wait_ge(gated, 2)
            pe.wait_ge(ones_set, 3)
            pe.wait_ge(rows_out, len(ROW))
            for n in range(TT + LAG + 1):
                if n < TT:
                    if n % (TT // NCH) == 0:
                        pe.wait_ge(att_ready, n // (TT // NCH) + 1)
                    if n >= A_BANKS:
                        pe.wait_ge(x1_done, n - A_BANKS + 1)
                    nc.tensor.matmul(ps_a[n % A_BANKS], att[:, n * P:(n + 1) * P], wos[:], start=True, stop=True).then_inc(att_mm, 1)
                t = n - LAG
                if 0 <= t < TT:
                    pe.wait_ge(h_done, t + 1)
                    if t >= 2:
                        pe.wait_ge(ht_out, t - 1)
                    for k in range(KT):
                        last = nc.tensor.transpose(ps_ht[t % 2][:, k * P:(k + 1) * P], h[:, t, k * P:(k + 1) * P], g.ident[:])
                    last.then_inc(ht_mm, 1)
                t = n - LAG - 1
                if 0 <= t < TT:
                    pe.wait_ge(ht_out, t + 1)
                    out = ps_gate[:, t * EXPERTS:(t + 1) * EXPERTS]
                    for k in range(KT):
                        last = nc.tensor.matmul(out, ht[:, t % 2, k * P:(k + 1) * P], wg[:, k, :], start=(k == 0), stop=(k == KT - 1))
                    last.then_inc(gate_mm, 1)
            pe.wait_ge(chosen_done, 1)
            flat = onehot[:].rearrange("p t e -> p (t e)")
            nc.tensor.matmul(ps_before, order[:, 0], flat, start=True, stop=True)
            nc.tensor.matmul(ps_total, order[:, 1], flat, start=True, stop=True).then_inc(count_mm, 1)
            for i in range(NCH):
                for t in range(TT // NCH):
                    last = nc.tensor.transpose(ps_turn[i][:, t * P:(t + 1) * P], onehot[:, i * TT // NCH + t, :], g.ident[:])
                last.then_inc(turn_mm, 1)
            for t in range(TT):
                if t % (TT // NCH) == 0:
                    pe.wait_ge(turned_out, t // (TT // NCH) + 1)
                if t >= 2:
                    pe.wait_ge(biased, t - 1)
                nc.tensor.matmul(ps_bias[t % 2], turned[:, t * P:(t + 1) * P], bes[:], start=True, stop=True).then_inc(bias_mm, 1)
            pe.wait_ge(owner_done, 1)
            pe.wait_ge(experts_in, 16 * EXPERTS)

            def turn(j):
                pe.wait_ge(srt_in[j % LOADS], 16 * (j // LOADS + 1))
                if j >= 2:
                    pe.wait_ge(st_out, j - 1)
                for k in range(KT):
                    last = nc.tensor.transpose(ps_st[j % 2][:, k * P:(k + 1) * P], srt[:, j % LOADS, k * P:(k + 1) * P], g.ident[:])
                last.then_inc(st_mm, 1)

            turn(0)
            for j in range(TILES):
                expert = pe.value_load(owner_int[0:1, j:j + 1], min_val=0, max_val=EXPERTS - 1)
                if j + 1 < TILES:
                    turn(j + 1)
                pe.wait_ge(st_out, j + 1)
                if j >= YSLOTS:
                    pe.wait_ge(y_done, j - YSLOTS + 1)
                for k in range(KT):
                    last = nc.tensor.matmul(ps_y[j % YSLOTS], ht[:, j % 2, k * P:(k + 1) * P],
                                            we[:, bass.ds(expert, 1), k, :].rearrange("p o m -> p (o m)"), start=(k == 0), stop=(k == KT - 1))
                last.then_inc(y_mm, 1)
            for t in range(TT):
                pe.wait_ge(x2_done, t + 1)
                if t >= len(ps_x2):
                    pe.wait_ge(x2_out, t - len(ps_x2) + 1)
                for k in range(KT):
                    last = nc.tensor.transpose(ps_x2[t % len(ps_x2)][:, k * P:(k + 1) * P], x[:, t, k * P:(k + 1) * P], g.ident[:])
                last.then_inc(x2_mm, 1)

        @block.scalar
        def _(act):
            for i in range(len(ROW)):
                act.wait_ge(rows_mm, i + 1)
                nc.scalar.copy(rows[:, i], ps_rows[i]).then_inc(rows_out, 1)
            for n in range(TT + 4):
                if n < TT:
                    act.wait_ge(var_done, n + 1)
                    nc.scalar.activation(sd[:, n:n + 1], meanvar[:, n, 1:2], ACT.Sqrt, bias=g.ln_eps[:, 0:1]).then_inc(sd_done, 1)
                t = n - 4
                if t >= 0:
                    act.wait_ge(ht_mm, t + 1)
                    if t >= 2:
                        act.wait_ge(gate_mm, t - 1)
                    nc.scalar.copy(ht[:, t % 2], ps_ht[t % 2]).then_inc(ht_out, 1)
            for i in range(NCH):
                act.wait_ge(turn_mm, i + 1)
                nc.scalar.copy(turned[:, i * W:(i + 1) * W], ps_turn[i]).then_inc(turned_out, 1)

            def store(j):
                act.wait_ge(y_done, j + 1)
                act.dma_start(scratch.sorted_y[j * P:(j + 1) * P, :], y[:, j % YSLOTS]).then_inc(y_stored[j % YSLOTS], 16)

            for j in range(TILES):
                act.wait_ge(st_mm, j + 1)
                act.wait_ge(gate_mm, TT)
                if j >= 2:
                    act.wait_ge(y_mm, j - 1)
                nc.scalar.copy(ht[:, j % 2], ps_st[j % 2]).then_inc(st_out, 1)
                if j >= 3:
                    store(j - 3)
            for j in range(TILES - 3, TILES):
                store(j)
            for t in range(TT):
                act.wait_ge(x2_mm, t + 1)
                if t >= TT // NCH and t % (TT // NCH) == 0:
                    act.wait_ge(x2_stored, 16 * (t // (TT // NCH)))
                at = t % (TT // NCH) * P
                nc.scalar.copy(x2t[:, :, at:at + P], ps_x2[t % len(ps_x2)].rearrange("p (k t) -> p k t", k=KT)).then_inc(x2_out, 1)

        @block.vector
        def _(dve):
            nc.vector.memset(zeros[:], 0.0).then_inc(zeros_set, 1)
            for filled in (att, wos):
                nc.vector.memset(filled[HEADS * E:, :], 0.0).then_inc(ones_set, 1)
            dve.wait_ge(ones_set, 2)
            nc.vector.memset(att[HEADS * E:HEADS * E + 1, :], 1.0).then_inc(ones_set, 1)
            dve.wait_ge(weights_in, 16 * (len(CONSTS) + 2))
            dve.wait_ge(rows_out, len(ROW))
            nc.vector.tensor_tensor(wos[0:HEADS * E + 1], wo[:], rows[0:HEADS * E + 1, ROW[GATE_A]], ALU.mult).then_inc(gated, 1)
            nc.vector.tensor_tensor(bes[:], be[:], rows[0:EXPERTS, ROW[GATE_B]], ALU.mult).then_inc(gated, 1)
            dve.wait_ge(att_in, 32)

            for i in range(NCH):
                sl = slice(i * W, (i + 1) * W)
                nc.vector.scalar_tensor_tensor(att[0:HEADS * E, sl], att[0:HEADS * E, sl], float((HEADS * E) ** -0.5), rec[:, sl],
                                               ALU.mult, ALU.mult).then_inc(att_ready, 1)

            def residual(t):
                if t % (TT // NCH) == 0:
                    i = t // (TT // NCH)
                    dve.wait_ge(x_in[i % 2], 16 * (i // 2 + 1))
                dve.wait_ge(att_mm, t + 1)
                nc.vector.tensor_tensor(x[:, t], x[:, t], ps_a[t % A_BANKS], ALU.add).then_inc(x1_done, 1)

            def statistics(t):
                dve.wait_ge(x1_done, t + 1)
                nc.vector.bn_stats(stat[:, t], x[:, t]).then_inc(stat_done, 1)

            def variance(t):
                dve.wait_ge(stat_done, t + 1)
                nc.vector.bn_aggr(meanvar[:, t], stat[:, t]).then_inc(var_done, 1)

            def inverse(t):
                dve.wait_ge(sd_done, t + 1)
                nc.vector.reciprocal(rstd[:, t:t + 1], sd[:, t:t + 1]).then_inc(rstd_done, 1)

            def normalise(t):
                dve.wait_ge(rstd_done, t + 1)
                if t in DVE_TILES:
                    nc.vector.scalar_tensor_tensor(h[:, t], x[:, t], meanvar[:, t, 0:1], rows[:, ROW[SCALE_B]],
                                                   ALU.subtract, ALU.mult).then_inc(centred, 1)
                else:
                    nc.vector.tensor_scalar(h[:, t], x[:, t], meanvar[:, t, 0:1], rstd[:, t:t + 1], ALU.subtract, ALU.mult).then_inc(norm_done, 1)

            def modulate(t):
                dve.wait_ge(centred, DVE_TILES.index(t) + 1)
                nc.vector.scalar_tensor_tensor(h[:, t], h[:, t], rstd[:, t:t + 1], rows[:, ROW[SHIFT_B]], ALU.mult, ALU.add).then_inc(norm_done, 1)

            for n in range(TT + 3):
                if 0 <= n - 2 < TT:
                    inverse(n - 2)
                if n < TT:
                    residual(n)
                if 0 <= n - 1 < TT:
                    variance(n - 1)
                if 0 <= n - 2 < TT:
                    normalise(n - 2)
                if n < TT:
                    statistics(n)
                if n - 2 in DVE_TILES:
                    modulate(n - 2)

            def step(instruction, semaphore, n):
                instruction.then_inc(semaphore, 1)
                dve.wait_ge(semaphore, n)

            each = [P, TT, EXPERTS]
            dve.wait_ge(gate_mm, TT)
            step(nc.vector.tensor_tensor(logit[:], ps_gate.rearrange("p (t e) -> p t e", e=EXPERTS), bg[:].unsqueeze(1).to_broadcast(each), ALU.add), pick, 1)
            step(nc.vector.tensor_reduce(top[:], logit[:], AX.X, ALU.max), pick, 2)
            step(nc.vector.tensor_tensor(logit[:], logit[:], top[:].unsqueeze(2).to_broadcast(each), ALU.is_equal), pick, 3)
            step(nc.vector.scalar_tensor_tensor(logit[:], logit[:], -float(EXPERTS), iota[:].unsqueeze(1).to_broadcast(each), ALU.mult, ALU.add), pick, 4)
            step(nc.vector.tensor_reduce(chosen[:], logit[:], AX.X, ALU.min), pick, 5)
            step(nc.vector.tensor_scalar(chosen[:], chosen[:], float(EXPERTS), float(EXPERTS - 1), ALU.add, ALU.min), pick, 6)
            nc.vector.tensor_tensor(onehot[:], iota[:].unsqueeze(1).to_broadcast(each), chosen[:].unsqueeze(2).to_broadcast(each),
                                    ALU.is_equal).then_inc(chosen_done, 1)
            dve.wait_ge(count_mm, 1)
            by_expert = [P, EXPERTS, TT]
            step(nc.vector.tensor_copy(total[:], ps_total.rearrange("p (t e) -> p e t", e=EXPERTS)), place_step, 1)
            step(nc.vector.tensor_tensor_scan(upto[:].rearrange("p e t -> p (e t)"), first[:].rearrange("p e t -> p (e t)"),
                                              total[:].rearrange("p e t -> p (e t)"), 0.0, ALU.mult, ALU.add), place_step, 2)
            step(nc.vector.tensor_tensor(place[:], upto[:, :, TT - 1:TT].to_broadcast(by_expert), starts[:].unsqueeze(1).to_broadcast(by_expert),
                                         ALU.is_gt), place_step, 3)
            step(nc.vector.tensor_reduce(count[:], place[:], AX.X, ALU.add), place_step, 4)
            step(nc.vector.tensor_tensor_scan(ends[:], order[:, 1, 0:EXPERTS], count[:], 0.0, ALU.mult, ALU.add), place_step, 5)
            wide = [P, TILES, EXPERTS]
            step(nc.vector.tensor_tensor(past[:], ends[:].unsqueeze(1).to_broadcast(wide), tiles[:].unsqueeze(2).to_broadcast(wide), ALU.is_le), place_step, 6)
            step(nc.vector.tensor_reduce(owner[:], past[:], AX.X, ALU.add), place_step, 7)
            step(nc.vector.tensor_scalar(owner[:], owner[:], float(EXPERTS - 1), None, ALU.min), place_step, 8)
            nc.vector.tensor_copy(owner_int[:], owner[:]).then_inc(owner_done, 1)
            step(nc.vector.tensor_tensor(base[:], ends[:], count[:], ALU.subtract), place_step, 9)
            step(nc.vector.tensor_tensor(upto[:], upto[:], total[:], ALU.subtract), place_step, 10)
            step(nc.vector.scalar_tensor_tensor(upto[:], base[:].unsqueeze(2).to_broadcast(by_expert), float(P), upto[:], ALU.mult, ALU.add), place_step, 11)
            by_tile = logit
            step(nc.vector.tensor_tensor(by_tile[:], upto[:].rearrange("p e t -> p t e"), ps_before.rearrange("p (t e) -> p t e", e=EXPERTS), ALU.add), place_step, 12)
            step(nc.vector.tensor_tensor(by_tile[:], by_tile[:], onehot[:], ALU.mult), place_step, 13)
            step(nc.vector.tensor_reduce(pos[:], by_tile[:], AX.X, ALU.add), place_step, 14)
            nc.vector.tensor_copy(pos_int[:], pos[:]).then_inc(place_done, 1)
            for t in range(TT):
                dve.wait_ge(bias_mm, t + 1)
                nc.vector.tensor_tensor(x[:, t], x[:, t], ps_bias[t % 2], ALU.add).then_inc(biased, 1)
            for j in range(TILES):
                dve.wait_ge(y_mm, j + 1)
                if j >= YSLOTS:
                    dve.wait_ge(y_stored[j % YSLOTS], 16 * (j // YSLOTS))
                nc.vector.tensor_tensor(y[:, j % YSLOTS], ps_y[j % YSLOTS], rows[:, ROW[GATE_B]], ALU.mult).then_inc(y_done, 1)
            dve.wait_ge(biased, TT)
            for t in range(TT):
                dve.wait_ge(back_in[t % BACKS], 16 * (t // BACKS + 1))
                nc.vector.tensor_tensor(x[:, t], x[:, t], back[:, t], ALU.add).then_inc(x2_done, 1)


def state_space(nc, d, g, scratch):
    ROWS = RANK + 2 * NST
    ST = SW // P
    GROUPS = NST // NG
    J = P // 32
    UNITS = DT * GROUPS
    STEP_EXP = J * GROUPS
    HALF = DT // 2
    with ExitStack() as ctx:
        sb, sem = sb_alloc(ctx, nc), sem_alloc(ctx, nc, "ssm")
        win = sb("ssm_win", [P, KT, 2 * DI])
        wout = sb("ssm_wout", [P, DT, D])
        wx = sb("ssm_wx", [P, DT, ROWS])
        wdt = sb("ssm_wdt", [RANK, DI])
        convw = sb("ssm_convw", [P, DT, TAPS])
        convb = sb("ssm_convb", [P, DT])
        dtb = sb("ssm_dtb", [P, DT])
        amat = sb("ssm_a", [P, DT, GROUPS, J])
        dpar = sb("ssm_d", [P, DT])
        lnw = sb("ssm_lnw", [ROWS, 1])
        group = sb("ssm_group", [ROWS, 3])
        select = sb("ssm_select", [P, 32])
        conv = sb("ssm_conv", [P, DT, TAPS, P])
        x = sb("ssm_x", [P, KT, SW])
        xres = sb("ssm_xres", [P, KT, SW])
        logv = sb("ssm_logv", [P, ST])
        rstd = sb("ssm_rstd", [P, ST])
        h = sb("ssm_h", [P, 2, KT, SW])
        halo = sb("ssm_halo", [P, DT, TAPS - 1])
        upre = sb("ssm_upre", [P, 2, SW + TAPS - 1])
        u = sb("ssm_u", [P, 2, DT, SW])
        gate = sb("ssm_gate", [P, DT, SW])
        proj = sb("ssm_proj", [ROWS, SW])
        rms = sb("ssm_rms", [P, ST, 3])
        rwide = sb("ssm_rwide", [P, ST, ROWS])
        normed = sb("ssm_normed", [ROWS, SW])
        bc = sb("ssm_bc", [P, 2, 2, GROUPS, SW])
        soft = sb("ssm_soft", [P, DT - 2, SW])
        delta = sb("ssm_delta", [P, DT, SW])
        du = sb("ssm_du", [P, 2, SW])
        rep = sb("ssm_rep", [P, 2, 2, J, SW])
        decay = sb("ssm_decay", [P, SLOTS, J, SW])
        scan = sb("ssm_scan", [P, SLOTS, J, SW])
        state = sb("ssm_state", [P, DT, GROUPS, J])
        y = sb("ssm_y", [P, 2, DT, SW])
        psum = ctx.enter_context(nc.psum_tensor("ssm_psum", [P, 8, W], F32))
        ps_y = [psum[:, s, 0:SW] for s in (0, 1)]
        ps_p = [psum[:, s, 0:SW] for s in (2, 3)]
        ps_c = [psum[:, s, 0:SW] for s in (4, 5)]
        ps_z = psum[:, 6, :].rearrange("p (i t) -> p i t", i=2)
        ps_n, ps_v = psum[:, 7, 0:SW], psum[:, 7, SW:SW + 8]
        scale, shift, gates = g.mod[:, 1, SCALE_A], g.mod[:, 1, SHIFT_A], g.mod[:, 1, GATE_A]
        (weights_in, win_in, diag_done, zeroed, x_in, mean_done, centred_done, square_done, var_done, logv_done, rstd_done, bcast_done,
         norm_done, h_done, halo_in, halo_saved, proj_done, upre_out, conv_done, conv_out, u_done, wx_done, proj_out, stat_done, rlog_done,
         rms_done, rwide_done, rb_done, normed_done, bc_stored, wdt_done, abs_done, expneg_done, soft_done, relu_done,
         delta_done, du_done, drive_stored, decay_done, input_done, scan_done, carry_done, read_done, sum_done, skip_done, summed, yraw_done,
         gate_mm, gate_out, gate_done, ygate_done, out_mm, x3_done, x3_stored, xres_in) = (sem(n) for n in (
             "weights_in win_in diag_done zeroed x_in mean_done centred_done square_done var_done logv_done rstd_done bcast_done "
             "norm_done h_done halo_in halo_saved proj_done upre_out conv_done conv_out u_done wx_done proj_out stat_done rlog_done "
             "rms_done rwide_done rb_done normed_done bc_stored wdt_done abs_done expneg_done soft_done relu_done "
             "delta_done du_done drive_stored decay_done input_done scan_done carry_done read_done sum_done skip_done summed yraw_done "
             "gate_mm gate_out gate_done ygate_done out_mm x3_done x3_stored xres_in").split())
        rep_in = [sem("rep_even_in"), sem("rep_odd_in")]
        bc_in = [sem("bc_even_in"), sem("bc_odd_in")]
        block = ctx.enter_context(nc.Block())
        xsrc = scratch.x2.rearrange("(k p) t -> p k t", p=P)
        xdst = scratch.x3.rearrange("(k p) t -> p k t", p=P)

        PROJ = {0: 0, 1: 1, 3: 2, 4: 3, 5: 4, 7: 5, 9: 6, 10: 7}
        CARRY = {q + 2: i for q, i in PROJ.items()}
        U_COPY = {q + 3: i for q, i in PROJ.items()}
        SAVE = {q + 5: i for q, i in PROJ.items()}
        CONV = {q + 1: i for q, i in PROJ.items()}
        CONV_OUT = {q + 4: i for q, i in PROJ.items()}
        GATE = {12: 0, 13: 1, 15: 2, 16: 3, 17: 4, 18: 5, 19: 6, 20: 7}
        GATE_OUT = {q + 4: i for q, i in GATE.items()}
        SILU, WX, PROJ_OUT, STAT, RMS, RMS_WIDE, RB, NORMED, GATE_SILU = 16, 15, 18, 17, 20, 20, 20, 21, 24
        Z = {21: 0, 22: 1, 25: 2, 27: 3}
        ABS = {25: 0, 28: 1, 30: 2, 31: 3}
        LOG, DELTA = {28: 0, 31: 1}, 29
        DRIVE_FIRST = 28
        MEAN, CENTRED, SQUARE, VAR, RSTD, BCAST, NORM, H_OUT = 22, 24, 26, 24, 28, 26, 31, 31
        OUT = 24
        RESIDUAL = {OUT + 5 + 2 * m: m for m in range(KT)}
        PAIRS_Z = DT // 2
        BATCH = ((0, 2), (2, DT))

        def soft_of(batch):
            t0, t1 = BATCH[batch]
            at = (t0 - 2) % (DT - 2)
            return soft[:, at:at + t1 - t0]

        def ahead(c, t):
            return (c, t + 2) if t + 2 < DT else (c + 1, t + 2 - DT)

        @block.sync
        def _(sp):
            def load_x(c):
                sp.wait_ge(h_done, c)
                sp.dma_start(x[:], xsrc[:, :, c * SW:(c + 1) * SW]).then_inc(x_in, 16)

            def bc_rows(c):
                sp.wait_ge(normed_done, c + 1)
                sp.dma_start(scratch.bc, normed[RANK:ROWS, :]).then_inc(bc_stored, 16)
                sp.wait_ge(bc_stored, 16 * (c + 1))
                if c >= 2:
                    sp.wait_ge(read_done, (c - 1) * UNITS)
                src = scratch.bc.rearrange("(s k n) t -> n s k t", s=2, n=NG)
                for n in range(NG):
                    sp.dma_start(bc[32 * n:32 * n + 32, c % 2], src[n].unsqueeze(0).to_broadcast([32, 2, GROUPS, SW])).then_inc(bc_in[c % 2], 16)

            def repeat(c, t):
                s = c * DT + t
                sp.wait_ge(du_done, s + 1)
                sp.dma_start(scratch.drive[s % 2, 0], delta[:, t, :]).then_inc(drive_stored, 16)
                sp.dma_start(scratch.drive[s % 2, 1], du[:, s % 2]).then_inc(drive_stored, 16)
                sp.wait_ge(drive_stored, 32 * (s + 1))
                if s >= 2:
                    sp.wait_ge(decay_done, (s - 1) * STEP_EXP)
                    sp.wait_ge(input_done, (s - 1) * GROUPS)
                src = scratch.drive[s % 2].rearrange("q (j i) t -> i q j t", j=J)
                for n in range(NG):
                    sp.dma_start(rep[32 * n:32 * n + 32, s % 2], src).then_inc(rep_in[s % 2], 16)

            def load_residual(c):
                if c >= 1:
                    sp.wait_ge(x3_stored, 16 * c)
                sp.dma_start(xres[:], xsrc[:, :, c * SW:(c + 1) * SW]).then_inc(xres_in, 16)

            def store(c):
                sp.wait_ge(x3_done, (c + 1) * KT)
                sp.dma_start(xdst[:, :, c * SW:(c + 1) * SW], xres[:]).then_inc(x3_stored, 16)

            load_x(0)
            for dst, src in ((convw, d["convw"]), (convb, d["convb"]),
                             (wx, d["wx"].rearrange("(k p) m -> p k m", p=P)), (group, d["group"]), (lnw, d["lnw"]),
                             (wdt, d["wdt"]), (dtb, d["dtb"]), (amat, d["a"]), (dpar, d["d"]), (select, d["select"])):
                sp.dma_start(dst[:], src).then_inc(weights_in, 16)
            wsrc = d["win"].rearrange("(k p) m -> p k m", p=P)
            sp.dma_start(win[:, :, 0:DI], wsrc[:, :, 0:DI]).then_inc(win_in, 16)
            sp.wait_ge(win_in, 16)
            sp.dma_start(win[:, :, DI:], wsrc[:, :, DI:]).then_inc(win_in, 16)
            sp.dma_start(wout[:], d["wout"].rearrange("(k p) m -> p k m", p=P)).then_inc(win_in, 16)
            load_x(1)
            bc_rows(0)
            repeat(0, 0)
            repeat(0, 1)
            for c in range(SCH):
                for t in range(DT):
                    if t == 1 and c >= 2:
                        store(c - 2)
                    if t == 1 and c + 2 < SCH:
                        load_x(c + 2)
                    if t == 2 and c >= 1:
                        load_residual(c - 1)
                    c2, t2 = ahead(c, t)
                    if t == DT - 2 and c + 1 < SCH:
                        bc_rows(c + 1)
                    if c2 < SCH:
                        repeat(c2, t2)
            store(SCH - 2)
            load_residual(SCH - 1)
            store(SCH - 1)
            sp.wait_ge(x3_stored, 16 * SCH)

        @block.gpsimd
        def _(pool):
            nc.gpsimd.memset(state[:], 0.0).then_inc(zeroed, 1)
            nc.gpsimd.memset(halo[:], 0.0).then_inc(zeroed, 1)
            pool.wait_ge(weights_in, 16 * 10)
            for t in range(DT):
                for k in range(TAPS):
                    nc.gpsimd.tensor_scalar(conv[:, t, k, :], g.ident[:], convw[:, t, k:k + 1], 0.0, ALU.mult, ALU.add).then_inc(diag_done, 1)

            def drive_input(c, t):
                s = c * DT + t
                pool.wait_ge(delta_done, 2 * c + (1 if t < BATCH[0][1] else 2))
                pool.wait_ge(u_done, c + 1)
                if s >= 2:
                    pool.wait_ge(drive_stored, (s - 1) * 32)
                nc.gpsimd.tensor_tensor(du[:, s % 2], delta[:, t, :], u[:, c % 2, t, :], ALU.mult).then_inc(du_done, 1)

            def gate_y(c, part):
                pool.wait_ge(yraw_done, c * DT + 2 * part + 2)
                pool.wait_ge(gate_done, c + 1)
                sl = slice(2 * part, 2 * part + 2)
                nc.gpsimd.tensor_tensor(y[:, c % 2, sl], y[:, c % 2, sl], gate[:, sl], ALU.mult).then_inc(ygate_done, 1)

            drive_input(0, 0)
            drive_input(0, 1)
            for c in range(SCH):
                for q in range(UNITS):
                    t, gr = q // GROUPS, q % GROUPS
                    Q = c * UNITS + q
                    if c >= 1 and 3 <= q < 7:
                        gate_y(c - 1, q - 3)
                    if q == 0:
                        pool.wait_ge(bc_in[c % 2], 64 * (c // 2 + 1))
                    pool.wait_ge(scan_done, (Q + 1) * J)
                    nc.gpsimd.tensor_copy(state[:, t, gr, :], scan[:, Q % SLOTS, :, SW - 1]).then_inc(carry_done, 1)
                    pool.wait_ge(carry_done, Q + 1)
                    nc.gpsimd.tensor_tensor(scan[:, Q % SLOTS], scan[:, Q % SLOTS],
                                            bc[:, c % 2, 1, gr, :].unsqueeze(1).to_broadcast([P, J, SW]), ALU.mult).then_inc(read_done, 1)
                    c2, t2 = ahead(c, t)
                    if c2 < SCH and q == (DRIVE_FIRST if (c2, t2) == (c + 1, 0) else t * GROUPS + GROUPS - 1):
                        drive_input(c2, t2)
                    elif c + 1 < SCH and q == DRIVE_FIRST:
                        drive_input(c + 1, 0)
            for part in range(HALF):
                gate_y(SCH - 1, part)

        @block.tensor
        def _(pe):
            def mean(c):
                pe.wait_ge(x_in, 16 * (c + 1))
                if c >= 1:
                    pe.wait_ge(normed_done, c)
                for k in range(KT):
                    last = nc.tensor.matmul(ps_n, g.inv_d[:], x[:, k, :], start=(k == 0), stop=(k == KT - 1))
                last.then_inc(mean_done, 1)

            def var(c):
                pe.wait_ge(square_done, c + 1)
                for t in range(ST):
                    for k in range(KT):
                        last = nc.tensor.matmul(ps_v[:, t:t + 1], h[:, c % 2, k, t * P:(t + 1) * P], g.inv_d[:, 0:1],
                                                start=(k == 0), stop=(k == KT - 1))
                last.then_inc(var_done, 1)

            def bcast(c):
                pe.wait_ge(rstd_done, c + 1)
                for t in range(ST):
                    last = nc.tensor.matmul(ps_n[:, t * P:(t + 1) * P], rstd[:, t:t + 1].to_broadcast([P, P]), g.ident[:],
                                            start=True, stop=True)
                last.then_inc(bcast_done, 1)

            def project(c, i):
                if i == 0:
                    pe.wait_ge(h_done, c + 1)
                    if c >= 2:
                        pe.wait_ge(gate_out, (c - 1) * DT)
                if i >= 2:
                    pe.wait_ge(upre_out, c * DT + i - 1)
                for k in range(KT):
                    last = nc.tensor.matmul(ps_p[i % 2], win[:, k, i * P:(i + 1) * P], h[:, c % 2, k, :], start=(k == 0), stop=(k == KT - 1))
                last.then_inc(proj_done, 1)

            def convolve(c, i):
                pe.wait_ge(upre_out, c * DT + i + 1)
                if i >= 2:
                    pe.wait_ge(conv_out, c * DT + i - 1)
                elif c >= 3:
                    pe.wait_ge(x3_done, (c - 2) * KT)
                for k in range(TAPS):
                    last = nc.tensor.matmul(ps_c[i % 2], conv[:, i, k, :], upre[:, i % 2, k:k + SW], start=(k == 0), stop=(k == TAPS - 1))
                last.then_inc(conv_done, 1)

            def rows(c):
                pe.wait_ge(u_done, c + 1)
                for t in range(DT):
                    last = nc.tensor.matmul(ps_c[0][0:ROWS, :], wx[:, t, :], u[:, c % 2, t, :], start=(t == 0), stop=(t == DT - 1))
                last.then_inc(wx_done, 1)

            def mean_square(c):
                pe.wait_ge(proj_out, 2 * c + 2)
                for t in range(ST):
                    last = nc.tensor.matmul(ps_v[:, 3 * t:3 * t + 3], normed[:, t * P:(t + 1) * P], group[:], start=True, stop=True)
                last.then_inc(stat_done, 1)

            def rms_bcast(c):
                pe.wait_ge(rwide_done, 3 * (c + 1))
                for t in range(ST):
                    last = nc.tensor.matmul(ps_n[0:ROWS, t * P:(t + 1) * P], rwide[:, t, :], g.ident[:], start=True, stop=True)
                last.then_inc(rb_done, 1)

            def step_size(c, pair):
                n = c * PAIRS_Z + pair
                if pair == 0:
                    pe.wait_ge(normed_done, c + 1)
                if n >= 1:
                    pe.wait_ge(abs_done, 2 * n)
                    pe.wait_ge(relu_done, 2 * n)
                for i in range(2):
                    t = 2 * pair + i
                    last = nc.tensor.matmul(ps_z[:, i], wdt[:, t * P:(t + 1) * P], normed[0:RANK, :], start=True, stop=True)
                last.then_inc(wdt_done, 1)

            def gate_project(c, i):
                if i >= 2:
                    pe.wait_ge(gate_out, c * DT + i - 1)
                elif c + 1 < SCH:
                    pe.wait_ge(upre_out, (c + 2) * DT)
                for k in range(KT):
                    last = nc.tensor.matmul(ps_p[i % 2], win[:, k, DI + i * P:DI + (i + 1) * P], h[:, c % 2, k, :],
                                            start=(k == 0), stop=(k == KT - 1))
                last.then_inc(gate_mm, 1)

            def output(c, m, half):
                if half == 0:
                    if m == 0:
                        pe.wait_ge(ygate_done, (c + 1) * HALF)
                        if c + 2 < SCH:
                            pe.wait_ge(conv_out, (c + 3) * DT)
                            pe.wait_ge(proj_out, 2 * (c + 3))
                    if c * KT + m >= 2:
                        pe.wait_ge(x3_done, c * KT + m - 1)
                for t in range(half * HALF, (half + 1) * HALF):
                    last = nc.tensor.matmul(ps_c[m % 2], wout[:, t, m * P:(m + 1) * P], y[:, c % 2, t, :], start=(t == 0), stop=(t == DT - 1))
                if half == 1:
                    last.then_inc(out_mm, 1)

            def sum_states(c, q):
                t, gr = q // GROUPS, q % GROUPS
                Q, s = c * UNITS + q, c * DT + t
                if gr == 0 and s >= 2:
                    pe.wait_ge(yraw_done, s - 1)
                pe.wait_ge(read_done, Q + 1)
                for j in range(J):
                    last = nc.tensor.matmul(ps_y[t % 2][32 * j:32 * j + 32, :], select[:], scan[:, Q % SLOTS, j, :],
                                            start=(gr == 0), stop=False)
                last.then_inc(sum_done, 1)
                if gr == GROUPS - 1:
                    pe.wait_ge(skip_done, s + 1)
                    nc.tensor.matmul(ps_y[t % 2], g.ident[:], y[:, c % 2, t, :], start=False, stop=True).then_inc(summed, 1)

            def norm_chunk(c):
                mean(c)
                var(c)
                bcast(c)

            norm_chunk(0)
            pe.wait_ge(weights_in, 16 * 10)
            pe.wait_ge(win_in, 16)
            pe.wait_ge(diag_done, DT * TAPS)
            for i in range(DT):
                project(0, i)
                if i >= 1:
                    convolve(0, i - 1)
            convolve(0, DT - 1)
            rows(0)
            mean_square(0)
            rms_bcast(0)
            for pair in range(PAIRS_Z):
                step_size(0, pair)
            norm_chunk(1)
            pe.wait_ge(win_in, 48)
            for c in range(SCH):
                for q in range(UNITS):
                    if c + 1 < SCH:
                        if q in PROJ:
                            project(c + 1, PROJ[q])
                        if q in CONV:
                            convolve(c + 1, CONV[q])
                        if q == WX:
                            rows(c + 1)
                        if q == STAT:
                            mean_square(c + 1)
                        if q == RB:
                            rms_bcast(c + 1)
                    if q in GATE:
                        gate_project(c, GATE[q])
                    if c + 2 < SCH:
                        if q == MEAN:
                            mean(c + 2)
                        if q == VAR:
                            var(c + 2)
                        if q == BCAST:
                            bcast(c + 2)
                    if c >= 1 and q >= OUT:
                        output(c - 1, (q - OUT) // 2, (q - OUT) % 2)
                    if c + 1 < SCH and q in Z:
                        step_size(c + 1, Z[q])
                    sum_states(c, q)
            for m in range(KT):
                output(SCH - 1, m, 0)
                output(SCH - 1, m, 1)

        @block.scalar
        def _(act):
            def squares(c):
                act.wait_ge(centred_done, c + 1)
                if c >= 2:
                    act.wait_ge(gate_mm, (c - 1) * DT)
                nc.scalar.activation(h[:, c % 2], x[:], ACT.Square).then_inc(square_done, 1)

            def inverse_sd(c):
                act.wait_ge(var_done, c + 1)
                nc.scalar.activation(logv[:], ps_v[:, 0:ST], ACT.Ln, bias=g.ln_eps[:, 0:1]).then_inc(logv_done, 1)
                act.wait_ge(logv_done, c + 1)
                nc.scalar.activation(rstd[:], logv[:], ACT.Exp, scale=-0.5).then_inc(rstd_done, 1)

            def modulate(c):
                act.wait_ge(norm_done, c + 1)
                for k in range(KT):
                    last = nc.scalar.activation(h[:, c % 2, k, :], x[:, k, :], ACT.Identity, bias=shift[:, k:k + 1], scale=scale[:, k:k + 1])
                last.then_inc(h_done, 1)

            def copy_u(c, i):
                act.wait_ge(proj_done, c * DT + i + 1)
                n = c * DT + i
                act.wait_ge(halo_in, n + 1)
                if n >= 2:
                    act.wait_ge(halo_saved, n - 1)
                nc.scalar.copy(upre[:, i % 2, TAPS - 1:], ps_p[i % 2]).then_inc(upre_out, 1)

            def copy_conv(c, i):
                act.wait_ge(conv_done, c * DT + i + 1)
                if i == 0 and c >= 2:
                    act.wait_ge(skip_done, (c - 1) * DT)
                    act.wait_ge(du_done, (c - 1) * DT)
                nc.scalar.activation(u[:, c % 2, i, :], ps_c[i % 2], ACT.Identity, bias=convb[:, i:i + 1]).then_inc(conv_out, 1)

            def silu_u(c):
                act.wait_ge(conv_out, (c + 1) * DT)
                nc.scalar.activation(u[:, c % 2], u[:, c % 2], ACT.Silu).then_inc(u_done, 1)

            def copy_rows(c):
                act.wait_ge(wx_done, c + 1)
                if c >= 1:
                    act.wait_ge(wdt_done, c * PAIRS_Z)
                    act.wait_ge(bc_stored, c * 16)
                nc.scalar.activation(normed[:], ps_c[0][0:ROWS, :], ACT.Square).then_inc(proj_out, 1)
                act.wait_ge(normed_done, c)
                nc.scalar.copy(proj[:], ps_c[0][0:ROWS, :]).then_inc(proj_out, 1)

            def inverse_rms(c):
                act.wait_ge(stat_done, c + 1)
                flat = rms[:].rearrange("p t s -> p (t s)")
                act.wait_ge(rwide_done, 3 * c)
                nc.scalar.activation(flat, ps_v[:, 0:3 * ST], ACT.Ln, bias=g.rms_eps[:, 0:1]).then_inc(rlog_done, 1)
                act.wait_ge(rlog_done, c + 1)
                nc.scalar.activation(flat, flat, ACT.Exp, scale=-0.5).then_inc(rms_done, 1)

            def absolute(c, pair):
                n = c * PAIRS_Z + pair
                act.wait_ge(wdt_done, n + 1)
                if c >= 1:
                    act.wait_ge(drive_stored, ((c - 1) * DT + 2 * pair + 2) * 32)
                if pair == 0 and c >= 1:
                    act.wait_ge(delta_done, 2 * c)
                if pair == PAIRS_Z - 1:
                    act.wait_ge(delta_done, 2 * c + 1)
                for i in range(2):
                    t = 2 * pair + i
                    nc.scalar.activation(soft[:, (t - 2) % (DT - 2), :], ps_z[:, i], ACT.Abs, bias=dtb[:, t:t + 1]).then_inc(abs_done, 1)
                    nc.scalar.activation(delta[:, t, :], ps_z[:, i], ACT.Relu, bias=dtb[:, t:t + 1]).then_inc(relu_done, 1)

            def log1p_exp(c, batch):
                act.wait_ge(abs_done, c * DT + BATCH[batch][1])
                nc.scalar.activation(soft_of(batch), soft_of(batch), ACT.Exp, scale=-1.0).then_inc(expneg_done, 1)
                act.wait_ge(expneg_done, 2 * c + batch + 1)
                nc.scalar.activation(soft_of(batch), soft_of(batch), ACT.Ln, bias=1.0).then_inc(soft_done, 1)

            def copy_gate(c, i):
                act.wait_ge(gate_mm, c * DT + i + 1)
                if i == 0 and c >= 1:
                    act.wait_ge(ygate_done, c * HALF)
                nc.scalar.copy(gate[:, i, :], ps_p[i % 2]).then_inc(gate_out, 1)

            def silu_gate(c):
                act.wait_ge(gate_out, (c + 1) * DT)
                nc.scalar.activation(gate[:], gate[:], ACT.Silu).then_inc(gate_done, 1)

            def skip(c, t):
                if c >= 2:
                    act.wait_ge(out_mm, (c - 1) * KT)
                act.wait_ge(u_done, c + 1)
                nc.scalar.activation(y[:, c % 2, t, :], u[:, c % 2, t, :], ACT.Identity, scale=dpar[:, t:t + 1]).then_inc(skip_done, 1)

            def raw_y(c, t):
                act.wait_ge(summed, c * DT + t + 1)
                nc.scalar.copy(y[:, c % 2, t, :], ps_y[t % 2]).then_inc(yraw_done, 1)

            def decays(c, q):
                t, gr = q // GROUPS, q % GROUPS
                Q, s = c * UNITS + q, c * DT + t
                if gr == 0:
                    act.wait_ge(rep_in[s % 2], 64 * (s // 2 + 1))
                if Q >= SLOTS:
                    act.wait_ge(scan_done, (Q - SLOTS + 1) * J)
                for j in range(J):
                    nc.scalar.activation(decay[:, Q % SLOTS, j, :], rep[:, s % 2, 0, j, :], ACT.Exp,
                                         scale=amat[:, t, gr, j:j + 1]).then_inc(decay_done, 1)

            def norm_chunk(c):
                squares(c)
                inverse_sd(c)
                modulate(c)

            norm_chunk(0)
            act.wait_ge(weights_in, 16 * 10)
            for i in range(DT):
                copy_u(0, i)
                if i >= 1:
                    copy_conv(0, i - 1)
            copy_conv(0, DT - 1)
            silu_u(0)
            copy_rows(0)
            inverse_rms(0)
            absolute(0, 0)
            log1p_exp(0, 0)
            for pair in range(1, PAIRS_Z):
                absolute(0, pair)
            log1p_exp(0, 1)
            norm_chunk(1)
            for c in range(SCH):
                for q in range(UNITS):
                    if c + 1 < SCH:
                        if q in U_COPY:
                            copy_u(c + 1, U_COPY[q])
                        if q in CONV_OUT:
                            copy_conv(c + 1, CONV_OUT[q])
                        if q == SILU:
                            silu_u(c + 1)
                        if q == PROJ_OUT:
                            copy_rows(c + 1)
                        if q == RMS:
                            inverse_rms(c + 1)
                        if q in ABS:
                            absolute(c + 1, ABS[q])
                        if q in LOG:
                            log1p_exp(c + 1, LOG[q])
                    if q in GATE_OUT:
                        copy_gate(c, GATE_OUT[q])
                    if q % GROUPS == 0:
                        skip(c, q // GROUPS)
                    if q % GROUPS == 3 and c * DT + q // GROUPS >= 1:
                        s = c * DT + q // GROUPS - 1
                        raw_y(s // DT, s % DT)
                    if q == GATE_SILU:
                        silu_gate(c)
                    if c + 2 < SCH:
                        if q == SQUARE:
                            squares(c + 2)
                        if q == RSTD:
                            inverse_sd(c + 2)
                        if q == H_OUT:
                            modulate(c + 2)
                    decays(c, q)
            raw_y(SCH - 1, DT - 1)

        @block.vector
        def _(dve):
            def centre(c):
                dve.wait_ge(mean_done, c + 1)
                nc.vector.tensor_tensor(x[:], x[:], ps_n.unsqueeze(1).to_broadcast([P, KT, SW]), ALU.subtract).then_inc(centred_done, 1)

            def normalise(c):
                dve.wait_ge(bcast_done, c + 1)
                nc.vector.tensor_tensor(x[:], x[:], ps_n.unsqueeze(1).to_broadcast([P, KT, SW]), ALU.mult).then_inc(norm_done, 1)

            def carry_halo(c, i):
                n = c * DT + i
                if n >= 2:
                    dve.wait_ge(conv_done, n - 1)
                if c >= 1:
                    dve.wait_ge(halo_saved, n - DT + 1)
                nc.vector.tensor_copy(upre[:, i % 2, 0:TAPS - 1], halo[:, i, :]).then_inc(halo_in, 1)

            def save_halo(c, i):
                n = c * DT + i
                dve.wait_ge(upre_out, n + 1)
                dve.wait_ge(halo_in, n + 1)
                nc.vector.tensor_copy(halo[:, i, :], upre[:, i % 2, SW:SW + TAPS - 1]).then_inc(halo_saved, 1)

            def rms_wide(c):
                dve.wait_ge(rms_done, c + 1)
                for s, (at, n) in enumerate(((0, RANK), (RANK, NST), (RANK + NST, NST))):
                    nc.vector.tensor_copy(rwide[:, :, at:at + n], rms[:, :, s:s + 1].to_broadcast([P, ST, n])).then_inc(rwide_done, 1)

            def rms_norm(c):
                dve.wait_ge(rb_done, c + 1)
                nc.vector.scalar_tensor_tensor(normed[:], proj[:], lnw[:, 0:1], ps_n[0:ROWS, :], ALU.mult, ALU.mult).then_inc(normed_done, 1)

            def step_sizes(c, batch):
                t0, t1 = BATCH[batch]
                dve.wait_ge(relu_done, c * DT + t1)
                dve.wait_ge(soft_done, 2 * c + batch + 1)
                nc.vector.tensor_tensor(delta[:, t0:t1], delta[:, t0:t1], soft_of(batch), ALU.add).then_inc(delta_done, 1)

            def unit(c, q):
                t, gr = q // GROUPS, q % GROUPS
                Q, s = c * UNITS + q, c * DT + t
                if gr == 0:
                    dve.wait_ge(rep_in[s % 2], 64 * (s // 2 + 1))
                if q == 0:
                    dve.wait_ge(bc_in[c % 2], 64 * (c // 2 + 1))
                if Q >= SLOTS:
                    dve.wait_ge(sum_done, Q - SLOTS + 1)
                nc.vector.tensor_tensor(scan[:, Q % SLOTS], rep[:, s % 2, 1],
                                        bc[:, c % 2, 0, gr, :].unsqueeze(1).to_broadcast([P, J, SW]), ALU.mult).then_inc(input_done, 1)
                dve.wait_ge(input_done, Q + 1)
                if c >= 1:
                    dve.wait_ge(carry_done, Q - UNITS + 1)
                for j in range(J):
                    dve.wait_ge(decay_done, Q * J + j + 1)
                    nc.vector.tensor_tensor_scan(scan[:, Q % SLOTS, j, :], decay[:, Q % SLOTS, j, :], scan[:, Q % SLOTS, j, :],
                                                 state[:, t, gr, j:j + 1], ALU.mult, ALU.add).then_inc(scan_done, 1)

            def residual(c, m):
                if m == 0:
                    dve.wait_ge(xres_in, 16 * (c + 1))
                dve.wait_ge(out_mm, c * KT + m + 1)
                nc.vector.scalar_tensor_tensor(xres[:, m, :], ps_c[m % 2], gates[:, m:m + 1], xres[:, m, :], ALU.mult, ALU.add).then_inc(x3_done, 1)

            dve.wait_ge(x_in, 16)
            centre(0)
            normalise(0)
            dve.wait_ge(weights_in, 16 * 10)
            dve.wait_ge(zeroed, 2)
            for i in range(DT):
                carry_halo(0, i)
                save_halo(0, i)
            rms_wide(0)
            rms_norm(0)
            step_sizes(0, 0)
            step_sizes(0, 1)
            dve.wait_ge(x_in, 32)
            centre(1)
            normalise(1)
            for c in range(SCH):
                for q in range(UNITS):
                    if c + 1 < SCH:
                        if q in CARRY:
                            carry_halo(c + 1, CARRY[q])
                        if q in SAVE:
                            save_halo(c + 1, SAVE[q])
                        if q == RMS_WIDE:
                            rms_wide(c + 1)
                        if q == NORMED:
                            rms_norm(c + 1)
                        if q == DELTA:
                            step_sizes(c + 1, 0)
                    if c >= 1 and q == 0:
                        step_sizes(c, 1)
                    if c + 2 < SCH:
                        if q == CENTRED:
                            centre(c + 2)
                        if q == NORM:
                            normalise(c + 2)
                    if c >= 1 and q in RESIDUAL:
                        residual(c - 1, RESIDUAL[q])
                    if c >= 2 and q + UNITS in RESIDUAL:
                        residual(c - 2, RESIDUAL[q + UNITS])
                    unit(c, q)
            for q in range(UNITS, max(RESIDUAL) + 1):
                if q in RESIDUAL:
                    residual(SCH - 2, RESIDUAL[q])
            for m in range(KT):
                residual(SCH - 1, m)


def permuted_mlp(nc, d, g, scratch, out):
    MODS = (SCALE_B, SHIFT_B, GATE_B)
    QUAD = 4
    UPS, HIDS = 3, 2
    with ExitStack() as ctx:
        sb, sem = sb_alloc(ctx, nc), sem_alloc(ctx, nc, "mlp")
        perm = sb("mlp_perm", [P, KT], U32)
        rows = sb("mlp_rows", [P, NCH, KT], U32)
        x = sb("mlp_x", [P, KT, T])
        centred = sb("mlp_centred", [P, KT, T])
        modp = sb("mlp_mod", [P, KT, 4])
        modcols = sb("mlp_modcols", [P, KT, 4])
        up = sb("mlp_up", [P, MH, MM])
        down = sb("mlp_down", [P, MH, MD])
        hid = sb("mlp_hid", [P, HIDS, QUAD, W])
        y = sb("mlp_y", [P, 2, KT, W])
        psum = ctx.enter_context(nc.psum_tensor("mlp_psum", [P, 8, W], F32))
        scale = sb("mlp_scale", [P, KT])
        shift = sb("mlp_shift", [P, KT])
        ln = LayerNorm(nc, ctx, "ln4", g, psum, 4, x, centred, scale, shift)
        ps_up = [psum[:, b, :] for b in (4, 5, 6)]
        ps_y = [psum[:, b, :] for b in (0, 1, 2, 3, 7)]
        weights_in, perm_in, mod_set, mod_stored, mod_in, cols_done = (
            sem("weights_in"), sem("perm_in"), sem("mod_set"), sem("mod_stored"), sem("mod_in"), sem("cols_done"))
        rows_done = sem("rows_done")
        x_in = [sem("x_first_in"), sem("x_rest_in")]
        up_done, hid_done, down_done, y_done = sem("up_done"), sem("hid_done"), sem("down_done"), sem("y_done")
        block = ctx.enter_context(nc.Block())
        QUADS = NCH * KT

        @block.sync
        def _(sp):
            sp.dma_start(up[:], d["up"].rearrange("p (h m) -> p h m", h=MH)).then_inc(weights_in, 16)
            sp.dma_start(down[:], d["down"].rearrange("p (h e) -> p h e", h=MH)).then_inc(weights_in, 16)
            sp.wait_ge(mod_set, 4)
            sp.dma_start(scratch.modb.rearrange("(k p) s -> p k s", p=P), modcols[:]).then_inc(mod_stored, 16)

        @block.gpsimd
        def _(pool):
            pool.dma_start(perm[:], d["perm"]).then_inc(perm_in, 16)
            pool.wait_ge(perm_in, 16)
            for k in range(KT):
                pool.indirect_dma_start(x[:, k, :], None, scratch.x3, bass.IndirectOffsetOnAxis(ap=perm[:, k:k + 1], axis=0)).then_inc(x_in[k // 2], 16)
            pool.wait_ge(mod_stored, 16)
            for k in range(KT):
                pool.indirect_dma_start(modp[:, k, :], None, scratch.modb, bass.IndirectOffsetOnAxis(ap=perm[:, k:k + 1], axis=0)).then_inc(mod_in, 16)
            pool.wait_ge(rows_done, NCH)
            for i in range(NCH):
                for k in range(KT):
                    pool.wait_ge(y_done, i * KT + k + 1)
                    pool.indirect_dma_start(out, bass.IndirectOffsetOnAxis(ap=rows[:, i, k:k + 1], axis=0), y[:, i % 2, k, :], None
                                            ).then_inc(g.out_stored[i % 2], 16)
            for b in range(2):
                pool.wait_ge(g.out_stored[b], 16 * KT * NCH // 2)

        @block.tensor
        def _(pe):
            pe.wait_ge(weights_in, 32)
            for k in range(KT):
                if k % 2 == 0:
                    pe.wait_ge(x_in[k // 2], 32)
                ln.mean_part(pe, k)
            ln.variance(pe)
            ln.turn(pe)
            for i in range(NCH):
                ln.spread(pe, i)
            for q in range(QUADS + 1):
                if q < QUADS:
                    i, k = q // KT, q % KT
                    pe.wait_ge(ln.h_done, i + 1)
                    for s in range(QUAD):
                        n = q * QUAD + s
                        if n >= UPS:
                            pe.wait_ge(hid_done, n - UPS + 1)
                        nc.tensor.matmul(ps_up[n % UPS], up[:, k * QUAD + s, :], ln.h[:, i % 2, k, :], start=True, stop=True).then_inc(up_done, 1)
                if q >= 1:
                    last_q = q - 1
                    pe.wait_ge(hid_done, q * QUAD)
                    pe.wait_ge(ln.norm_done, NCH)
                    if last_q >= len(ps_y):
                        pe.wait_ge(y_done, last_q - len(ps_y) + 1)
                    for s in range(QUAD):
                        r = MD * s
                        last = nc.tensor.matmul(ps_y[last_q % len(ps_y)][r:r + MD, :], down[:, last_q % KT * QUAD + s, :],
                                                hid[:, last_q % HIDS, s, :], start=True, stop=True)
                    last.then_inc(down_done, 1)

        @block.scalar
        def _(act):
            for i in range(NCH):
                ln.squares(act, i)
            ln.deviation(act)
            act.wait_ge(cols_done, 2)
            ln.modulate(act, 0)
            for q in range(QUADS):
                i, k = q // KT, q % KT
                if k == 1 and i + 1 < NCH:
                    if i >= 1:
                        act.wait_ge(up_done, i * MH)
                    ln.modulate(act, i + 1)
                for s in range(QUAD):
                    n = q * QUAD + s
                    act.wait_ge(up_done, n + 1)
                    if q >= HIDS:
                        act.wait_ge(down_done, q - HIDS + 1)
                    nc.scalar.activation(hid[:, q % HIDS, s, :], ps_up[n % UPS], ACT.Gelu).then_inc(hid_done, 1)

        @block.vector
        def _(dve):
            ln.clear(dve)
            nc.vector.memset(modcols[:], 0.0).then_inc(mod_set, 1)
            dve.wait_ge(mod_set, 1)
            for s, which in enumerate(MODS):
                nc.vector.tensor_copy(modcols[:, :, s], g.mod[:, 1, which, :]).then_inc(mod_set, 1)
            dve.wait_ge(perm_in, 16)
            for i in range(NCH):
                nc.vector.tensor_scalar(rows[:, i, :], perm[:], float(i * D), None, ALU.add).then_inc(rows_done, 1)
            dve.wait_ge(mod_in, 16 * KT)
            nc.vector.tensor_copy(scale[:], modp[:, :, 0]).then_inc(cols_done, 1)
            nc.vector.tensor_copy(shift[:], modp[:, :, 1]).then_inc(cols_done, 1)
            for half in range(2):
                dve.wait_ge(x_in[half], 32)
            for i in range(NCH):
                ln.centre(dve, i)
            ln.inverse(dve)
            for i in range(NCH):
                ln.normalise(dve, i)
            for q in range(QUADS):
                i, k = q // KT, q % KT
                if i >= 2:
                    dve.wait_ge(g.out_stored[i % 2], i // 2 * 16 * KT)
                dve.wait_ge(down_done, q + 1)
                nc.vector.scalar_tensor_tensor(y[:, i % 2, k, :], ps_y[q % len(ps_y)], modp[:, k, 2:3], x[:, k, i * W:(i + 1) * W],
                                               ALU.mult, ALU.add).then_inc(y_done, 1)


STAGES = 6


def build(nc, d, out, stages=STAGES):
    scratch = Consts()
    scratch.parts = nc.dram_tensor("parts", [PARTS, 2 * HEADS * E, T], BF16).ap()
    neg = nc.dram_tensor("negmax_rows", [HEADS, 2, T // P, 4, 32], BF16).ap()

    class Rows:
        def __getitem__(self, hh):
            return neg[bass.ds(hh, 1)].rearrange("o s t q p -> (o s) t q p")
    scratch.neg = Rows()
    scratch.num = nc.dram_tensor("att_num", [HEADS * E, T], F32).ap()
    scratch.den = nc.dram_tensor("att_den", [HEADS, T], F32).ap()
    scratch.rec = nc.dram_tensor("att_den_inv", [HEADS, T], F32).ap()
    scratch.sorted_h = nc.dram_tensor("sorted_rows", [T + (EXPERTS - 1) * P, D], F32).ap()
    scratch.sorted_y = nc.dram_tensor("sorted_results", [T + (EXPERTS - 1) * P, D], F32).ap()
    scratch.x2 = nc.dram_tensor("x_layer0", [D, T], F32).ap()
    scratch.bc = nc.dram_tensor("bc_rows", [2 * NST, SW], F32).ap()
    scratch.drive = nc.dram_tensor("drive_rows", [2, 2, P, SW], F32).ap()
    scratch.x3 = nc.dram_tensor("x_after_ssm", [D, T], F32).ap()
    scratch.modb = nc.dram_tensor("mod_rows", [D, 4], F32).ap()
    with ExitStack() as ctx:
        sb = sb_alloc(ctx, nc)
        g = Consts()
        g.used = []
        g.out_stored = [ctx.enter_context(nc.semaphore(f"out_{b}_stored")) for b in ("even", "odd")]
        g.ident = sb("ident", [P, P])
        g.inv_d = sb("inv_d", [P, P])
        g.ones_row = sb("ones_row", [1, W])
        g.ln_eps = sb("ln_eps", [P, 1])
        g.rms_eps = sb("rms_eps", [P, 1])
        g.mod = sb("mod", [P, 2, 6, KT])
        with ExitStack() as layer0:
            g.v = layer0.enter_context(nc.sbuf_tensor("v_tokens", [P, T // P * HEADS * E], F32))
            g.q0, g.k0 = (layer0.enter_context(nc.sbuf_tensor(n, [P, T], BF16)) for n in ("q_head0", "k_head0"))
            if stages > 1:
                qkv(nc, d, g, scratch)
            if stages > 2:
                attention(nc, d, g, scratch)
        if stages > 3:
            experts(nc, d, g, scratch)
        if stages > 4:
            state_space(nc, d, g, scratch)
        if stages > 5:
            permuted_mlp(nc, d, g, scratch, out)


def layouts(a):
    import numpy as np

    def cols(v, n):
        return np.ascontiguousarray(v.reshape(n, P).T)

    def by_part(w):
        return np.ascontiguousarray(np.moveaxis(w.reshape((HEADS, E, 2) + w.shape[1:]), 2, 0)).reshape(w.shape)

    t = lambda w: np.ascontiguousarray(w.T)
    f = np.float32
    up = np.zeros((4, MD, KT, 4, MM), f)
    for s in range(4):
        up[s, :, :, s] = a["L1_ffn_up"].reshape(KT, 4, MD, MM)[:, s].transpose(1, 0, 2)
    group = np.zeros((RANK + 2 * NST, 3), f)
    group[:RANK, 0], group[RANK:RANK + NST, 1], group[RANK + NST:, 2] = 1.0 / RANK, 1.0 / NST, 1.0 / NST
    order = np.stack([np.triu(np.ones((P, P), f), 1), np.ones((P, P), f)], axis=1)
    first = np.ones((P, EXPERTS, T // P), f)
    first[:, :, 0] = 0.0
    every = lambda v: np.tile(np.asarray(v, f), (P, 1))
    return {
        "ones": np.ones((2, HEADS * T), mybir.dt.np(BF16)),
        "x": t(a["L0_attn_x"].reshape(T, D)), "xt": a["L0_attn_x"].reshape(T, D),
        "wqk": t(by_part(a["L0_attn_Wqk_w"])), "bqk": by_part(a["L0_attn_Wqk_b"])[:, None].copy(),
        "wv": t(a["L0_attn_Wv_w"]), "bv": a["L0_attn_Wv_b"][None].copy(),
        "wo": np.concatenate([a["L0_attn_Wo_w"].T, a["L0_attn_Wo_b"][None]]),
        "wg": t(a["L0_ffn_gate_w"]), "bg": a["L0_ffn_gate_b"][None].copy(),
        "we": np.ascontiguousarray(a["L0_ffn_expert_w"].transpose(0, 2, 1)), "be": a["L0_ffn_expert_b"],
        "c0": cols(a["L0_c"], KT), "c1": cols(a["L1_c"], KT), "wmod0": a["L0_wmod"], "wmod1": a["L1_wmod"],
        "win": t(a["L1_attn_W_in"]), "wout": t(a["L1_attn_W_out"]), "wx": t(a["L1_attn_Wx"]), "wdt": t(a["L1_attn_Wdt"]),
        "convw": np.ascontiguousarray(a["L1_attn_conv_w"].reshape(DT, P, TAPS).transpose(1, 0, 2)),
        "convb": cols(a["L1_attn_conv_b"], DT), "dtb": cols(a["L1_attn_dt_bias"], DT), "d": cols(a["L1_attn_D_param"], DT),
        "a": np.ascontiguousarray(a["L1_attn_A"].reshape(DT, 4, 32, NST // NG, NG).transpose(4, 2, 0, 3, 1)).reshape(P, DT, NST // NG, 4),
        "select": np.tile(np.eye(32, dtype=f), (NG, 1)),
        "lnw": np.concatenate([a["L1_attn_dt_ln_w"], a["L1_attn_b_ln_w"], a["L1_attn_c_ln_w"]])[:, None].copy(),
        "up": up.reshape(P, MH * MM),
        "down": np.ascontiguousarray(a["L1_ffn_down"].transpose(1, 0, 2)).reshape(P, MH * MD),
        "perm": np.ascontiguousarray(a["L1_ffn_perm"].reshape(KT, P).T).view(np.uint32),
        "ident": np.eye(P, dtype=f), "group": group,
        "order": order, "first": first, "iota": every(range(EXPERTS)), "starts": every(range(0, T, P)),
        "tiles": every(range(T // P + EXPERTS - 1)),
    }


def kernel(**inputs):
    import numpy as np
    import concourse.bacc as bacc
    from concourse.bass_utils import run_bass_kernel_spmd

    nc = bacc.Bacc("TRN2", target_bir_lowering=False, num_devices=1)
    arrays = layouts({k: np.asarray(v) for k, v in inputs.items()})
    d = {k: nc.dram_tensor("in_" + k, a.shape, mybir.dt.from_np(a.dtype), kind="ExternalInput").ap() for k, a in arrays.items()}
    out = nc.dram_tensor("out", [NCH * D, W], F32, kind="ExternalOutput").ap()
    build(nc, d, out)
    r = run_bass_kernel_spmd(nc, [{"in_" + k: a for k, a in arrays.items()}], core_ids=[0])
    y = r.results[0]["out"].reshape(NCH, D, W)
    return np.ascontiguousarray(y.transpose(0, 2, 1)).reshape(1, T, D)
```
